# Optimizing a Trainium2 kernel written in Bass

```python
import numpy as np
import jax
import jax.numpy as jnp

def _softmax(x, axis=-1):
    return jax.nn.softmax(x, axis=axis)

def _gelu(x):
    return jax.nn.gelu(x, approximate=True)

def _silu(x):
    return jax.nn.silu(x)

def _sigmoid(x):
    return jax.nn.sigmoid(x)

def _layernorm(x, axis=-1, eps=1e-05):
    m = jnp.mean(x, axis=axis, keepdims=True)
    v = jnp.var(x, axis=axis, keepdims=True)
    return (x - m) / jnp.sqrt(v + eps)

def _scatter_add(tgt, idx, src, axis=0):
    return tgt.at[idx].add(src)

def _segment_sum(src, seg, n):
    return jax.ops.segment_sum(src, seg, n)
kernel_name = 'mk_gnn_ffn_d1_gnn_r32_f4c2a4'

def setup_inputs(seed: int=0):
    np.random.seed(seed)
    _w = jnp.asarray

    def _rec_inputs():
        import jax
        import jax.numpy as jnp
        _gk = jax.random.key(seed)
        x = -0.0003713 + 1 * jax.random.normal(jax.random.fold_in(_gk, 1), (50000, 256), jnp.float32)
        _s = jax.random.randint(jax.random.fold_in(_gk, 2), (12500,), 0, 50000, jnp.int32)
        _d = jax.random.randint(jax.random.fold_in(_gk, 3), (12500,), 0, 50000, jnp.int32)
        _loop = jnp.arange(50000, dtype=jnp.int32)
        src = jnp.concatenate([_s, _d, _loop])
        dst = jnp.concatenate([_d, _s, _loop])
        _o = jnp.argsort(dst, stable=True)
        src = src[_o]
        dst = dst[_o]
        return (x, src, dst)
    x, src, dst = _rec_inputs()

    def _L0_gnn_setup():
        import jax, jax.numpy as jnp
        import numpy as np
        N_NODES = 50000
        N_EDGES = 25000
        IN_FEATS = 256
        HIDDEN = 256

        def _sage_conv(x, src, dst, Wl, bl, Wr):
            msg = x[src]
            agg = jax.ops.segment_sum(msg, dst, num_segments=N_NODES)
            cnt = jax.ops.segment_sum(jnp.ones((src.shape[0],), dtype=x.dtype), dst, num_segments=N_NODES)
            mean = agg / jnp.maximum(cnt, 1.0)[:, None]
            return mean @ Wl.T + bl + x @ Wr.T
        key = jax.random.key(seed)
        ks = jax.random.split(key, 8)
        x = jax.random.normal(ks[0], (N_NODES, IN_FEATS), dtype=jnp.float32)
        edge_index = jax.random.randint(ks[1], (2, N_EDGES), 0, N_NODES, dtype=jnp.int32)
        s = 1.0 / np.sqrt(IN_FEATS)
        W1l = jax.random.uniform(ks[2], (HIDDEN, IN_FEATS), minval=-s, maxval=s, dtype=jnp.float32)
        b1 = jax.random.uniform(ks[3], (HIDDEN,), minval=-s, maxval=s, dtype=jnp.float32)
        W1r = jax.random.uniform(ks[4], (HIDDEN, IN_FEATS), minval=-s, maxval=s, dtype=jnp.float32)
        s2 = 1.0 / np.sqrt(HIDDEN)
        W2l = jax.random.uniform(ks[5], (HIDDEN, HIDDEN), minval=-s2, maxval=s2, dtype=jnp.float32)
        b2 = jax.random.uniform(ks[6], (HIDDEN,), minval=-s2, maxval=s2, dtype=jnp.float32)
        W2r = jax.random.uniform(ks[7], (HIDDEN, HIDDEN), minval=-s2, maxval=s2, dtype=jnp.float32)
        return {'x': x, 'edge_index': edge_index, 'W1l': W1l, 'b1': b1, 'W1r': W1r, 'W2l': W2l, 'b2': b2, 'W2r': W2r}
    _L0_gnn_all = _L0_gnn_setup()
    _L0_gnn_in = {k: v for k, v in _L0_gnn_all.items() if k in ('W1l', 'b1', 'W1r', 'W2l', 'b2', 'W2r')}
    del _L0_gnn_all

    def _L0_ffn_setup():
        import jax, jax.numpy as jnp
        import numpy as np
        B, A = (128, 8)
        IN, OUT = (256, 256)
        SH1, SH2 = (256, 128)
        EH1, EH2 = (128, 64)
        E, TOPK = (4, 2)

        def _shared_mlp(x, W1, b1, W2, b2, W3, b3):
            h = jax.nn.relu(x @ W1 + b1)
            h = jax.nn.relu(h @ W2 + b2)
            return h @ W3 + b3

        def _experts_mlp(x, eW1, eb1, eW2, eb2, eW3, eb3):
            h = jax.nn.relu(jnp.einsum('baf,efh->ebah', x, eW1) + eb1[:, None, None, :])
            h = jax.nn.relu(jnp.einsum('ebah,ehg->ebag', h, eW2) + eb2[:, None, None, :])
            o = jnp.einsum('ebag,ego->ebao', h, eW3) + eb3[:, None, None, :]
            return jnp.moveaxis(o, 0, -1)
        key = jax.random.key(seed)
        ks = jax.random.split(key, 16)
        s = 0.05
        return {'x': jax.random.normal(ks[0], (B, A, IN), jnp.float32), 'sW1': jax.random.normal(ks[1], (IN, SH1), jnp.float32) * s, 'sb1': jnp.zeros((SH1,), jnp.float32), 'sW2': jax.random.normal(ks[2], (SH1, SH2), jnp.float32) * s, 'sb2': jnp.zeros((SH2,), jnp.float32), 'sW3': jax.random.normal(ks[3], (SH2, OUT), jnp.float32) * s, 'sb3': jnp.zeros((OUT,), jnp.float32), 'eW1': jax.random.normal(ks[4], (E, IN, EH1), jnp.float32) * s, 'eb1': jnp.zeros((E, EH1), jnp.float32), 'eW2': jax.random.normal(ks[5], (E, EH1, EH2), jnp.float32) * s, 'eb2': jnp.zeros((E, EH2), jnp.float32), 'eW3': jax.random.normal(ks[6], (E, EH2, OUT), jnp.float32) * s, 'eb3': jnp.zeros((E, OUT), jnp.float32), 'gW': jax.random.normal(ks[7], (IN, E), jnp.float32) * s, 'gb': jnp.zeros((E,), jnp.float32)}
    _L0_ffn_all = _L0_ffn_setup()
    _L0_ffn_in = {k: v for k, v in _L0_ffn_all.items() if k in ('sW1', 'sb1', 'sW2', 'sb2', 'sW3', 'sb3', 'eW1', 'eb1', 'eW2', 'eb2', 'eW3', 'eb3', 'gW', 'gb')}
    del _L0_ffn_all
    return {'x': x, 'src': src, 'dst': dst, 'L0_gnn_W1l': _L0_gnn_in['W1l'], 'L0_gnn_b1': _L0_gnn_in['b1'], 'L0_gnn_W1r': _L0_gnn_in['W1r'], 'L0_gnn_W2l': _L0_gnn_in['W2l'], 'L0_gnn_b2': _L0_gnn_in['b2'], 'L0_gnn_W2r': _L0_gnn_in['W2r'], 'L0_ffn_sW1': _L0_ffn_in['sW1'], 'L0_ffn_sb1': _L0_ffn_in['sb1'], 'L0_ffn_sW2': _L0_ffn_in['sW2'], 'L0_ffn_sb2': _L0_ffn_in['sb2'], 'L0_ffn_sW3': _L0_ffn_in['sW3'], 'L0_ffn_sb3': _L0_ffn_in['sb3'], 'L0_ffn_eW1': _L0_ffn_in['eW1'], 'L0_ffn_eb1': _L0_ffn_in['eb1'], 'L0_ffn_eW2': _L0_ffn_in['eW2'], 'L0_ffn_eb2': _L0_ffn_in['eb2'], 'L0_ffn_eW3': _L0_ffn_in['eW3'], 'L0_ffn_eb3': _L0_ffn_in['eb3'], 'L0_ffn_gW': _L0_ffn_in['gW'], 'L0_ffn_gb': _L0_ffn_in['gb']}

def reference(x, src, dst, L0_gnn_W1l, L0_gnn_b1, L0_gnn_W1r, L0_gnn_W2l, L0_gnn_b2, L0_gnn_W2r, L0_ffn_sW1, L0_ffn_sb1, L0_ffn_sW2, L0_ffn_sb2, L0_ffn_sW3, L0_ffn_sb3, L0_ffn_eW1, L0_ffn_eb1, L0_ffn_eW2, L0_ffn_eb2, L0_ffn_eW3, L0_ffn_eb3, L0_ffn_gW, L0_ffn_gb):
    import jax
    import jax.numpy as jnp

    def _L0_gnn_ref(x, edge_index, W1l, b1, W1r, W2l, b2, W2r):
        import jax, jax.numpy as jnp
        import numpy as np
        N_NODES = 50000
        N_EDGES = 25000
        IN_FEATS = 256
        HIDDEN = 256

        def _sage_conv(x, src, dst, Wl, bl, Wr):
            msg = x[src]
            agg = jax.ops.segment_sum(msg, dst, num_segments=N_NODES)
            cnt = jax.ops.segment_sum(jnp.ones((src.shape[0],), dtype=x.dtype), dst, num_segments=N_NODES)
            mean = agg / jnp.maximum(cnt, 1.0)[:, None]
            return mean @ Wl.T + bl + x @ Wr.T
        src, dst = (edge_index[0], edge_index[1])
        h = jax.nn.relu(_sage_conv(x, src, dst, W1l, b1, W1r))
        out = _sage_conv(h, src, dst, W2l, b2, W2r)
        return out

    def _L0_ffn_ref(x, sW1, sb1, sW2, sb2, sW3, sb3, eW1, eb1, eW2, eb2, eW3, eb3, gW, gb):
        import jax, jax.numpy as jnp
        import numpy as np
        B, A = (128, 8)
        IN, OUT = (256, 256)
        SH1, SH2 = (256, 128)
        EH1, EH2 = (128, 64)
        E, TOPK = (4, 2)

        def _shared_mlp(x, W1, b1, W2, b2, W3, b3):
            h = jax.nn.relu(x @ W1 + b1)
            h = jax.nn.relu(h @ W2 + b2)
            return h @ W3 + b3

        def _experts_mlp(x, eW1, eb1, eW2, eb2, eW3, eb3):
            h = jax.nn.relu(jnp.einsum('baf,efh->ebah', x, eW1) + eb1[:, None, None, :])
            h = jax.nn.relu(jnp.einsum('ebah,ehg->ebag', h, eW2) + eb2[:, None, None, :])
            o = jnp.einsum('ebag,ego->ebao', h, eW3) + eb3[:, None, None, :]
            return jnp.moveaxis(o, 0, -1)
        all_out = _experts_mlp(x, eW1, eb1, eW2, eb2, eW3, eb3)
        shared = _shared_mlp(x, sW1, sb1, sW2, sb2, sW3, sb3)
        gates = jax.nn.softmax(x @ gW + gb, axis=-1)
        topv, topi = jax.lax.top_k(gates, TOPK)
        topw = jax.nn.softmax(topv, axis=-1)
        sel = jnp.take_along_axis(all_out, topi[:, :, None, :], axis=-1)
        gated = jnp.sum(sel * topw[:, :, None, :], axis=-1)
        return shared + gated
    edge_index = jnp.stack([src, dst])
    x = x + _L0_gnn_ref(_layernorm(x, axis=-1), edge_index, L0_gnn_W1l, L0_gnn_b1, L0_gnn_W1r, L0_gnn_W2l, L0_gnn_b2, L0_gnn_W2r)
    x = x + _L0_ffn_ref(_layernorm(x, axis=-1)[None], L0_ffn_sW1, L0_ffn_sb1, L0_ffn_sW2, L0_ffn_sb2, L0_ffn_sW3, L0_ffn_sb3, L0_ffn_eW1, L0_ffn_eb1, L0_ffn_eW2, L0_ffn_eb2, L0_ffn_eW3, L0_ffn_eb3, L0_ffn_gW, L0_ffn_gb)[0]
    return x

_drawn_inputs = setup_inputs


def setup_inputs(seed=0):
    import zlib

    import numpy as np

    out = dict(_drawn_inputs(seed))
    spreads = {'L0_ffn_sb1': (0.0, 0.458),
     'L0_ffn_sb2': (0.0, 0.1),
     'L0_ffn_sb3': (0.0, 0.1),
     'L0_ffn_eb1': (0.0, 0.8),
     'L0_ffn_eb2': (0.0, 0.537),
     'L0_ffn_eb3': (0.0, 0.1),
     'L0_ffn_gb': (0.0, 0.394)}
    factors = {'L0_gnn_b1': 3.11}
    for name, (base, spread) in spreads.items():
        noise = np.random.default_rng([zlib.crc32(name.encode()), seed]).standard_normal(out[name].shape)
        drawn = base * np.exp(spread * noise) if base else spread * noise
        out[name] = jnp.asarray(drawn.astype(out[name].dtype))
    for name, factor in factors.items():
        out[name] = (out[name] * factor).astype(out[name].dtype)
    return out
```

```python
import concourse.bass as bass
from concourse import mybir
from contextlib import ExitStack

N, E, D, P = 50000, 75000, 256, 128
TILES = 4
ROWS = TILES * P
GROUPS = -(-N // ROWS)
NPAD = GROUPS * ROWS
NBLK = GROUPS * TILES
LAST = N - (GROUPS - 1) * ROWS
EPS = 1e-5
NEXP = 4

WROW, WK = 64, 5
WIN = WROW * WK
ETROWS = E // WROW + 1 + WK + 1
FAR = 1 << 20
WJ = 4
CHUNKS = [(0, 128), (128, 128), (256, 64)]
EP, EC = 120, 625
assert EP * EC == E
HA, HC = 16, 32
OOB = 65536.0

WCOLS = {}
_at = 0
for _name, _n in (("w1l", 512), ("w1r", 512), ("w2", 1024), ("sw1", 512), ("sw2", 256),
                  ("sw3", 256), ("ew1", 1024), ("ew2", 256), ("ew3", 512), ("gw", 8)):
    WCOLS[_name] = (_at, _n)
    _at += _n
WTOTAL = _at
BCOLS = {"b1": 0, "sb1": 2, "sb2": 4, "eb1": 5, "eb2": 9}
BTOTAL = 11

GATE_STEPS, GATE_EXP1, GATE_EXP2 = 22, 4, 13


def build(nc, x, src, dst, wpack, bpack, b2, gb, b3, out):
    fp32, fr, bf16 = mybir.dt.float32, mybir.dt.float32r, mybir.dt.bfloat16
    i32, u32 = mybir.dt.int32, mybir.dt.uint32
    ALU, ACT, AX = mybir.AluOpType, mybir.ActivationFunctionType, mybir.AxisListType

    edges = nc.dram_tensor("edge_table", [ETROWS, 2 * WROW], i32, kind="Internal").ap()
    starts = nc.dram_tensor("tile_starts", [HA * HC], i32, kind="Internal").ap()
    hl_d = nc.dram_tensor("hl_rows", [NPAD, D], fp32, kind="Internal").ap()
    z_d = nc.dram_tensor("z_rows", [NPAD, D], fp32, kind="Internal").ap()

    ctx = ExitStack()
    with ctx:
        def sb(name, shape, dt=fp32, scope=ctx):
            return scope.enter_context(nc.sbuf_tensor(name, shape, dt))

        def sem(name):
            return ctx.enter_context(nc.semaphore(name))

        def sems(name, n=2):
            return [sem(f"{name}{k}") for k in range(n)]

        w1_hi, w1_lo = (sb(f"w1_{h}", [P, 2, 2, D], fr) for h in ("hi", "lo"))
        w2_hi, w2_lo = (sb(f"w2_{h}", [P, 2, 2 * D], fr) for h in ("hi", "lo"))
        sw1_hi, sw1_lo = (sb(f"sw1_{h}", [P, 2, D], fr) for h in ("hi", "lo"))
        sw2_hi, sw2_lo = (sb(f"sw2_{h}", [P, 2, P], fr) for h in ("hi", "lo"))
        sw3_hi, sw3_lo = (sb(f"sw3_{h}", [P, D], fr) for h in ("hi", "lo"))
        ew1_hi, ew1_lo = (sb(f"ew1_{h}", [P, 2, NEXP, P], fr) for h in ("hi", "lo"))
        ew2_hi, ew2_lo = (sb(f"ew2_{h}", [P, NEXP, P], fr) for h in ("hi", "lo"))
        ew3_hi, ew3_lo = (sb(f"ew3_{h}", [P, 2, D], fr) for h in ("hi", "lo"))
        gw_hl = sb("gw_hl", [P, 2, 2 * NEXP], fr)
        b3s = sb("b3s", [96, D], fr)
        sel = sb("sel", [96, 2, P], fr)
        bcol = sb("bcol", [P, BTOTAL])
        b2b = sb("b2b", [P, D])
        gbb = sb("gbb", [P, NEXP])
        prio = sb("prio", [P, TILES, NEXP])
        ident = sb("ident", [P, P])
        iota = sb("iota", [P, D])
        eps = sb("eps", [P, 1])
        idx_all = sb("idx_all", [P, NBLK], u32)
        dloc_all = sb("dloc_all", [P, NBLK])
        inv_all = sb("inv_all", [P, NBLK])
        sinv_all = sb("sinv_all", [P, NBLK])

        prep = ExitStack()
        wst = sb("wst", [P, WTOTAL], scope=prep)
        b3f = sb("b3f", [96, D], scope=prep)
        selj = sb("selj", [96, 2 * P], scope=prep)
        win = sb("win", [P, WJ * WK, 2 * WROW], i32, scope=prep)
        dstN = sb("dstN", [EP, EC], i32, scope=prep)
        ea, ec = (sb(n, [EP, EC], i32, scope=prep) for n in ("ea", "ec"))
        oa = sb("oa", [EP, 2, 25, HA], bf16, scope=prep)
        oc = sb("oc", [EP, 2, 25, HC + 1], bf16, scope=prep)
        iot33 = sb("iot33", [EP, HC + 1], scope=prep)
        tri = sb("tri", [HA, HA], scope=prep)
        cum = sb("cum", [HA, HC + 1], scope=prep)
        pre = sb("pre", [HA, 1], scope=prep)
        sti = sb("sti", [HA, HC], i32, scope=prep)
        s4 = sb("s4", [P, WJ], i32, scope=prep)
        r0 = sb("r0", [P, WJ], i32, scope=prep)
        r0f = sb("r0f", [P, WJ], scope=prep)
        ridx = sb("ridx", [P, WJ * WK], u32, scope=prep)
        far = sb("far", [P, 2 * WROW], i32, scope=prep)
        tb = sb("tb", [P, WJ], scope=prep)
        wd, ws, wv, wn, wc, wk_ = (sb(n, [P, WJ, WIN], scope=prep)
                                   for n in ("wd", "ws", "wv", "wn", "wc", "wk_"))
        shi = sb("shi", [P, WJ, WIN], i32, scope=prep)
        slo = sb("slo", [P, WJ, WIN], i32, scope=prep)
        keyT = sb("keyT", [P, 3, WJ * P], scope=prep)
        vT = sb("vT", [P, 3, WJ * P, 4], bf16, scope=prep)
        iob = sb("iob", [P, D], bf16, scope=prep)
        hot = sb("hot", [P, 2, TILES, 3, D], bf16, scope=prep)
        mh = sb("mh", [P, 2, TILES, P], bf16, scope=prep)
        oneb = sb("oneb", [P, 2], bf16, scope=prep)
        info = sb("info", [P, NBLK, 8], scope=prep)
        cnt = sb("cnt", [P, NBLK], scope=prep)
        idxf = sb("idxf", [P, NBLK], scope=prep)
        prep.close()

        one = ExitStack()
        xg = [sb(f"xg{u}", [P, TILES, D], scope=one) for u in range(2)]
        xb = [sb(f"xb{u}", [P, TILES, D], scope=one) for u in range(2)]
        xn = [sb(f"xn{u}", [P, TILES, D], scope=one) for u in range(2)]
        xgn = [sb(f"xgn{u}", [P, TILES, D], scope=one) for u in range(2)]
        m1 = [sb(f"m1{u}", [P, TILES, P], scope=one) for u in range(2)]
        idx1 = [sb(f"idx1{u}", [P, TILES], u32, scope=one) for u in range(2)]
        sinv1 = [sb(f"sinv1{u}", [P, TILES], scope=one) for u in range(2)]
        st1 = [sb(f"st1{u}", [P, 2 * TILES, 6], scope=one) for u in range(2)]
        mv1 = [sb(f"mv1{u}", [P, 2 * TILES, 2], scope=one) for u in range(2)]
        sd1 = [sb(f"sd1{u}", [P, 2 * TILES], scope=one) for u in range(2)]
        rs1 = [sb(f"rs1{u}", [P, 2 * TILES], scope=one) for u in range(2)]
        nm1 = [sb(f"nm1{u}", [P, 2 * TILES], scope=one) for u in range(2)]
        sx = [sb(f"sx{u}", [P, TILES, D], scope=one) for u in range(2)]
        mean = [sb(f"mean{u}", [P, TILES, D], scope=one) for u in range(2)]
        xT_hi, xT_lo, mT_hi, mT_lo = (
            [sb(f"{n}{u}", [P, 2, ROWS], fr, scope=one) for u in range(2)]
            for n in ("xT_hi", "xT_lo", "mT_hi", "mT_lo"))
        ha = sb("ha", [P, 2, ROWS], scope=one)
        hh = sb("hh", [P, 2, ROWS], fr, scope=one)
        hlo = sb("hlo", [P, 2, ROWS], fr, scope=one)
        hl = [sb(f"hl{u}", [P, TILES, D], scope=one) for u in range(2)]
        zs = [sb(f"zs{u}", [P, TILES, D], scope=one) for u in range(2)]
        one.close()

        two = ExitStack()
        gg = [sb(f"gg{u}", [P, TILES, D], scope=two) for u in range(2)]
        zb = [sb(f"zb{u}", [P, TILES, D], scope=two) for u in range(2)]
        xr = [sb(f"xr{u}", [P, TILES, D], scope=two) for u in range(2)]
        m2 = [sb(f"m2{u}", [P, TILES, P], scope=two) for u in range(2)]
        idx2 = [sb(f"idx2{u}", [P, TILES], u32, scope=two) for u in range(2)]
        x2 = [sb(f"x2{u}", [P, TILES, D], scope=two) for u in range(2)]
        x2n = [sb(f"x2n{u}", [P, TILES, D], scope=two) for u in range(2)]
        st2 = [sb(f"st2{u}", [P, TILES, 6], scope=two) for u in range(2)]
        mv2 = [sb(f"mv2{u}", [P, TILES, 2], scope=two) for u in range(2)]
        sd2 = [sb(f"sd2{u}", [P, TILES], scope=two) for u in range(2)]
        rs2 = [sb(f"rs2{u}", [P, TILES], scope=two) for u in range(2)]
        nm2 = [sb(f"nm2{u}", [P, TILES], scope=two) for u in range(2)]
        yT_hi, yT_lo = ([sb(f"{n}{u}", [P, 2, ROWS], fr, scope=two) for u in range(2)]
                        for n in ("yT_hi", "yT_lo"))
        act_a = sb("act_a", [P, 9, ROWS], scope=two)
        act_hi = sb("act_hi", [P, 9, ROWS], fr, scope=two)
        act_lo = sb("act_lo", [P, 9, ROWS], fr, scope=two)
        ob = [sb(f"ob{u}", [P, TILES, D], scope=two) for u in range(2)]
        lg = sb("lg", [P, TILES, 2 * NEXP], scope=two)
        g_t = [sb(f"g_t{k}", [P, TILES, NEXP], scope=two) for k in range(9)]
        g_s = [sb(f"g_s{k}", [P, TILES, 1], scope=two) for k in range(10)]
        wx = sb("wx", [P, TILES, 96], scope=two)
        wxT = sb("wxT", [96, ROWS], fr, scope=two)
        two.close()

        ps = [ctx.enter_context(nc.psum_tensor(f"ps{k}", [P, 512], fp32)) for k in range(8)]
        TP, AG, HB, ZB = ps[0:2], ps[2:4], ps[4:6], ps[6:8]
        RB, WB, OBS = ps[4:6], ps[6], (ps[7], ps[6])

        phase_end = sem("phase_end")
        w_in, bias_in, dst_in, et_in, far_set = map(sem, ("w_in", "bias_in", "dst_in", "et_in", "far_set"))
        starts_out, starts_in, win_in = map(sem, ("starts_out", "starts_in", "win_in"))
        dstep, pstep = sem("vector_step"), sem("pool_step")
        const_set, hot_edge, hist_done, cum_ready, pre_done, sti_ready, ridx_ready = map(sem, (
            "const_set", "hot_edge", "hist_done", "cum_ready", "pre_done", "sti_ready", "ridx_ready"))
        fields_ready, ft_done, ft_taken, hot_ready, slots_done, slots_taken = map(sem, (
            "fields_ready", "ft_done", "ft_taken", "hot_ready", "slots_done", "slots_taken"))
        hist_step, mh_ready, cnt_done, cnt_taken = map(sem, ("hist_step", "mh_ready", "cnt_done", "cnt_taken"))
        x_in, xg_in, xr_in, hl_out, z_out = (sems(n) for n in ("x_in", "xg_in", "xr_in", "hl_out", "z_out"))
        stats1, ln1a, std1, rstd1, ln1b, xn_ready, xgn_ready, m1_ready = map(sem, (
            "stats1", "ln1a", "std1", "rstd1", "ln1b", "xn_ready", "xgn_ready", "m1_ready"))
        idx1_ready, sinv_ready, sx_ready, xb_ready = map(sem, ("idx1_ready", "sinv_ready", "sx_ready", "xb_ready"))
        agg_done, xT_done, mT_done, mean_ready = map(sem, ("agg_done", "xT_done", "mT_done", "mean_ready"))
        xhi, xlo, mhi, mlo = map(sem, ("xhi", "xlo", "mhi", "mlo"))
        h_done, h_relu, h_hi, h_lo, z_done, hl_ready, z1_ready, z_ready = map(sem, (
            "h_done", "h_relu", "h_hi", "h_lo", "z_done", "hl_ready", "z1_ready", "z_ready"))
        zl_in, gg_in, o_out = sems("zl_in"), sems("gg_in"), sems("o_out")
        idx2_ready, m2_ready, agg2_done, x2_ready, stats2, ln2a, std2, rstd2, ln2b, x2n_ready = map(sem, (
            "idx2_ready", "m2_ready", "agg2_done", "x2_ready", "stats2", "ln2a", "std2", "rstd2", "ln2b", "x2n_ready"))
        yT_done, yhi, ylo, lg_done, gate_step, wx_ready, wxT_done, wxT_hi, wxT_lo = map(sem, (
            "yT_done", "yhi", "ylo", "lg_done", "gate_step", "wx_ready", "wxT_done", "wxT_hi", "wxT_lo"))
        gate_exp = sem("gate_exp")
        gathers_asked = sem("gathers_asked")
        r_done, r_relu, r_hi_a, r_hi_v, r_lo, wb_done, wb_taken, o_done, o_ready = map(sem, (
            "r_done", "r_relu", "r_hi_a", "r_hi_v", "r_lo", "wb_done", "wb_taken", "o_done", "o_ready"))
        gated_ready = sem("gated_ready")

        block = ctx.enter_context(nc.Block())

        def wait(eng, s, v):
            if isinstance(v, int) and v <= 0:
                return
            eng.wait_ge(s, v)

        def end_phase(eng, n):
            eng.drain().then_inc(phase_end, 1)
            eng.wait_ge(phase_end, 5 * n)

        def pipeline(eng, body):
            for u in range(2):
                body(0, u)
            with eng.Fori(1, GROUPS // 2 - 3) as j:
                for u in range(2):
                    body(j, u)
            for j in range(GROUPS // 2 - 3, GROUPS // 2):
                for u in range(2):
                    body(j, u)

        def ahead(j, u, k):
            return j + (u + k) // 2, (u + k) % 2

        def exists(j, u, k):
            return not isinstance(j, int) or 2 * j + u + k < GROUPS

        def no(j, u):
            return 2 * j + u

        def mm3(pe, o, l_hi, l_lo, r_hi_, r_lo_, first, last):
            pe.matmul(o, l_hi, r_hi_, start=first, stop=False)
            pe.matmul(o, l_hi, r_lo_, start=False, stop=False)
            return pe.matmul(o, l_lo, r_hi_, start=False, stop=last)

        def rows_of(t, j, u, half=None):
            first, n = no(j, u) * ROWS, ROWS
            if half is not None:
                first, n = first + half * 2 * P, 2 * P
            if isinstance(first, int):
                ap = t[first:first + n, :]
            else:
                ap = t[bass.ds(first, n), :]
            return ap.rearrange("(t p) d -> p t d", p=P)

        def first_tile(eng, j, u):
            c = no(j, u) * TILES
            return c if isinstance(c, int) else eng.snap(c)

        def cols(t, c):
            return t[:, c:c + TILES] if isinstance(c, int) else t[:, bass.ds(c, TILES)]

        def col(t, j, u, k):
            c = no(j, u) * TILES + k
            return t[:, c:c + 1] if isinstance(c, int) else t[:, bass.ds(c, 1)]

        def tail_rows(t, half):
            first = (GROUPS - 1) * ROWS
            if half == 0:
                return t[first:first + 2 * P, :].rearrange("(t p) d -> p t d", p=P), P
            n = LAST - 2 * P
            return t[first + 2 * P:N, :], n

        def is_last(j, u):
            return isinstance(j, int) and 2 * j + u == GROUPS - 1

        @block.sync
        def _(sp):
            sp.dma_start(dstN[:, :], dst.rearrange("(p c) -> p c", p=EP)).then_inc(dst_in, 16)
            sp.dma_start(wst[:, :], wpack).then_inc(w_in, 16)
            whole = E // WROW
            rest = E - whole * WROW
            for k, t in enumerate((dst, src)):
                c = k * WROW
                sp.dma_start(edges[0:whole, c:c + WROW],
                             t[0:whole * WROW].rearrange("(r w) -> r w", w=WROW)).then_inc(et_in, 16)
                sp.dma_start(edges[whole:whole + 1, c:c + rest],
                             t[whole * WROW:E].rearrange("(r w) -> r w", r=1)).then_inc(et_in, 16)
            sp.wait_ge(far_set, 1)
            for k in range(2):
                c = k * WROW
                sp.dma_start(edges[whole:whole + 1, c + rest:c + WROW], far[0:1, 0:WROW - rest]).then_inc(et_in, 16)
            sp.dma_start(edges[whole + 1:ETROWS, :], far[0:ETROWS - whole - 1, :]).then_inc(et_in, 16)
            sp.dma_start(bcol[:, :], bpack).then_inc(bias_in, 16)
            sp.dma_start(b2b[:, :], b2[None, :].to_broadcast([P, D])).then_inc(bias_in, 16)
            sp.dma_start(gbb[:, :], gb[None, :].to_broadcast([P, NEXP])).then_inc(bias_in, 16)
            sp.wait_ge(const_set, 1)
            for k in (0, 32, 64):
                sp.dma_start(b3f[k:k + 5, :], b3).then_inc(bias_in, 16)
            sp.wait_ge(sti_ready, 1)
            sp.dma_start(starts.rearrange("(a c) -> a c", a=HA), sti[:, :]).then_inc(starts_out, 16)
            sp.wait_ge(starts_out, 16)
            with nc.allow_non_contiguous_dma(reason="512 tile starts, one per partition"):
                sp.dma_start(s4[:, :], starts.rearrange("(j p) -> p j", p=P)).then_inc(starts_in, 16)
            sp.wait_ge(bias_in, 96)
            sp.wait_ge(starts_in, 16)
            end_phase(sp, 1)

            def load_x(j, u):
                for half in range(2):
                    if is_last(j, u):
                        rows, n = tail_rows(x, half)
                        to = xb[u][0:n, 0:2, :] if half == 0 else xb[u][0:n, 2, :]
                    else:
                        rows, to = rows_of(x, j, u, half), xb[u][:, 2 * half:2 * half + 2, :]
                    sp.dma_start(to, rows).then_inc(x_in[u], 16)

            for g in range(2):
                load_x(0, g)
            for g in range(2, 4):
                sp.wait_ge(xn_ready, TILES * (g - 1))
                load_x(1, g % 2)

            def body(j, u):
                i = no(j, u)
                if exists(j, u, 4):
                    sp.wait_ge(xn_ready, TILES * (i + 3))
                    load_x(*ahead(j, u, 4))
                sp.wait_ge(hl_ready, TILES * (i + 1))
                sp.dma_start(rows_of(hl_d, j, u), hl[u][:, :, :]).then_inc(hl_out[u], 16)
                sp.wait_ge(z_ready, TILES * (i + 1))
                sp.dma_start(rows_of(z_d, j, u), zs[u][:, :, :]).then_inc(z_out[u], 16)

            pipeline(sp, body)
            for u in range(2):
                sp.wait_ge(hl_out[u], 16 * (GROUPS // 2))
                sp.wait_ge(z_out[u], 16 * (GROUPS // 2))
            end_phase(sp, 2)

            def load_xr(j, u):
                for half in range(2):
                    if is_last(j, u):
                        rows, n = tail_rows(x, half)
                        to = xr[u][0:n, 0:2, :] if half == 0 else xr[u][0:n, 2, :]
                    else:
                        rows, to = rows_of(x, j, u, half), xr[u][:, 2 * half:2 * half + 2, :]
                    sp.dma_start(to, rows).then_inc(xr_in[u], 16)

            def load_z(j, u):
                sp.dma_start(zb[u][:, :, :], rows_of(z_d, j, u)).then_inc(zl_in[u], 16)
                load_xr(j, u)

            for g in range(2):
                load_z(0, g)
            sp.wait_ge(x2_ready, TILES)
            load_z(1, 0)

            def body2(j, u):
                i = no(j, u)
                if exists(j, u, 3):
                    sp.wait_ge(x2_ready, TILES * (i + 2))
                    load_z(*ahead(j, u, 3))
                sp.wait_ge(o_ready, TILES * (i + 1))
                for half in range(2):
                    if is_last(j, u):
                        rows, n = tail_rows(out, half)
                        of = ob[u][0:n, 0:2, :] if half == 0 else ob[u][0:n, 2, :]
                    else:
                        rows, of = rows_of(out, j, u, half), ob[u][:, 2 * half:2 * half + 2, :]
                    sp.dma_start(rows, of).then_inc(o_out[u], 16)

            pipeline(sp, body2)
            for u in range(2):
                sp.wait_ge(o_out[u], 32 * (GROUPS // 2))

        @block.gpsimd
        def _(pool):
            step = [0]

            def link(ins):
                step[0] += 1
                ins.then_inc(pstep, 1)
                pool.wait_ge(pstep, step[0])

            pool.memset(far[:, :], FAR).then_inc(far_set, 1)
            link(pool.memset(b3f[:, :], 0.0))
            pool.nop().then_inc(const_set, 1)
            pool.iota(iota[:, :], [[1, D]], base=0, channel_multiplier=0,
                      allow_small_or_imprecise_dtypes=True)
            pool.iota(iot33[:, :], [[1, HC + 1]], base=0, channel_multiplier=0,
                      allow_small_or_imprecise_dtypes=True)
            pool.iota(iob[:, :], [[1, D]], base=0, channel_multiplier=0,
                      allow_small_or_imprecise_dtypes=True)
            pool.iota(tb[:, :], [[P * P, WJ]], base=0, channel_multiplier=P,
                      allow_small_or_imprecise_dtypes=True)
            pool.iota(prio[:, :, :], [[0, TILES], [-1, NEXP]], base=NEXP, channel_multiplier=0,
                      allow_small_or_imprecise_dtypes=True)
            pool.memset(oneb[:, :], 1.0)
            pool.memset(eps[:, :], EPS)
            link(pool.memset(ident[:, :], 0.0))
            link(pool.affine_select(out=ident[:, :], in_=ident[:, :], compare_op=ALU.not_equal, fill=1.0,
                                    base=0, pattern=[[-1, P]], channel_multiplier=1))
            link(pool.memset(tri[:, :], 1.0))
            link(pool.affine_select(out=tri[:, :], in_=tri[:, :], compare_op=ALU.is_gt, fill=0.0,
                                    base=0, pattern=[[1, HA]], channel_multiplier=-1))
            link(pool.memset(selj[:, :], 1.0))
            for first in (0, 32):
                v = selj[first:first + 32, :].rearrange("r (q m) -> r q m", q=2)
                link(pool.affine_select(out=v, in_=v, compare_op=ALU.is_ge, fill=0.0, base=0,
                                        pattern=[[P, 2], [1, P]], channel_multiplier=-64))
                link(pool.affine_select(out=v, in_=v, compare_op=ALU.is_ge, fill=0.0, base=63,
                                        pattern=[[-P, 2], [-1, P]], channel_multiplier=64))
            link(pool.memset(selj[64:96, :], 0.0))
            pool.drain().then_inc(const_set, 1)

            pool.wait_ge(et_in, 16 * 7)
            pool.wait_ge(ridx_ready, 1)
            for k in range(WJ * WK):
                pool.indirect_dma_start(win[:, k, :], None, edges[:, :],
                                        bass.IndirectOffsetOnAxis(ridx[:, k:k + 1], 0)).then_inc(win_in, 16)
            pool.wait_ge(win_in, 16 * WJ * WK)
            end_phase(pool, 1)

            bound = pool.to_reg(N - 1)

            for u in range(2):
                link(pool.memset(xg[u][:, :, :], 1.0))

            def gather(j, u, wait_for=None):
                i = no(j, u)
                c = first_tile(pool, j, u)
                if wait_for is not None:
                    pool.wait_ge(xgn_ready, wait_for)
                pool.tensor_copy(idx1[u][:, :], cols(idx_all, c)).then_inc(idx1_ready, 1)
                pool.wait_ge(idx1_ready, i + 1)
                pool.sem_inc(gathers_asked, 1)
                for t in range(TILES):
                    pool.indirect_dma_start(xg[u][:, t, :], None, x,
                                            bass.IndirectOffsetOnAxis(idx1[u][:, t:t + 1], 0),
                                            bounds_check=bound, oob_is_err=False).then_inc(xg_in[u], 16)

            def scaled_own(j, u):
                i = no(j, u)
                c = first_tile(pool, j, u)
                pool.wait_ge(xn_ready, TILES * (i + 1))
                wait(pool, mean_ready, TILES * (i - 1))
                pool.tensor_copy(sinv1[u][:, :], cols(sinv_all, c)).then_inc(sinv_ready, 1)
                pool.wait_ge(sinv_ready, i + 1)
                pool.tensor_tensor(sx[u][:, :, :], xn[u][:, :, :],
                                   sinv1[u][:, :].unsqueeze(2).to_broadcast([P, TILES, D]),
                                   ALU.mult).then_inc(sx_ready, 1)

            for g in range(4):
                gather(g // 2, g % 2, TILES * (g - 1) if g >= 2 else None)
            for g in range(2):
                scaled_own(0, g)

            def body(j, u):
                if exists(j, u, 4):
                    gather(*ahead(j, u, 4), TILES * (no(j, u) + 3))
                if exists(j, u, 2):
                    scaled_own(*ahead(j, u, 2))

            pipeline(pool, body)
            end_phase(pool, 2)

            for u in range(2):
                link(pool.memset(gg[u][:, :, :], 1.0))
            link(pool.memset(wx[:, :, :], 0.0))
            for c in (NEXP, 64 + NEXP):
                link(pool.memset(wx[:, :, c:c + 1], 1.0))

            def gather2(j, u, wait_for=None):
                i = no(j, u)
                c = first_tile(pool, j, u)
                if wait_for is not None:
                    pool.wait_ge(agg2_done, wait_for)
                pool.tensor_copy(idx2[u][:, :], cols(idx_all, c)).then_inc(idx2_ready, 1)
                pool.wait_ge(idx2_ready, i + 1)
                pool.sem_inc(gathers_asked, 1)
                for t in range(TILES):
                    pool.indirect_dma_start(gg[u][:, t, :], None, hl_d,
                                            bass.IndirectOffsetOnAxis(idx2[u][:, t:t + 1], 0),
                                            bounds_check=bound, oob_is_err=False).then_inc(gg_in[u], 16)

            for g in range(3):
                gather2(g // 2, g % 2, 1 if g == 2 else None)

            def own_share(j, u):
                i = no(j, u)
                pool.wait_ge(zl_in[u], 16 * (j + 1))
                pool.tensor_tensor(zb[u][:, :, :], zb[u][:, :, :],
                                   b2b[:, None, :].to_broadcast([P, TILES, D]), ALU.add).then_inc(xb_ready, 1)
                pool.wait_ge(xr_in[u], 32 * (j + 1))
                pool.wait_ge(xb_ready, 2 * i + 1)
                pool.tensor_tensor(zb[u][:, :, :], zb[u][:, :, :], xr[u][:, :, :], ALU.add).then_inc(xb_ready, 1)

            for g in range(2):
                own_share(0, g)

            def body2(j, u):
                if exists(j, u, 3):
                    gather2(*ahead(j, u, 3), no(j, u) + 2)
                if exists(j, u, 2):
                    own_share(*ahead(j, u, 2))

            pipeline(pool, body2)

        @block.scalar
        def _(act):
            for f in range(4):
                for q, (_, n) in enumerate(CHUNKS):
                    k = 3 * f + q
                    act.wait_ge(ft_done, k + 1)
                    to = keyT[0:n, q, :] if f == 0 else vT[0:n, q, :, f - 1]
                    act.activation(to, ps[k % 4][0:n, :], ACT.Copy).then_inc(ft_taken, 1)
            with act.Fori(0, GROUPS // 2) as j:
                for u in range(2):
                    act.wait_ge(slots_done, 2 * j + u + 1)
                    act.activation(info[:, bass.ds((2 * j + u) * TILES, TILES), :],
                                   ps[u][:, 0:8 * TILES].rearrange("p (t k) -> p t k", k=8),
                                   ACT.Copy).then_inc(slots_taken, 1)
            with act.Fori(0, GROUPS // 2) as j:
                for u in range(2):
                    act.wait_ge(cnt_done, 2 * j + u + 1)
                    act.activation(cnt[:, bass.ds((2 * j + u) * TILES, TILES)], ps[u][:, 0:TILES],
                                   ACT.Copy).then_inc(cnt_taken, 1)
            end_phase(act, 1)

            def deviations(j, u):
                i = no(j, u)
                act.wait_ge(ln1a, i + 1)
                act.activation(sd1[u][:, :], mv1[u][:, :, 1], ACT.Sqrt, bias=eps[:, 0:1]).then_inc(std1, 1)

            def normalise(j, u, tiles):
                i = no(j, u)
                for t in tiles:
                    if t == 0:
                        act.wait_ge(ln1b, i + 1)
                        wait(act, agg_done, i - 1)
                    if t == TILES:
                        wait(act, xT_done, i - 1)
                        wait(act, sx_ready, i - 1)
                    k = (t + TILES) % (2 * TILES)
                    to, of, ready = (xgn, xg, xgn_ready) if t < TILES else (xn, xb, xn_ready)
                    act.activation(to[u][:, t % TILES, :], of[u][:, t % TILES, :], ACT.Identity,
                                   bias=nm1[u][:, k:k + 1], scale=rs1[u][:, k:k + 1]).then_inc(ready, 1)

            def part(to, done, free, taken, j, u):
                i = no(j, u)
                act.wait_ge(done, i + 1)
                wait(act, h_done, 2 * (i - 1))
                for k in range(2):
                    act.activation(to[u][:, k, :], TP[k][:, :], ACT.Copy).then_inc(taken, 1)

            def x_part(j, u):
                part(xT_hi, xT_done, None, xhi, j, u)

            def m_part(j, u):
                part(mT_hi, mT_done, None, mhi, j, u)

            def both(j, u):
                deviations(j, u)
                normalise(j, u, range(2 * TILES))

            both(0, 0)
            both(0, 1)
            x_part(0, 0)
            m_part(0, 0)
            x_part(0, 1)
            both(1, 0)

            def body(j, u):
                i = no(j, u)
                for k in range(2):
                    act.wait_ge(h_done, 2 * i + k + 1)
                    wait(act, h_lo, 2 * (i - 1) + k + 1)
                    act.activation(ha[:, k, :], HB[k][:, :], ACT.Relu,
                                   bias=bcol[:, BCOLS["b1"] + k:BCOLS["b1"] + k + 1]).then_inc(h_relu, 1)
                    act.wait_ge(h_relu, 2 * i + k + 1)
                    wait(act, z_done, TILES * i)
                    act.activation(hh[:, k, :], ha[:, k, :], ACT.Copy).then_inc(h_hi, 1)
                    if k == 0 and exists(j, u, 3):
                        deviations(*ahead(j, u, 3))
                if exists(j, u, 1):
                    m_part(*ahead(j, u, 1))
                if exists(j, u, 2):
                    x_part(*ahead(j, u, 2))
                for t in range(TILES):
                    act.wait_ge(z_done, TILES * i + t + 1)
                    if t == 0:
                        wait(act, hl_out[u], 16 * j)
                        wait(act, z_ready, TILES * (i - 1))
                    act.activation(hl[u][:, t, :], ZB[t % 2][:, 0:D], ACT.Copy).then_inc(hl_ready, 1)
                    if exists(j, u, 3):
                        normalise(*ahead(j, u, 3), (2 * t, 2 * t + 1))

            pipeline(act, body)
            end_phase(act, 2)

            def normalise2(j, u, tiles):
                i = no(j, u)
                if 0 in tiles:
                    act.wait_ge(ln2a, i + 1)
                    act.activation(sd2[u][:, :], mv2[u][:, :, 1], ACT.Sqrt, bias=eps[:, 0:1]).then_inc(std2, 1)
                    act.wait_ge(ln2b, i + 1)
                    wait(act, yT_done, i - 1)
                for t in tiles:
                    act.activation(x2n[u][:, t, :], x2[u][:, t, :], ACT.Identity, bias=nm2[u][:, t:t + 1],
                                   scale=rs2[u][:, t:t + 1]).then_inc(x2n_ready, 1)

            def y_part(j, u):
                i = no(j, u)
                act.wait_ge(yT_done, i + 1)
                for k in range(2):
                    act.activation(yT_hi[u][:, k, :], TP[k][:, :], ACT.Copy).then_inc(yhi, 1)

            def relu(j, u, r):
                i = no(j, u)
                act.wait_ge(r_done, 9 * i + r + 1)
                wait(act, r_lo, 9 * (i - 1) + r + 1)
                c = BCOLS["sb1"] + r if r < 2 else BCOLS["eb1"] + r - 2 if r < 6 else \
                    {6: BCOLS["eb2"], 7: BCOLS["sb2"], 8: BCOLS["eb2"] + 1}[r]
                act.activation(act_a[:, r, :], RB[r % 2][:, :], ACT.Relu, bias=bcol[:, c:c + 1])\
                   .then_inc(r_relu, 1)
                if r < 6:
                    act.wait_ge(r_relu, 9 * i + r + 1)
                    wait(act, o_done, TILES * i)
                    act.activation(act_hi[:, r, :], act_a[:, r, :], ACT.Copy).then_inc(r_hi_a, 1)

            normalise2(0, 0, range(TILES))
            y_part(0, 0)

            def body2(j, u):
                i = no(j, u)
                act.wait_ge(gate_step, GATE_STEPS * i + GATE_EXP1)
                act.activation(g_t[1][:, :, :], g_t[1][:, :, :], ACT.Exp).then_inc(gate_exp, 1)
                relu(j, u, 0)
                relu(j, u, 1)
                act.wait_ge(gate_step, GATE_STEPS * i + GATE_EXP2)
                act.activation(g_s[6][:, :, :], g_s[6][:, :, :], ACT.Exp).then_inc(gate_exp, 1)
                for r in range(2, 5):
                    relu(j, u, r)
                act.wait_ge(wxT_done, i + 1)
                wait(act, o_done, TILES * i)
                act.activation(wxT[:, :], TP[1][0:96, :], ACT.Copy).then_inc(wxT_hi, 1)
                relu(j, u, 5)
                if exists(j, u, 1):
                    normalise2(*ahead(j, u, 1), (0, 1))
                relu(j, u, 6)
                if exists(j, u, 1):
                    normalise2(*ahead(j, u, 1), (2, 3))
                relu(j, u, 7)
                relu(j, u, 8)
                if exists(j, u, 1):
                    y_part(*ahead(j, u, 1))

            pipeline(act, body2)

        @block.vector
        def _(dve):
            step = [0]

            def link(ins):
                step[0] += 1
                ins.then_inc(dstep, 1)
                dve.wait_ge(dstep, step[0])

            dve.wait_ge(dst_in, 16)
            dve.tensor_scalar(ea[:, :], dstN[:, :], 12, None, ALU.logical_shift_right)
            link(dve.tensor_scalar(ec[:, :], dstN[:, :], 7, HC - 1, ALU.logical_shift_right, ALU.bitwise_and))
            dve.wait_ge(const_set, 2)

            def edge_hots(c, b, n):
                wait(dve, hist_step, n - 1)
                at = bass.ds(25 * c, 25) if not isinstance(c, int) else slice(25 * c, 25 * c + 25)
                dve.tensor_tensor(oa[:, b, :, :], ea[:, at].unsqueeze(2).to_broadcast([EP, 25, HA]),
                                  iot33[:, None, 0:HA].to_broadcast([EP, 25, HA]), ALU.is_equal)\
                   .then_inc(hot_edge, 1)
                dve.tensor_tensor(oc[:, b, :, :], ec[:, at].unsqueeze(2).to_broadcast([EP, 25, HC + 1]),
                                  iot33[:, None, :].to_broadcast([EP, 25, HC + 1]), ALU.is_lt)\
                   .then_inc(hot_edge, 1)

            edge_hots(0, 0, 0)
            edge_hots(1, 1, 1)
            with dve.Fori(1, 12) as j:
                edge_hots(2 * j, 0, 2 * j)
                edge_hots(2 * j + 1, 1, 2 * j + 1)
            edge_hots(24, 0, 24)

            dve.wait_ge(hist_done, 1)
            dve.tensor_copy(cum[:, :], ps[4][0:HA, 0:HC + 1]).then_inc(cum_ready, 1)
            dve.wait_ge(pre_done, 1)
            link(dve.tensor_copy(pre[:, :], ps[5][0:HA, 0:1]))
            dve.tensor_scalar(sti[:, :], cum[:, 0:HC], pre[:, 0:1], None, ALU.add).then_inc(sti_ready, 1)

            dve.wait_ge(w_in, 16)
            def w(name, **k):
                a, n = WCOLS[name]
                return wst[:, a:a + n].rearrange(*([k.pop("pat")]), **k) if k else wst[:, a:a + n]
            link(dve.memset(ew2_hi[:, :, :].bitcast(fp32), 0.0))
            link(dve.memset(ew2_lo[:, :, :].bitcast(fp32), 0.0))
            splits = [
                (w1_hi[:, 0], w1_lo[:, 0], w("w1l", pat="p (k n) -> p k n", k=2)),
                (w1_hi[:, 1], w1_lo[:, 1], w("w1r", pat="p (k n) -> p k n", k=2)),
                (w2_hi[:, :], w2_lo[:, :], w("w2", pat="p (k n) -> p k n", k=2)),
                (sw1_hi[:, :], sw1_lo[:, :], w("sw1", pat="p (k n) -> p k n", k=2)),
                (sw2_hi[:, :], sw2_lo[:, :], w("sw2", pat="p (k n) -> p k n", k=2)[:, :, 0:64]) if False else None,
                (sw3_hi[:, :], sw3_lo[:, :], w("sw3")),
                (ew1_hi[:, :, :, :].rearrange("p k e n -> p k (e n)"), ew1_lo[:, :, :, :].rearrange("p k e n -> p k (e n)"),
                 w("ew1", pat="p (k n) -> p k n", k=2)),
                (ew3_hi[:, :], ew3_lo[:, :], w("ew3", pat="p (k n) -> p k n", k=2)),
                (gw_hl[:, :, 0:NEXP], gw_hl[:, :, NEXP:2 * NEXP], w("gw", pat="p (k n) -> p k n", k=2)),
            ]
            splits = [s_ for s_ in splits if s_]
            splits.append((sw2_hi[:, :, :], sw2_lo[:, :, :], w("sw2", pat="p (k n) -> p k n", k=2)))
            for e in range(NEXP):
                c = 64 * (e % 2)
                a = WCOLS["ew2"][0] + 64 * e
                splits.append((ew2_hi[:, e, c:c + 64], ew2_lo[:, e, c:c + 64], wst[:, a:a + 64]))
            for hi_, _, of in splits:
                dve.tensor_copy(hi_, of).then_inc(dstep, 1)
                step[0] += 1
            dve.wait_ge(dstep, step[0])
            for hi_, lo_, of in splits:
                dve.tensor_tensor(lo_, of, hi_.bitcast(fp32), ALU.subtract)
            dve.tensor_copy(sel[:, :, :], selj[:, :].rearrange("r (q m) -> r q m", q=2))
            dve.wait_ge(bias_in, 96)
            link(dve.tensor_copy(b3s[:, :], b3f[:, :]))
            link(dve.tensor_tensor(b3s[64:96, :], b3f[64:96, :], b3s[64:96, :].bitcast(fp32), ALU.subtract))

            dve.wait_ge(starts_in, 16)
            link(dve.tensor_scalar(r0[:, :], s4[:, :], 6, None, ALU.logical_shift_right))
            link(dve.tensor_copy(r0f[:, :], r0[:, :]))
            for k in range(WK):
                ins = dve.tensor_scalar(ridx[:, :].rearrange("p (j k) -> p j k", k=WK)[:, :, k], r0f[:, :],
                                        float(k), None, ALU.add)
            ins.then_inc(ridx_ready, 1)
            link(dve.memset(vT[:, :, :, :], 1.0))

            dve.wait_ge(win_in, 16 * WJ * WK)

            def jk(t):
                return t[:, :, :].rearrange("p j (k w) -> p (j k) w", w=WROW)

            link(dve.tensor_copy(jk(wd), win[:, :, 0:WROW]))
            link(dve.tensor_copy(jk(ws), win[:, :, WROW:2 * WROW]))
            link(dve.tensor_scalar(jk(shi), win[:, :, WROW:2 * WROW], 8, None, ALU.logical_shift_right))
            link(dve.tensor_scalar(jk(slo), win[:, :, WROW:2 * WROW], 255, None, ALU.bitwise_and))
            for j in range(WJ):
                link(dve.tensor_scalar(wd[:, j, :], wd[:, j, :], tb[:, j:j + 1], None, ALU.subtract))
                link(dve.tensor_scalar(ws[:, j, :], ws[:, j, :], tb[:, j:j + 1], None, ALU.subtract))
            link(dve.tensor_scalar(wv[:, :, :], wd[:, :, :], 0.0, None, ALU.is_ge))
            link(dve.scalar_tensor_tensor(out=wv[:, :, :], in0=wd[:, :, :], scalar=float(P), in1=wv[:, :, :],
                                          op0=ALU.is_lt, op1=ALU.mult))
            link(dve.tensor_tensor(wn[:, :, :], ws[:, :, :], wd[:, :, :], ALU.not_equal))
            link(dve.tensor_tensor(wn[:, :, :], wn[:, :, :], wv[:, :, :], ALU.mult))
            for j in range(WJ):
                link(dve.tensor_tensor_scan(wc[:, j, :], wn[:, j, :], wn[:, j, :], 0.0, ALU.add, ALU.max))
            link(dve.tensor_tensor(wc[:, :, :], wc[:, :, :], wn[:, :, :], ALU.mult))
            link(dve.tensor_tensor(ws[:, :, :], wv[:, :, :], wn[:, :, :], ALU.subtract))
            link(dve.scalar_tensor_tensor(out=ws[:, :, :], in0=wd[:, :, :], scalar=float(P + 1), in1=ws[:, :, :],
                                          op0=ALU.add, op1=ALU.mult))
            link(dve.scalar_tensor_tensor(out=wk_[:, :, :], in0=wc[:, :, :], scalar=-1.0, in1=ws[:, :, :],
                                          op0=ALU.add, op1=ALU.add))
            link(dve.tensor_copy(ws[:, :, :], shi[:, :, :]))
            link(dve.tensor_copy(wn[:, :, :], slo[:, :, :]))
            dve.sem_inc(fields_ready, 1)

            dve.wait_ge(ft_taken, 12)

            def key_hots(j, u):
                i = no(j, u)
                wait(dve, slots_done, i - 1)
                for t in range(TILES):
                    for q, (_, n) in enumerate(CHUNKS):
                        c = i * TILES + t
                        c = slice(c, c + 1) if isinstance(c, int) else bass.ds(c, 1)
                        ins = dve.tensor_scalar(hot[0:n, u, t, q, :], iob[0:n, :], keyT[0:n, q, c], None,
                                                ALU.is_equal)
                ins.then_inc(hot_ready, 1)

            for u in range(2):
                key_hots(0, u)
            with dve.Fori(1, GROUPS // 2) as j:
                for u in range(2):
                    key_hots(j, u)
            dve.wait_ge(slots_taken, GROUPS)
            link(dve.scalar_tensor_tensor(out=idxf[:, :], in0=info[:, :, 0], scalar=256.0, in1=info[:, :, 1],
                                          op0=ALU.mult, op1=ALU.add))
            link(dve.scalar_tensor_tensor(out=idxf[:, :], in0=info[:, :, 3], scalar=-OOB, in1=idxf[:, :],
                                          op0=ALU.mult, op1=ALU.add))
            link(dve.tensor_scalar(idx_all[:, :], idxf[:, :], OOB, None, ALU.add))
            link(dve.scalar_tensor_tensor(out=dloc_all[:, :], in0=info[:, :, 3], scalar=-1000.0, in1=info[:, :, 2],
                                          op0=ALU.mult, op1=ALU.add))
            link(dve.tensor_scalar(dloc_all[:, :], dloc_all[:, :], 1000.0, None, ALU.add))

            def slot_hots(j, u):
                i = no(j, u)
                wait(dve, cnt_done, i - 1)
                for t in range(TILES):
                    ins = dve.tensor_scalar(mh[:, u, t, :], iob[:, 0:P], col(dloc_all, j, u, t), None, ALU.is_equal)
                ins.then_inc(mh_ready, 1)

            for u in range(2):
                slot_hots(0, u)
            with dve.Fori(1, GROUPS // 2) as j:
                for u in range(2):
                    slot_hots(j, u)
            dve.wait_ge(cnt_taken, GROUPS)
            link(dve.tensor_tensor(cnt[:, :], cnt[:, :], info[:, :, 7], ALU.add))
            link(dve.tensor_scalar(cnt[:, :], cnt[:, :], 1.0, None, ALU.max))
            link(dve.reciprocal(inv_all[:, :], cnt[:, :]))
            link(dve.tensor_tensor(sinv_all[:, :], inv_all[:, :], info[:, :, 7], ALU.mult))
            end_phase(dve, 1)

            def statistics(j, u):
                i = no(j, u)
                dve.wait_ge(x_in[u], 32 * (j + 1))
                wait(dve, xgn_ready, TILES * (i - 1))
                wait(dve, xn_ready, TILES * (i - 1))
                for t in range(TILES):
                    dve.bn_stats(st1[u][:, t, :], xb[u][:, t, :]).then_inc(stats1, 1)
                dve.wait_ge(xg_in[u], 64 * (j + 1))
                for t in range(TILES):
                    dve.bn_stats(st1[u][:, TILES + t, :], xg[u][:, t, :]).then_inc(stats1, 1)
                dve.wait_ge(stats1, 2 * TILES * (i + 1))
                wait(dve, agg_done, i - 1)
                for t in range(TILES):
                    dve.tensor_scalar(m1[u][:, t, :], iota[:, 0:P], col(dloc_all, j, u, t), None,
                                      ALU.is_equal).then_inc(m1_ready, 1)
                for t in range(2 * TILES):
                    ins = dve.bn_aggr(mv1[u][:, t, :], st1[u][:, t, :])
                ins.then_inc(ln1a, 1)

            def scales(j, u):
                i = no(j, u)
                dve.wait_ge(std1, i + 1)
                dve.reciprocal(rs1[u][:, :], sd1[u][:, :]).then_inc(rstd1, 1)
                dve.wait_ge(rstd1, i + 1)
                dve.scalar_tensor_tensor(out=nm1[u][:, :], in0=mv1[u][:, :, 0], scalar=-1.0, in1=rs1[u][:, :],
                                         op0=ALU.mult, op1=ALU.mult).then_inc(ln1b, 1)

            def remainder(to, hi_, done, taken, taken_hi, j, u):
                i = no(j, u)
                for k in range(2):
                    dve.wait_ge(taken_hi, 2 * i + k + 1)
                    dve.tensor_tensor(to[u][:, k, :], TP[k][:, :], hi_[u][:, k, :].bitcast(fp32),
                                      ALU.subtract).then_inc(taken, 1)

            def means(j, u):
                i = no(j, u)
                dve.wait_ge(agg_done, i + 1)
                dve.wait_ge(sx_ready, i + 1)
                wait(dve, mT_done, i - 1)
                for t in range(TILES):
                    c = (t % 2) * D
                    dve.scalar_tensor_tensor(out=mean[u][:, t, :], in0=AG[t // 2][:, c:c + D],
                                             scalar=col(inv_all, j, u, t), in1=sx[u][:, t, :],
                                             op0=ALU.mult, op1=ALU.add).then_inc(mean_ready, 1)

            def x_rest(j, u):
                remainder(xT_lo, xT_hi, xT_done, xlo, xhi, j, u)

            def m_rest(j, u):
                remainder(mT_lo, mT_hi, mT_done, mlo, mhi, j, u)

            for g in range(2):
                statistics(0, g)
                scales(0, g)
            means(0, 0)
            x_rest(0, 0)
            m_rest(0, 0)
            x_rest(0, 1)
            means(0, 1)
            statistics(1, 0)
            scales(1, 0)

            def body(j, u):
                i = no(j, u)
                if exists(j, u, 3):
                    statistics(*ahead(j, u, 3))
                for k in range(2):
                    dve.wait_ge(h_hi, 2 * i + k + 1)
                    wait(dve, z_done, TILES * i)
                    dve.tensor_tensor(hlo[:, k, :], ha[:, k, :], hh[:, k, :].bitcast(fp32),
                                      ALU.subtract).then_inc(h_lo, 1)
                    if k == 0 and exists(j, u, 3):
                        scales(*ahead(j, u, 3))
                if exists(j, u, 1):
                    m_rest(*ahead(j, u, 1))
                if exists(j, u, 2):
                    means(*ahead(j, u, 2))
                    x_rest(*ahead(j, u, 2))
                wait(dve, z_out[u], 16 * j)
                for t in range(TILES):
                    dve.wait_ge(hl_ready, TILES * i + t + 1)
                    dve.scalar_tensor_tensor(out=zs[u][:, t, :], in0=hl[u][:, t, :],
                                             scalar=col(sinv_all, j, u, t), in1=ZB[t % 2][:, D:2 * D],
                                             op0=ALU.mult, op1=ALU.add).then_inc(z_ready, 1)

            pipeline(dve, body)
            end_phase(dve, 2)

            def slots2(j, u):
                wait(dve, agg2_done, no(j, u) - 1)
                for t in range(TILES):
                    dve.tensor_scalar(m2[u][:, t, :], iota[:, 0:P], col(dloc_all, j, u, t), None,
                                      ALU.is_equal).then_inc(m2_ready, 1)

            def second(j, u):
                i = no(j, u)
                dve.wait_ge(agg2_done, i + 1)
                dve.wait_ge(xb_ready, 2 * (i + 1))
                for t in range(TILES):
                    c = (t % 2) * D
                    dve.scalar_tensor_tensor(out=x2[u][:, t, :], in0=AG[t // 2][:, c:c + D],
                                             scalar=col(inv_all, j, u, t), in1=zb[u][:, t, :],
                                             op0=ALU.mult, op1=ALU.add).then_inc(x2_ready, 1)

            def statistics2(j, u):
                i = no(j, u)
                for t in range(TILES):
                    dve.wait_ge(x2_ready, TILES * i + t + 1)
                    dve.bn_stats(st2[u][:, t, :], x2[u][:, t, :]).then_inc(stats2, 1)
                dve.wait_ge(stats2, TILES * (i + 1))
                if exists(j, u, 1):
                    slots2(*ahead(j, u, 1))
                for t in range(TILES):
                    ins = dve.bn_aggr(mv2[u][:, t, :], st2[u][:, t, :])
                ins.then_inc(ln2a, 1)

            def scales2(j, u):
                i = no(j, u)
                dve.wait_ge(std2, i + 1)
                dve.reciprocal(rs2[u][:, :], sd2[u][:, :]).then_inc(rstd2, 1)
                dve.wait_ge(rstd2, i + 1)
                dve.scalar_tensor_tensor(out=nm2[u][:, :], in0=mv2[u][:, :, 0], scalar=-1.0, in1=rs2[u][:, :],
                                         op0=ALU.mult, op1=ALU.mult).then_inc(ln2b, 1)

            def y_rest(j, u):
                i = no(j, u)
                for k in range(2):
                    dve.wait_ge(yhi, 2 * i + k + 1)
                    dve.tensor_tensor(yT_lo[u][:, k, :], TP[k][:, :], yT_hi[u][:, k, :].bitcast(fp32),
                                      ALU.subtract).then_inc(ylo, 1)

            def rest(j, u, r):
                i = no(j, u)
                dve.wait_ge(r_relu, 9 * i + r + 1)
                if r in (6, 8):
                    q = (r - 6) // 2
                    dve.wait_ge(wb_done, 2 * i + q + 1)
                    dve.tensor_tensor(act_a[:, r, :], act_a[:, r, :], WB[:, :], ALU.mult).then_inc(wb_taken, 1)
                    dve.wait_ge(wb_taken, 2 * i + q + 1)
                wait(dve, o_done, TILES * i)
                if r >= 6:
                    dve.tensor_copy(act_hi[:, r, :], act_a[:, r, :]).then_inc(r_hi_v, 1)
                    dve.wait_ge(r_hi_v, 3 * i + r - 5)
                else:
                    dve.wait_ge(r_hi_a, 6 * i + r + 1)
                dve.tensor_tensor(act_lo[:, r, :], act_a[:, r, :], act_hi[:, r, :].bitcast(fp32),
                                  ALU.subtract).then_inc(r_lo, 1)

            def gates(j, u):
                i = no(j, u)
                n = [0]
                B = [P, TILES, NEXP]
                S = [P, TILES, 1]
                lgt, d, c1, oh1, e2, q2, oh2, w1, w2 = (t[:, :, :] for t in g_t)
                mx, sm, ri, m1_, v2, m2_, d2, den, a1, a2 = (t[:, :, :] for t in g_s)
                lgs = TP[0][:, 0:8 * TILES].rearrange("p (t k) -> p t k", k=8)

                def done(ins):
                    n[0] += 1
                    ins.then_inc(gate_step, 1)

                def due():
                    dve.wait_ge(gate_step, GATE_STEPS * i + n[0])

                dve.wait_ge(lg_done, i + 1)
                done(dve.tensor_tensor(lgt, lgs[:, :, 0:NEXP], gbb[:, None, :].to_broadcast(B), ALU.add))
                yield
                due()
                done(dve.tensor_tensor(lgt, lgt, lgs[:, :, NEXP:2 * NEXP], ALU.add))
                yield
                due()
                done(dve.tensor_reduce(mx, lgt, AX.X, ALU.max))
                yield
                due()
                done(dve.tensor_tensor(d, lgt, mx.to_broadcast(B), ALU.subtract))
                done(dve.scalar_tensor_tensor(out=c1, in0=lgt, scalar=1.0, in1=mx.to_broadcast(B),
                                              op0=ALU.mult, op1=ALU.is_equal))
                assert n[0] == GATE_EXP1 + 1
                yield
                due()
                done(dve.tensor_tensor(c1, c1, prio[:, :, :], ALU.mult))
                yield
                due()
                done(dve.tensor_reduce(m1_, c1, AX.X, ALU.max))
                yield
                due()
                done(dve.tensor_tensor(oh1, c1, m1_.to_broadcast(B), ALU.is_equal))
                yield
                due()
                dve.wait_ge(gate_exp, 2 * i + 1)
                done(dve.tensor_reduce(sm, d, AX.X, ALU.add))
                done(dve.scalar_tensor_tensor(out=e2, in0=oh1, scalar=-4.0, in1=d, op0=ALU.mult, op1=ALU.add))
                yield
                due()
                done(dve.reciprocal(ri, sm))
                done(dve.tensor_reduce(v2, e2, AX.X, ALU.max))
                yield
                due()
                done(dve.scalar_tensor_tensor(out=d2, in0=v2, scalar=-1.0, in1=ri, op0=ALU.add, op1=ALU.mult))
                assert n[0] == GATE_EXP2
                done(dve.tensor_tensor(q2, e2, v2.to_broadcast(B), ALU.is_equal))
                yield
                due()
                done(dve.tensor_tensor(q2, q2, prio[:, :, :], ALU.mult))
                yield
                due()
                done(dve.tensor_reduce(m2_, q2, AX.X, ALU.max))
                yield
                due()
                done(dve.tensor_tensor(oh2, q2, m2_.to_broadcast(B), ALU.is_equal))
                yield
                due()
                dve.wait_ge(gate_exp, 2 * i + 2)
                done(dve.tensor_scalar(den, d2, 1.0, None, ALU.add))
                yield
                due()
                done(dve.reciprocal(a1, den))
                yield
                due()
                done(dve.tensor_tensor(a2, d2, a1, ALU.mult))
                done(dve.tensor_tensor(w1, oh1, a1.to_broadcast(B), ALU.mult))
                yield
                due()
                done(dve.tensor_tensor(w2, oh2, a2.to_broadcast(B), ALU.mult))
                yield
                due()
                wait(dve, wxT_done, i)
                for c in (0, 32, 64):
                    ins = dve.tensor_tensor(wx[:, :, c:c + NEXP], w1, w2, ALU.add)
                ins.then_inc(wx_ready, 1)
                assert n[0] == GATE_STEPS, n[0]

            slots2(0, 0)
            second(0, 0)
            statistics2(0, 0)
            scales2(0, 0)
            y_rest(0, 0)

            def body2(j, u):
                i = no(j, u)
                gate = gates(j, u)

                def gate_to(n):
                    for _ in range(n):
                        next(gate, None)

                gate_to(5)
                rest(j, u, 0)
                gate_to(2)
                rest(j, u, 1)
                gate_to(7)
                if exists(j, u, 1):
                    second(*ahead(j, u, 1))
                rest(j, u, 2)
                gate_to(20)
                if exists(j, u, 1):
                    statistics2(*ahead(j, u, 1))
                rest(j, u, 3)
                rest(j, u, 4)
                dve.wait_ge(wxT_hi, i + 1)
                dve.tensor_tensor(wxT[32:64, :], TP[1][32:64, :], wxT[32:64, :].bitcast(fp32),
                                  ALU.subtract).then_inc(wxT_lo, 1)
                rest(j, u, 5)
                if exists(j, u, 1):
                    scales2(*ahead(j, u, 1))
                for r in (6, 7, 8):
                    rest(j, u, r)
                wait(dve, o_out[u], 32 * j)
                for t in range(TILES):
                    if t == 2 and exists(j, u, 1):
                        y_rest(*ahead(j, u, 1))
                    dve.wait_ge(o_done, TILES * i + t + 1)
                    dve.tensor_tensor(ob[u][:, t, :], OBS[t % 2][:, 0:D], x2[u][:, t, :],
                                      ALU.add).then_inc(o_ready, 1)

            pipeline(dve, body2)

        @block.tensor
        def _(pe):
            hist = ps[4][0:HA, 0:HC + 1]

            def histogram(b, n, first=False, last=False):
                pe.wait_ge(hot_edge, 2 * n + 2)
                for k in range(25):
                    ins = pe.matmul(hist, oa[:, b, k, :], oc[:, b, k, :], start=first and k == 0,
                                    stop=last and k == 24)
                ins.then_inc(hist_step, 1)
                return ins

            histogram(0, 0, first=True)
            histogram(1, 1)
            with pe.Fori(1, 12) as j:
                histogram(0, 2 * j)
                histogram(1, 2 * j + 1)
            histogram(0, 24, last=True)
            pe.wait_ge(hist_step, 25)
            pe.nop().then_inc(hist_done, 1)
            pe.wait_ge(cum_ready, 1)
            pe.wait_ge(const_set, 2)
            pe.matmul(ps[5][0:HA, 0:1], tri[:, :], cum[:, HC:HC + 1], start=True, stop=True).then_inc(pre_done, 1)
            pe.wait_ge(fields_ready, 1)
            for f, t in enumerate((wk_, ws, wn, wd)):
                for q, (c, n) in enumerate(CHUNKS):
                    k = 3 * f + q
                    wait(pe, ft_taken, k - 3)
                    for j in range(WJ):
                        ins = pe.transpose(ps[k % 4][0:n, P * j:P * j + P], t[:, j, c:c + n], ident[:, :])
                    ins.then_inc(ft_done, 1)
            pe.wait_ge(ft_taken, 12)

            def pack(j, u):
                i = no(j, u)
                pe.wait_ge(hot_ready, i + 1)
                wait(pe, slots_taken, i - 1)
                for t in range(TILES):
                    c = (i * TILES + t) * 4
                    c = slice(c, c + 4) if isinstance(c, int) else bass.ds(c, 4)
                    for part in range(2):
                        o = ps[u][:, 8 * t + 4 * part:8 * t + 4 * part + 4]
                        for q, (_, n) in enumerate(CHUNKS):
                            ins = pe.matmul(o, hot[0:n, u, t, q, P * part:P * part + P],
                                            vT[0:n, q, :, :].rearrange("p b k -> p (b k)")[:, c],
                                            start=q == 0, stop=q == 2)
                ins.then_inc(slots_done, 1)

            for u in range(2):
                pack(0, u)
            with pe.Fori(1, GROUPS // 2) as j:
                for u in range(2):
                    pack(j, u)
            pe.wait_ge(slots_taken, GROUPS)

            def count(j, u):
                i = no(j, u)
                pe.wait_ge(mh_ready, i + 1)
                wait(pe, cnt_taken, i - 1)
                for t in range(TILES):
                    ins = pe.matmul(ps[u][:, t:t + 1], mh[:, u, t, :], oneb[:, 0:1], start=True, stop=True)
                ins.then_inc(cnt_done, 1)

            for u in range(2):
                count(0, u)
            with pe.Fori(1, GROUPS // 2) as j:
                for u in range(2):
                    count(j, u)
            end_phase(pe, 1)

            def aggregate(j, u):
                i = no(j, u)
                pe.wait_ge(m1_ready, TILES * (i + 1))
                wait(pe, mean_ready, TILES * i)
                for t in range(TILES):
                    pe.wait_ge(xgn_ready, TILES * i + t + 1)
                    c = (t % 2) * D
                    ins = pe.matmul(AG[t // 2][:, c:c + D], m1[u][:, t, :], xgn[u][:, t, :], start=True, stop=True)
                ins.then_inc(agg_done, 1)
                wait(pe, mhi, 2 * i)
                wait(pe, mlo, 2 * i)
                pe.wait_ge(xn_ready, TILES * (i + 1))
                for k in range(2):
                    for t in range(TILES):
                        ins = pe.transpose(TP[k][:, P * t:P * t + P], xn[u][:, t, P * k:P * k + P], ident[:, :])
                ins.then_inc(xT_done, 1)

            def transpose_means(j, u):
                i = no(j, u)
                pe.wait_ge(mean_ready, TILES * (i + 1))
                pe.wait_ge(xhi, 2 * (i + 1))
                pe.wait_ge(xlo, 2 * (i + 1))
                for k in range(2):
                    for t in range(TILES):
                        ins = pe.transpose(TP[k][:, P * t:P * t + P], mean[u][:, t, P * k:P * k + P], ident[:, :])
                ins.then_inc(mT_done, 1)

            def layer(j, u):
                i = no(j, u)
                pe.wait_ge(mhi, 2 * (i + 1))
                pe.wait_ge(mlo, 2 * (i + 1))
                for k in range(2):
                    wait(pe, h_relu, 2 * (i - 1) + k + 1)
                    c = slice(P * k, P * k + P)
                    terms = [(side, kk) for side in range(2) for kk in range(2)]
                    for n, (side, kk) in enumerate(terms):
                        hi_, lo_ = (mT_hi, mT_lo) if side == 0 else (xT_hi, xT_lo)
                        ins = mm3(pe, HB[k][:, :], w1_hi[:, side, kk, c], w1_lo[:, side, kk, c],
                                  hi_[u][:, kk, :], lo_[u][:, kk, :], n == 0, n == 3)
                    ins.then_inc(h_done, 1)

            def second_layer(j, u):
                i = no(j, u)
                for t in range(TILES):
                    wait(pe, z_ready, TILES * i + t - 1)
                    for k in range(2):
                        if t == 0:
                            pe.wait_ge(h_hi, 2 * i + k + 1)
                            pe.wait_ge(h_lo, 2 * i + k + 1)
                        c = slice(P * t, P * t + P)
                        ins = mm3(pe, ZB[t % 2][:, :], hh[:, k, c], hlo[:, k, c], w2_hi[:, k, :], w2_lo[:, k, :],
                                  k == 0, k == 1)
                    ins.then_inc(z_done, 1)

            aggregate(0, 0)
            transpose_means(0, 0)
            aggregate(0, 1)

            def body(j, u):
                layer(j, u)
                if exists(j, u, 1):
                    transpose_means(*ahead(j, u, 1))
                if exists(j, u, 2):
                    aggregate(*ahead(j, u, 2))
                second_layer(j, u)

            pipeline(pe, body)
            end_phase(pe, 2)

            def aggregate2(j, u):
                i = no(j, u)
                pe.wait_ge(m2_ready, TILES * (i + 1))
                pe.wait_ge(gg_in[u], 64 * (j + 1))
                wait(pe, x2_ready, TILES * i)
                for t in range(TILES):
                    c = (t % 2) * D
                    ins = pe.matmul(AG[t // 2][:, c:c + D], m2[u][:, t, :], gg[u][:, t, :], start=True, stop=True)
                ins.then_inc(agg2_done, 1)

            def transpose_rows(j, u):
                i = no(j, u)
                pe.wait_ge(x2n_ready, TILES * (i + 1))
                wait(pe, gate_step, GATE_STEPS * (i - 1) + 2)
                wait(pe, wxT_lo, i)
                for k in range(2):
                    for t in range(TILES):
                        ins = pe.transpose(TP[k][:, P * t:P * t + P], x2n[u][:, t, P * k:P * k + P], ident[:, :])
                ins.then_inc(yT_done, 1)

            def first_product(j, u, r):
                i = no(j, u)
                wait(pe, r_relu, 9 * i + (r - 1 if r >= 2 else 0))
                for k in range(2):
                    if r < 2:
                        l_hi, l_lo = sw1_hi[:, k, P * r:P * r + P], sw1_lo[:, k, P * r:P * r + P]
                    else:
                        l_hi, l_lo = ew1_hi[:, k, r - 2, :], ew1_lo[:, k, r - 2, :]
                    ins = mm3(pe, RB[r % 2][:, :], l_hi, l_lo, yT_hi[u][:, k, :], yT_lo[u][:, k, :],
                              k == 0, k == 1)
                ins.then_inc(r_done, 1)

            def second_product(j, u, r):
                i = no(j, u)
                pe.wait_ge(r_relu, 9 * i + r - 1)
                for k in range(2):
                    if r == 7:
                        of, l_hi, l_lo = k, sw2_hi[:, k, :], sw2_lo[:, k, :]
                    else:
                        e = (r - 6) + k
                        of, l_hi, l_lo = 2 + e, ew2_hi[:, e, :], ew2_lo[:, e, :]
                    pe.wait_ge(r_hi_a, 6 * i + of + 1)
                    pe.wait_ge(r_lo, 9 * i + of + 1)
                    ins = mm3(pe, RB[r % 2][:, :], l_hi, l_lo, act_hi[:, of, :], act_lo[:, of, :], k == 0, k == 1)
                ins.then_inc(r_done, 1)

            def spread(j, u, q):
                i = no(j, u)
                wait(pe, wb_taken, 2 * i + q)
                wait(pe, o_ready, TILES * i)
                pe.matmul(WB[:, :], sel[:, q, :], wxT[:, :], start=True, stop=True).then_inc(wb_done, 1)

            def out_terms(j, u, t, terms, first, last):
                i = no(j, u)
                c = slice(P * t, P * t + P)
                o = OBS[t % 2][:, 0:D]
                for n, term in enumerate(terms):
                    f, l = first and n == 0, last and n == len(terms) - 1
                    if term == "bias":
                        ins = pe.matmul(o, wxT[:, c], b3s[:, :], start=f, stop=l)
                        continue
                    r = {"pair0": 6, "shared": 7, "pair1": 8}[term]
                    pe.wait_ge(r_hi_v, 3 * i + r - 5)
                    pe.wait_ge(r_lo, 9 * i + r + 1)
                    w_hi, w_lo = (sw3_hi[:, :], sw3_lo[:, :]) if r == 7 else \
                        (ew3_hi[:, (r - 6) // 2, :], ew3_lo[:, (r - 6) // 2, :])
                    ins = mm3(pe, o, act_hi[:, r, c], act_lo[:, r, c], w_hi, w_lo, f, l)
                return ins

            aggregate2(0, 0)
            transpose_rows(0, 0)

            def body2(j, u):
                i = no(j, u)
                pe.wait_ge(yhi, 2 * (i + 1))
                pe.wait_ge(ylo, 2 * (i + 1))
                for t in range(TILES):
                    c = slice(P * t, P * t + P)
                    for k in range(2):
                        pe.matmul(TP[0][:, 8 * t:8 * t + 8], yT_hi[u][:, k, c], gw_hl[:, k, :],
                                  start=k == 0, stop=False)
                        ins = pe.matmul(TP[0][:, 8 * t:8 * t + 8], yT_lo[u][:, k, c], gw_hl[:, k, :],
                                        start=False, stop=k == 1)
                ins.then_inc(lg_done, 1)
                for r in range(2):
                    first_product(j, u, r)
                if exists(j, u, 1):
                    aggregate2(*ahead(j, u, 1))
                for r in range(2, 5):
                    first_product(j, u, r)
                pe.wait_ge(wx_ready, i + 1)
                for t in range(TILES):
                    ins = pe.transpose(TP[1][0:96, P * t:P * t + P], wx[:, t, :], ident[:, :])
                ins.then_inc(wxT_done, 1)
                first_product(j, u, 5)
                pe.wait_ge(wxT_lo, i + 1)
                spread(j, u, 0)
                second_product(j, u, 6)
                second_product(j, u, 7)
                spread(j, u, 1)
                second_product(j, u, 8)
                if exists(j, u, 1):
                    transpose_rows(*ahead(j, u, 1))
                for t in range(2):
                    if t == 1:
                        pe.wait_ge(wb_taken, 2 * i + 2)
                    out_terms(j, u, t, ("pair0", "bias", "shared"), True, False)
                for t in range(2):
                    out_terms(j, u, t, ("pair1",), False, True).then_inc(o_done, 1)
                for t in range(2, TILES):
                    pe.wait_ge(o_ready, TILES * i + t - 1)
                    out_terms(j, u, t, ("pair0", "bias", "shared", "pair1"), True, True).then_inc(o_done, 1)

            pipeline(pe, body2)


def _cols(w):
    k = w.shape[0] // P
    return w.reshape(k, P, w.shape[1]).transpose(1, 0, 2).reshape(P, -1)


def kernel(**inputs):
    import numpy as np
    import concourse.bacc as bacc
    from concourse.bass_utils import run_bass_kernel_spmd

    a = {k.replace("L0_gnn_", "").replace("L0_ffn_", ""): np.asarray(v) for k, v in inputs.items()}
    w2 = np.concatenate([a["W2l"].T, a["W2r"].T], axis=1)
    ew1 = a["eW1"].transpose(1, 0, 2).reshape(D, NEXP * P)
    ew2 = a["eW2"].transpose(1, 0, 2).reshape(P, NEXP * 64)
    ew3 = a["eW3"].reshape(NEXP * 64, D)
    parts = [_cols(m) for m in (a["W1l"].T, a["W1r"].T, w2, a["sW1"])]
    parts += [_cols(a["sW2"]), a["sW3"], _cols(ew1), ew2, _cols(ew3), _cols(a["gW"])]
    bias = [a["b1"].reshape(2, P).T, a["sb1"].reshape(2, P).T, a["sb2"].reshape(1, P).T,
            a["eb1"].T, a["eb2"].reshape(2, P).T]
    arrays = {
        "x": a["x"], "src": a["src"], "dst": a["dst"],
        "wpack": np.ascontiguousarray(np.concatenate(parts, axis=1)),
        "bpack": np.ascontiguousarray(np.concatenate(bias, axis=1)),
        "b2": a["b2"], "gb": a["gb"],
        "b3": np.ascontiguousarray(np.concatenate([a["eb3"], a["sb3"][None]], axis=0)),
    }
    nc = bacc.Bacc("TRN2", target_bir_lowering=False, num_devices=1)
    args = [nc.dram_tensor(f"in_{n}", v.shape, mybir.dt.from_np(v.dtype), kind="ExternalInput").ap()
            for n, v in arrays.items()]
    out = nc.dram_tensor("out_x", (N, D), mybir.dt.float32, kind="ExternalOutput").ap()
    build(nc, *args, out)
    r = run_bass_kernel_spmd(nc, [{f"in_{n}": v for n, v in arrays.items()}], core_ids=[0])
    return r.results[0]["out_x"]
```

```python
import concourse.bass as bass
from concourse import mybir
from contextlib import ExitStack

N, E, D, P = 50000, 75000, 256, 128
TILES = 4
ROWS = TILES * P
GROUPS = -(-N // ROWS)
NPAD = GROUPS * ROWS
NBLK = GROUPS * TILES
LAST = N - (GROUPS - 1) * ROWS
EPS = 1e-5
NEXP = 4

WROW, WK = 64, 5
WIN = WROW * WK
ETROWS = E // WROW + 1 + WK + 1
FAR = 1 << 20
WJ = 4
CHUNKS = [(0, 128), (128, 128), (256, 64)]
EP, EC = 120, 625
assert EP * EC == E
HA, HC = 16, 32
OOB = 65536.0

WCOLS = {}
_at = 0
for _name, _n in (("w1l", 512), ("w1r", 512), ("w2", 1024), ("sw1", 512), ("sw2", 256),
                  ("sw3", 256), ("ew1", 1024), ("ew2", 256), ("ew3", 512), ("gw", 8)):
    WCOLS[_name] = (_at, _n)
    _at += _n
WTOTAL = _at
BCOLS = {"b1": 0, "sb1": 2, "sb2": 4, "eb1": 5, "eb2": 9}
BTOTAL = 11

GATE_STEPS, GATE_EXP1, GATE_EXP2 = 22, 4, 13
GATE_AHEAD = (4, 1, 6, 2)


def build(nc, x, src, dst, wpack, bpack, b2, gb, b3, out):
    fp32, fr, bf16 = mybir.dt.float32, mybir.dt.float32r, mybir.dt.bfloat16
    i32, u32 = mybir.dt.int32, mybir.dt.uint32
    ALU, ACT, AX = mybir.AluOpType, mybir.ActivationFunctionType, mybir.AxisListType

    edges = nc.dram_tensor("edge_table", [ETROWS, 2 * WROW], i32, kind="Internal").ap()
    starts = nc.dram_tensor("tile_starts", [HA * HC], i32, kind="Internal").ap()
    hl_d = nc.dram_tensor("hl_rows", [NPAD, D], fp32, kind="Internal").ap()
    z_d = nc.dram_tensor("z_rows", [NPAD, D], fp32, kind="Internal").ap()
    sums_d = nc.dram_tensor("general_sums", [NPAD, D], fp32, kind="Internal").ap()

    ctx = ExitStack()
    with ctx:
        def sb(name, shape, dt=fp32, scope=ctx):
            return scope.enter_context(nc.sbuf_tensor(name, shape, dt))

        def sem(name):
            return ctx.enter_context(nc.semaphore(name))

        def sems(name, n=2):
            return [sem(f"{name}{k}") for k in range(n)]

        w1_hi, w1_lo = (sb(f"w1_{h}", [P, 2, 2, D], fr) for h in ("hi", "lo"))
        w2_hi, w2_lo = (sb(f"w2_{h}", [P, 2, 2 * D], fr) for h in ("hi", "lo"))
        sw1_hi, sw1_lo = (sb(f"sw1_{h}", [P, 2, D], fr) for h in ("hi", "lo"))
        sw2_hi, sw2_lo = (sb(f"sw2_{h}", [P, 2, P], fr) for h in ("hi", "lo"))
        sw3_hi, sw3_lo = (sb(f"sw3_{h}", [P, D], fr) for h in ("hi", "lo"))
        ew1_hi, ew1_lo = (sb(f"ew1_{h}", [P, 2, NEXP, P], fr) for h in ("hi", "lo"))
        ew2_hi, ew2_lo = (sb(f"ew2_{h}", [P, NEXP, P], fr) for h in ("hi", "lo"))
        ew3_hi, ew3_lo = (sb(f"ew3_{h}", [P, 2, D], fr) for h in ("hi", "lo"))
        gw_hl = sb("gw_hl", [P, 2, 2 * NEXP], fr)
        b3s = sb("b3s", [96, D], fr)
        sel = sb("sel", [96, 2, P], fr)
        bcol = sb("bcol", [P, BTOTAL])
        b2b = sb("b2b", [P, D])
        gbb = sb("gbb", [P, NEXP])
        prio = sb("prio", [P, TILES, NEXP])
        ident = sb("ident", [P, P])
        iota = sb("iota", [P, D])
        eps = sb("eps", [P, 1])
        idx_all = sb("idx_all", [P, NBLK], u32)
        dloc_all = sb("dloc_all", [P, NBLK])
        inv_all = sb("inv_all", [P, NBLK])
        sinv_all = sb("sinv_all", [P, NBLK])
        gen, own, neg_own = sb("gen", [P, 1]), sb("own", [P, 1]), sb("neg_own", [P, 1])
        gen_i = sb("gen_i", [1, 1], i32)

        prep = ExitStack()
        wst = sb("wst", [P, WTOTAL], scope=prep)
        b3f = sb("b3f", [96, D], scope=prep)
        selj = sb("selj", [96, 2 * P], scope=prep)
        win = sb("win", [P, WJ * WK, 2 * WROW], i32, scope=prep)
        dstN = sb("dstN", [EP, EC], i32, scope=prep)
        ea, ec = (sb(n, [EP, EC], i32, scope=prep) for n in ("ea", "ec"))
        oa = sb("oa", [EP, 2, 25, HA], bf16, scope=prep)
        oc = sb("oc", [EP, 2, 25, HC + 1], bf16, scope=prep)
        iot33 = sb("iot33", [EP, HC + 1], scope=prep)
        tri = sb("tri", [HA, HA], scope=prep)
        cum = sb("cum", [HA, HC + 1], scope=prep)
        pre = sb("pre", [HA, 1], scope=prep)
        sti = sb("sti", [HA, HC], i32, scope=prep)
        s4 = sb("s4", [P, WJ], i32, scope=prep)
        r0 = sb("r0", [P, WJ], i32, scope=prep)
        r0f = sb("r0f", [P, WJ], scope=prep)
        ridx = sb("ridx", [P, WJ * WK], u32, scope=prep)
        far = sb("far", [P, 2 * WROW], i32, scope=prep)
        tb = sb("tb", [P, WJ], scope=prep)
        wd, ws, wv, wn, wc, wk_ = (sb(n, [P, WJ, WIN], scope=prep)
                                   for n in ("wd", "ws", "wv", "wn", "wc", "wk_"))
        shi = sb("shi", [P, WJ, WIN], i32, scope=prep)
        slo = sb("slo", [P, WJ, WIN], i32, scope=prep)
        keyT = sb("keyT", [P, 3, WJ * P], scope=prep)
        vT = sb("vT", [P, 3, WJ * P, 4], bf16, scope=prep)
        iob = sb("iob", [P, D], bf16, scope=prep)
        hot = sb("hot", [P, 2, TILES, 3, D], bf16, scope=prep)
        mh = sb("mh", [P, 2, TILES, P], bf16, scope=prep)
        oneb = sb("oneb", [P, 2], bf16, scope=prep)
        info = sb("info", [P, NBLK, 8], scope=prep)
        cnt = sb("cnt", [P, NBLK], scope=prep)
        idxf = sb("idxf", [P, NBLK], scope=prep)
        dstS = sb("dstS", [EP, EC], i32, scope=prep)
        falls = sb("falls", [EP, EC], scope=prep)
        ones = sb("ones", [P, P], scope=prep)
        unfit = sb("unfit", [P, 1], scope=prep)
        unfit_w = sb("unfit_w", [P, WJ], scope=prep)
        prep.close()

        one = ExitStack()
        xg = [sb(f"xg{u}", [P, TILES, D], scope=one) for u in range(2)]
        xb = [sb(f"xb{u}", [P, TILES, D], scope=one) for u in range(2)]
        xn = [sb(f"xn{u}", [P, TILES, D], scope=one) for u in range(2)]
        xgn = [sb(f"xgn{u}", [P, TILES, D], scope=one) for u in range(2)]
        m1 = [sb(f"m1{u}", [P, TILES, P], scope=one) for u in range(2)]
        idx1 = [sb(f"idx1{u}", [P, TILES], u32, scope=one) for u in range(2)]
        sinv1 = [sb(f"sinv1{u}", [P, TILES], scope=one) for u in range(2)]
        st1 = [sb(f"st1{u}", [P, 2 * TILES, 6], scope=one) for u in range(2)]
        mv1 = [sb(f"mv1{u}", [P, 2 * TILES, 2], scope=one) for u in range(2)]
        sd1 = [sb(f"sd1{u}", [P, 2 * TILES], scope=one) for u in range(2)]
        rs1 = [sb(f"rs1{u}", [P, 2 * TILES], scope=one) for u in range(2)]
        nm1 = [sb(f"nm1{u}", [P, 2 * TILES], scope=one) for u in range(2)]
        sx = [sb(f"sx{u}", [P, TILES, D], scope=one) for u in range(2)]
        mean = [sb(f"mean{u}", [P, TILES, D], scope=one) for u in range(2)]
        xT_hi, xT_lo, mT_hi, mT_lo = (
            [sb(f"{n}{u}", [P, 2, ROWS], fr, scope=one) for u in range(2)]
            for n in ("xT_hi", "xT_lo", "mT_hi", "mT_lo"))
        ha = sb("ha", [P, 2, ROWS], scope=one)
        hh = sb("hh", [P, 2, ROWS], fr, scope=one)
        hlo = sb("hlo", [P, 2, ROWS], fr, scope=one)
        hl = [sb(f"hl{u}", [P, TILES, D], scope=one) for u in range(2)]
        zs = [sb(f"zs{u}", [P, TILES, D], scope=one) for u in range(2)]
        one.close()

        two = ExitStack()
        gg = [sb(f"gg{u}", [P, TILES, D], scope=two) for u in range(2)]
        zb = [sb(f"zb{u}", [P, TILES, D], scope=two) for u in range(2)]
        xr = [sb(f"xr{u}", [P, TILES, D], scope=two) for u in range(2)]
        m2 = [sb(f"m2{u}", [P, TILES, P], scope=two) for u in range(2)]
        idx2 = [sb(f"idx2{u}", [P, TILES], u32, scope=two) for u in range(2)]
        x2 = [sb(f"x2{u}", [P, TILES, D], scope=two) for u in range(2)]
        x2n = [sb(f"x2n{u}", [P, TILES, D], scope=two) for u in range(2)]
        st2 = [sb(f"st2{u}", [P, TILES, 6], scope=two) for u in range(2)]
        mv2 = [sb(f"mv2{u}", [P, TILES, 2], scope=two) for u in range(2)]
        sd2 = [sb(f"sd2{u}", [P, TILES], scope=two) for u in range(2)]
        rs2 = [sb(f"rs2{u}", [P, TILES], scope=two) for u in range(2)]
        nm2 = [sb(f"nm2{u}", [P, TILES], scope=two) for u in range(2)]
        yT_hi, yT_lo = ([sb(f"{n}{u}", [P, 2, ROWS], fr, scope=two) for u in range(2)]
                        for n in ("yT_hi", "yT_lo"))
        act_a = sb("act_a", [P, 9, ROWS], scope=two)
        act_hi = sb("act_hi", [P, 9, ROWS], fr, scope=two)
        act_lo = sb("act_lo", [P, 9, ROWS], fr, scope=two)
        ob = [sb(f"ob{u}", [P, TILES, D], scope=two) for u in range(2)]
        lg = sb("lg", [P, TILES, 2 * NEXP], scope=two)
        g_t = [sb(f"g_t{k}", [P, TILES, NEXP], scope=two) for k in range(9)]
        g_s = [sb(f"g_s{k}", [P, TILES, 1], scope=two) for k in range(10)]
        sqrt_table = sb("sqrt_table", [P, 1], scope=two)
        wx = sb("wx", [P, TILES, 96], scope=two)
        wxT = sb("wxT", [96, ROWS], fr, scope=two)
        two.close()

        gp = ExitStack()
        g_dst, g_src = (sb(n, [EP, EC], i32, scope=gp) for n in ("g_dst", "g_src"))
        g_dstf = sb("g_dstf", [EP, EC], scope=gp)
        g_tile, g_row = (sb(n, [EP, EC], i32, scope=gp) for n in ("g_tile", "g_row"))
        g_tilef, g_rowf = (sb(n, [EP, EC], scope=gp) for n in ("g_tilef", "g_rowf"))
        g_zero = sb("g_zero", [P, TILES, D], scope=gp)
        g_blocks = sb("g_blocks", [EP, NBLK], scope=gp)
        g_nodes = sb("g_nodes", [P, NBLK], scope=gp)
        g_lower = sb("g_lower", [EP, EP], scope=gp)
        g_from, g_to, g_keep = (sb(n, [EP, 1], u32, scope=gp) for n in ("g_from", "g_to", "g_keep"))
        g_d = sb("g_d", [EP, 1], scope=gp)
        g_db, g_same, g_twin = (sb(n, [EP, EP], scope=gp) for n in ("g_db", "g_same", "g_twin"))
        g_later = sb("g_later", [EP, 1], scope=gp)
        g_in, g_ln, g_sum = (sb(n, [EP, D], scope=gp) for n in ("g_in", "g_ln", "g_sum"))
        g_st, g_mv = sb("g_st", [EP, 6], scope=gp), sb("g_mv", [EP, 2], scope=gp)
        g_sd, g_rs = sb("g_sd", [EP, 1], scope=gp), sb("g_rs", [EP, 1], scope=gp)
        g_hrow, g_htile = sb("g_hrow", [EP, P], scope=gp), sb("g_htile", [EP, NBLK], scope=gp)
        g_cnt = sb("g_cnt", [P, NBLK], scope=gp)
        gp.close()

        ps = [ctx.enter_context(nc.psum_tensor(f"ps{k}", [P, 512], fp32)) for k in range(8)]
        TP, AG, HB, ZB = ps[0:2], ps[2:4], ps[4:6], ps[6:8]
        WB, OBS = ps[6:8], (ps[2], ps[3], ps[7], ps[6])
        RB = (*ps[4:8], *ps[4:6], ps[4], ps[5], ps[4])

        phase_end = sem("phase_end")
        w_in, bias_in, dst_in, et_in, far_set = map(sem, ("w_in", "bias_in", "dst_in", "et_in", "far_set"))
        starts_out, starts_in, win_in = map(sem, ("starts_out", "starts_in", "win_in"))
        dstep, pstep = sem("vector_step"), sem("pool_step")
        const_set, hot_edge, hist_done, cum_ready, pre_done, sti_ready, ridx_ready = map(sem, (
            "const_set", "hot_edge", "hist_done", "cum_ready", "pre_done", "sti_ready", "ridx_ready"))
        fields_ready, ft_done, ft_taken, hot_ready, slots_done, slots_taken = map(sem, (
            "fields_ready", "ft_done", "ft_taken", "hot_ready", "slots_done", "slots_taken"))
        hist_step, mh_ready, cnt_done, cnt_taken = map(sem, ("hist_step", "mh_ready", "cnt_done", "cnt_taken"))
        x_in, xg_in, xr_in, hl_out, z_out = (sems(n) for n in ("x_in", "xg_in", "xr_in", "hl_out", "z_out"))
        stats1, ln1a, std1, rstd1, ln1b, xn_ready, xgn_ready, m1_ready = map(sem, (
            "stats1", "ln1a", "std1", "rstd1", "ln1b", "xn_ready", "xgn_ready", "m1_ready"))
        idx1_ready, sinv_ready, sx_ready, xb_ready = map(sem, ("idx1_ready", "sinv_ready", "sx_ready", "xb_ready"))
        agg_done, xT_done, mT_done, mean_ready = map(sem, ("agg_done", "xT_done", "mT_done", "mean_ready"))
        xhi, xlo, mhi, mlo = map(sem, ("xhi", "xlo", "mhi", "mlo"))
        h_done, h_relu, h_hi, h_lo, z_done, hl_ready, z1_ready, z_ready = map(sem, (
            "h_done", "h_relu", "h_hi", "h_lo", "z_done", "hl_ready", "z1_ready", "z_ready"))
        zl_in, gg_in, o_out = sems("zl_in"), sems("gg_in"), sems("o_out")
        idx2_ready, m2_ready, agg2_done, x2_ready, stats2, ln2a, std2, rstd2, ln2b, x2n_ready = map(sem, (
            "idx2_ready", "m2_ready", "agg2_done", "x2_ready", "stats2", "ln2a", "std2", "rstd2", "ln2b", "x2n_ready"))
        yT_done, yhi, ylo, lg_done, gate_step, wx_ready, wxT_done, wxT_hi, wxT_lo = map(sem, (
            "yT_done", "yhi", "ylo", "lg_done", "gate_step", "wx_ready", "wxT_done", "wxT_hi", "wxT_lo"))
        gate_exp = sem("gate_exp")
        gathers_asked = sem("gathers_asked")
        r_done, r_relu, r_hi_a, r_hi_v, r_lo, wb_done, wb_taken, o_done, o_ready = map(sem, (
            "r_done", "r_relu", "r_hi_a", "r_hi_v", "r_lo", "wb_done", "wb_taken", "o_done", "o_ready"))
        r_lo_p = sem("r_lo_p")
        g_edges_in, g_asked = sem("g_edges_in"), sem("g_asked")
        g_made, g_set = sems("g_made"), sems("g_set")
        g_zeroed, g_cols, g_turned, g_step, g_std, g_rows_in, g_sums_in, g_summed, g_counted, g_added, g_stored = (
            sems(n) for n in ("g_zeroed", "g_cols", "g_turned", "g_step", "g_std", "g_rows_in", "g_sums_in",
                              "g_summed", "g_counted", "g_added", "g_stored"))
        succ_in, unfit_ready, unfit_sum = map(sem, ("succ_in", "unfit_ready", "unfit_sum"))

        block = ctx.enter_context(nc.Block())

        def wait(eng, s, v):
            if isinstance(v, int) and v <= 0:
                return
            eng.wait_ge(s, v)

        def end_phase(eng, n):
            eng.drain().then_inc(phase_end, 1)
            eng.wait_ge(phase_end, 5 * n)

        def pipeline(eng, body):
            for u in range(2):
                body(0, u)
            with eng.Fori(1, GROUPS // 2 - 3) as j:
                for u in range(2):
                    body(j, u)
            for j in range(GROUPS // 2 - 3, GROUPS // 2):
                for u in range(2):
                    body(j, u)

        def ahead(j, u, k):
            return j + (u + k) // 2, (u + k) % 2

        def exists(j, u, k):
            return not isinstance(j, int) or 2 * j + u + k < GROUPS

        def no(j, u):
            return 2 * j + u

        def wait_low(eng, i, r):
            if r < 2:
                wait(eng, r_lo_p, 2 * i + r + 1)
            else:
                wait(eng, r_lo, 7 * i + r - 1)

        def wait_high(eng, i, r):
            if r < 4:
                eng.wait_ge(r_hi_a, 4 * i + r + 1)
            else:
                eng.wait_ge(r_hi_v, 5 * i + r - 3)

        def mm3(pe, o, l_hi, l_lo, r_hi_, r_lo_, first, last):
            pe.matmul(o, l_hi, r_hi_, start=first, stop=False)
            pe.matmul(o, l_hi, r_lo_, start=False, stop=False)
            return pe.matmul(o, l_lo, r_hi_, start=False, stop=last)

        def rows_of(t, j, u, half=None):
            first, n = no(j, u) * ROWS, ROWS
            if half is not None:
                first, n = first + half * 2 * P, 2 * P
            if isinstance(first, int):
                ap = t[first:first + n, :]
            else:
                ap = t[bass.ds(first, n), :]
            return ap.rearrange("(t p) d -> p t d", p=P)

        def first_tile(eng, j, u):
            c = no(j, u) * TILES
            return c if isinstance(c, int) else eng.snap(c)

        def cols(t, c):
            return t[:, c:c + TILES] if isinstance(c, int) else t[:, bass.ds(c, TILES)]

        def col(t, j, u, k):
            c = no(j, u) * TILES + k
            return t[:, c:c + 1] if isinstance(c, int) else t[:, bass.ds(c, 1)]

        def tail_rows(t, half):
            first = (GROUPS - 1) * ROWS
            if half == 0:
                return t[first:first + 2 * P, :].rearrange("(t p) d -> p t d", p=P), P
            n = LAST - 2 * P
            return t[first + 2 * P:N, :], n

        def is_last(j, u):
            return isinstance(j, int) and 2 * j + u == GROUPS - 1

        def edge_steps(eng, step):
            step(0)
            with eng.Fori(1, EC) as c:
                step(c)

        def edge_col(t, c):
            return t[:, c:c + 1] if isinstance(c, int) else t[:, bass.ds(c, 1)]

        G_STEPS = (11, 4)

        def general_pool(pool, q):
            pool.dma_start(g_dst[:, :], dst.rearrange("(p c) -> p c", p=EP)).then_inc(g_edges_in, 16)
            pool.dma_start(g_src[:, :], src.rearrange("(p c) -> p c", p=EP)).then_inc(g_edges_in, 16)
            pool.iota(g_blocks[:, :], [[1, NBLK]], base=0, channel_multiplier=0,
                      allow_small_or_imprecise_dtypes=True)
            pool.iota(g_nodes[:, :], [[P, NBLK]], base=0, channel_multiplier=1,
                      allow_small_or_imprecise_dtypes=True)
            pool.iota(dloc_all[:, :], [[0, NBLK]], base=0, channel_multiplier=1,
                      allow_small_or_imprecise_dtypes=True)
            pool.memset(g_zero[:, :, :], 0.0)
            pool.memset(g_lower[:, :], 1.0).then_inc(g_made[q], 1)
            pool.wait_ge(g_made[q], 1)
            pool.affine_select(out=g_lower[:, :], in_=g_lower[:, :], compare_op=ALU.is_gt, fill=0.0,
                               base=0, pattern=[[-1, EP]], channel_multiplier=1).then_inc(g_made[q], 1)
            pool.wait_ge(g_made[q], 2)
            with pool.Fori(0, GROUPS) as g:
                pool.dma_start(rows_of(sums_d, 0, g), g_zero[:, :, :]).then_inc(g_zeroed[q], 16)
            pool.wait_ge(g_zeroed[q], 16 * GROUPS)
            bound = pool.to_reg(N - 1)
            table = x if q == 0 else hl_d

            def step(c):
                pool.wait_ge(g_cols[q], 4 * (c + 1))
                pool.sem_inc(g_asked, 1)
                pool.indirect_dma_start(g_in[:, :], None, table,
                                        bass.IndirectOffsetOnAxis(g_from[:, 0:1], 0),
                                        bounds_check=bound, oob_is_err=False).then_inc(g_rows_in[q], 16)
                pool.indirect_dma_start(g_sum[:, :], None, sums_d,
                                        bass.IndirectOffsetOnAxis(g_to[:, 0:1], 0),
                                        bounds_check=bound, oob_is_err=False).then_inc(g_sums_in[q], 16)
                pool.wait_ge(g_added[q], c + 1)
                pool.sem_inc(g_asked, 1)
                pool.indirect_dma_start(sums_d, bass.IndirectOffsetOnAxis(g_keep[:, 0:1], 0),
                                        g_sum[:, :], None,
                                        bounds_check=bound, oob_is_err=False).then_inc(g_stored[q], 16)

            edge_steps(pool, step)
            pool.wait_ge(g_stored[q], 16 * EC)

        def general_vector(dve, q):
            dve.wait_ge(g_edges_in, 32 * (q + 1))
            dve.wait_ge(g_made[q], 2)
            dve.tensor_copy(g_dstf[:, :], g_dst[:, :]).then_inc(g_set[q], 1)
            dve.tensor_scalar(g_tile[:, :], g_dst[:, :], 7, None, ALU.logical_shift_right).then_inc(g_set[q], 1)
            dve.tensor_scalar(g_row[:, :], g_dst[:, :], P - 1, None, ALU.bitwise_and).then_inc(g_set[q], 1)
            dve.memset(g_cnt[:, :], 0.0).then_inc(g_set[q], 1)
            dve.wait_ge(g_set[q], 4)
            dve.tensor_copy(g_tilef[:, :], g_tile[:, :]).then_inc(g_set[q], 1)
            dve.tensor_copy(g_rowf[:, :], g_row[:, :]).then_inc(g_set[q], 1)
            dve.wait_ge(g_set[q], 6)

            def step(c):
                n = [0]

                def done(ins):
                    n[0] += 1
                    return ins.then_inc(g_step[q], 1)

                def due():
                    dve.wait_ge(g_step[q], G_STEPS[q] * c + n[0])

                wait(dve, g_stored[q], 16 * c)
                wait(dve, g_step[q], G_STEPS[q] * c)
                dve.tensor_copy(g_from[:, :], edge_col(g_src, c)).then_inc(g_cols[q], 1)
                dve.tensor_copy(g_to[:, :], edge_col(g_dst, c)).then_inc(g_cols[q], 1)
                dve.tensor_copy(g_d[:, :], edge_col(g_dstf, c)).then_inc(g_cols[q], 1)
                dve.tensor_copy(g_db[:, :], edge_col(g_dstf, c).to_broadcast([EP, EP])).then_inc(g_cols[q], 1)
                dve.wait_ge(g_turned[q], c + 1)
                done(dve.tensor_scalar(g_same[:, :], ps[0][0:EP, 0:EP], g_d[:, 0:1], None, ALU.is_equal))
                due()
                done(dve.tensor_tensor(g_twin[:, :], g_same[:, :], g_lower[:, :], ALU.mult))
                due()
                done(dve.tensor_reduce(g_later[:, :], g_twin[:, :], AX.X, ALU.max))
                due()
                done(dve.scalar_tensor_tensor(out=g_keep[:, :], in0=g_later[:, :], scalar=OOB, in1=g_d[:, :],
                                              op0=ALU.mult, op1=ALU.add))
                dve.wait_ge(g_rows_in[q], 16 * (c + 1))
                if q == 0:
                    done(dve.bn_stats(g_st[:, :], g_in[:, :]))
                    due()
                    done(dve.tensor_scalar(g_hrow[:, :], iota[0:EP, 0:P], edge_col(g_rowf, c), None, ALU.is_equal))
                    done(dve.bn_aggr(g_mv[:, :], g_st[:, :]))
                    done(dve.tensor_scalar(g_htile[:, :], g_blocks[:, :], edge_col(g_tilef, c), None, ALU.is_equal))
                    dve.wait_ge(g_std[q], c + 1)
                    done(dve.reciprocal(g_rs[:, :], g_sd[:, :]))
                    due()
                    done(dve.tensor_scalar(g_ln[:, :], g_in[:, :], g_mv[:, 0:1], g_rs[:, 0:1],
                                           ALU.subtract, ALU.mult))
                    dve.wait_ge(g_counted[q], c + 1)
                    done(dve.tensor_tensor(g_cnt[:, :], ps[2][:, 0:NBLK], g_cnt[:, :], ALU.add))
                assert n[0] == G_STEPS[q]
                due()
                dve.wait_ge(g_summed[q], c + 1)
                dve.wait_ge(g_sums_in[q], 16 * (c + 1))
                dve.tensor_tensor(g_sum[:, :], ps[1][0:EP, 0:D], g_sum[:, :], ALU.add).then_inc(g_added[q], 1)

            edge_steps(dve, step)
            if q == 0:
                dve.wait_ge(g_step[q], G_STEPS[q] * EC)
                dve.tensor_copy(idx_all[:, :], g_nodes[:, :])
                dve.memset(sinv_all[:, :], 0.0)
                dve.tensor_scalar(g_cnt[:, :], g_cnt[:, :], 1.0, None, ALU.max).then_inc(g_set[q], 1)
                dve.wait_ge(g_set[q], 7)
                dve.reciprocal(inv_all[:, :], g_cnt[:, :])

        def general_scalar(act, q):
            def step(c):
                act.wait_ge(g_step[q], G_STEPS[q] * c + 7)
                act.activation(g_sd[:, :], g_mv[:, 1:2], ACT.Sqrt, bias=eps[0:EP, 0:1]).then_inc(g_std[q], 1)

            if q == 0:
                edge_steps(act, step)

        def general_tensor(pe, q):
            def step(c):
                pe.wait_ge(g_cols[q], 4 * (c + 1))
                pe.transpose(ps[0][0:EP, 0:EP], g_db[:, :], ident[0:EP, 0:EP]).then_inc(g_turned[q], 1)
                if q == 0:
                    pe.wait_ge(g_step[q], G_STEPS[q] * c + 10)
                    pe.matmul(ps[1][0:EP, 0:D], g_same[:, :], g_ln[:, :], start=True, stop=True)\
                      .then_inc(g_summed[q], 1)
                    pe.matmul(ps[2][:, 0:NBLK], g_hrow[:, :], g_htile[:, :], start=True, stop=True)\
                      .then_inc(g_counted[q], 1)
                else:
                    pe.wait_ge(g_step[q], G_STEPS[q] * c + 1)
                    pe.wait_ge(g_rows_in[q], 16 * (c + 1))
                    pe.matmul(ps[1][0:EP, 0:D], g_same[:, :], g_in[:, :], start=True, stop=True)\
                      .then_inc(g_summed[q], 1)

            edge_steps(pe, step)

        def general(eng, q, program):
            needed = eng.value_load(gen_i[0:1, 0:1], min_val=0, max_val=1)
            if program is not None:
                with eng.If(needed > 0):
                    program(eng, q)
            end_phase(eng, 2 * q + 2)
            return needed

        @block.sync
        def _(sp):
            sp.dma_start(dstN[:, :], dst.rearrange("(p c) -> p c", p=EP)).then_inc(dst_in, 16)
            sp.dma_start(wst[:, :], wpack).then_inc(w_in, 16)
            whole = E // WROW
            rest = E - whole * WROW
            for k, t in enumerate((dst, src)):
                c = k * WROW
                sp.dma_start(edges[0:whole, c:c + WROW],
                             t[0:whole * WROW].rearrange("(r w) -> r w", w=WROW)).then_inc(et_in, 16)
                sp.dma_start(edges[whole:whole + 1, c:c + rest],
                             t[whole * WROW:E].rearrange("(r w) -> r w", r=1)).then_inc(et_in, 16)
            sp.wait_ge(far_set, 2)
            for k in range(2):
                c = k * WROW
                sp.dma_start(edges[whole:whole + 1, c + rest:c + WROW], far[0:1, 0:WROW - rest]).then_inc(et_in, 16)
            sp.dma_start(edges[whole + 1:ETROWS, :], far[0:ETROWS - whole - 1, :]).then_inc(et_in, 16)
            sp.dma_start(dstS[0:EP - 1, :], dst[1:1 + (EP - 1) * EC].rearrange("(p c) -> p c", c=EC))\
              .then_inc(succ_in, 16)
            sp.dma_start(dstS[EP - 1:EP, 0:EC - 1], dst[1 + (EP - 1) * EC:E].rearrange("(p c) -> p c", p=1))\
              .then_inc(succ_in, 16)
            sp.dma_start(bcol[:, :], bpack).then_inc(bias_in, 16)
            sp.dma_start(b2b[:, :], b2[None, :].to_broadcast([P, D])).then_inc(bias_in, 16)
            sp.dma_start(gbb[:, :], gb[None, :].to_broadcast([P, NEXP])).then_inc(bias_in, 16)
            sp.wait_ge(const_set, 1)
            for k in (0, 32, 64):
                sp.dma_start(b3f[k:k + 5, :], b3).then_inc(bias_in, 16)
            sp.wait_ge(sti_ready, 1)
            sp.dma_start(starts.rearrange("(a c) -> a c", a=HA), sti[:, :]).then_inc(starts_out, 16)
            sp.wait_ge(starts_out, 16)
            with nc.allow_non_contiguous_dma(reason="512 tile starts, one per partition"):
                sp.dma_start(s4[:, :], starts.rearrange("(j p) -> p j", p=P)).then_inc(starts_in, 16)
            sp.wait_ge(bias_in, 96)
            sp.wait_ge(starts_in, 16)
            end_phase(sp, 1)
            general(sp, 0, None)

            def load_x(j, u):
                for half in range(2):
                    if is_last(j, u):
                        rows, n = tail_rows(x, half)
                        to = xb[u][0:n, 0:2, :] if half == 0 else xb[u][0:n, 2, :]
                    else:
                        rows, to = rows_of(x, j, u, half), xb[u][:, 2 * half:2 * half + 2, :]
                    sp.dma_start(to, rows).then_inc(x_in[u], 16)

            for g in range(2):
                load_x(0, g)
            for g in range(2, 4):
                sp.wait_ge(xn_ready, TILES * (g - 1))
                load_x(1, g % 2)

            def body(j, u):
                i = no(j, u)
                if exists(j, u, 4):
                    sp.wait_ge(xn_ready, TILES * (i + 3))
                    load_x(*ahead(j, u, 4))
                sp.wait_ge(hl_ready, TILES * (i + 1))
                sp.dma_start(rows_of(hl_d, j, u), hl[u][:, :, :]).then_inc(hl_out[u], 16)
                sp.wait_ge(z_ready, TILES * (i + 1))
                sp.dma_start(rows_of(z_d, j, u), zs[u][:, :, :]).then_inc(z_out[u], 16)

            pipeline(sp, body)
            for u in range(2):
                sp.wait_ge(hl_out[u], 16 * (GROUPS // 2))
                sp.wait_ge(z_out[u], 16 * (GROUPS // 2))
            end_phase(sp, 3)
            general(sp, 1, None)

            def load_xr(j, u):
                for half in range(2):
                    if is_last(j, u):
                        rows, n = tail_rows(x, half)
                        to = xr[u][0:n, 0:2, :] if half == 0 else xr[u][0:n, 2, :]
                    else:
                        rows, to = rows_of(x, j, u, half), xr[u][:, 2 * half:2 * half + 2, :]
                    sp.dma_start(to, rows).then_inc(xr_in[u], 16)

            def load_z(j, u):
                sp.dma_start(zb[u][:, :, :], rows_of(z_d, j, u)).then_inc(zl_in[u], 16)
                load_xr(j, u)

            for g in range(2):
                load_z(0, g)
            sp.wait_ge(x2_ready, TILES)
            load_z(1, 0)

            def body2(j, u):
                i = no(j, u)
                if exists(j, u, 3):
                    sp.wait_ge(x2_ready, TILES * (i + 2))
                    load_z(*ahead(j, u, 3))
                sp.wait_ge(o_ready, TILES * (i + 1))
                for half in range(2):
                    if is_last(j, u):
                        rows, n = tail_rows(out, half)
                        of = ob[u][0:n, 0:2, :] if half == 0 else ob[u][0:n, 2, :]
                    else:
                        rows, of = rows_of(out, j, u, half), ob[u][:, 2 * half:2 * half + 2, :]
                    sp.dma_start(rows, of).then_inc(o_out[u], 16)

            pipeline(sp, body2)
            for u in range(2):
                sp.wait_ge(o_out[u], 32 * (GROUPS // 2))

        @block.gpsimd
        def _(pool):
            step = [0]

            def link(ins):
                step[0] += 1
                ins.then_inc(pstep, 1)
                pool.wait_ge(pstep, step[0])

            pool.memset(far[:, :], FAR).then_inc(far_set, 1)
            pool.memset(dstS[:, :], FAR).then_inc(far_set, 1)
            link(pool.memset(b3f[:, :], 0.0))
            pool.nop().then_inc(const_set, 1)
            pool.iota(iota[:, :], [[1, D]], base=0, channel_multiplier=0,
                      allow_small_or_imprecise_dtypes=True)
            pool.iota(iot33[:, :], [[1, HC + 1]], base=0, channel_multiplier=0,
                      allow_small_or_imprecise_dtypes=True)
            pool.iota(iob[:, :], [[1, D]], base=0, channel_multiplier=0,
                      allow_small_or_imprecise_dtypes=True)
            pool.iota(tb[:, :], [[P * P, WJ]], base=0, channel_multiplier=P,
                      allow_small_or_imprecise_dtypes=True)
            pool.iota(prio[:, :, :], [[0, TILES], [-1, NEXP]], base=NEXP, channel_multiplier=0,
                      allow_small_or_imprecise_dtypes=True)
            pool.memset(oneb[:, :], 1.0)
            pool.memset(ones[:, :], 1.0)
            pool.memset(unfit[:, :], 0.0)
            pool.memset(eps[:, :], EPS)
            link(pool.memset(ident[:, :], 0.0))
            link(pool.affine_select(out=ident[:, :], in_=ident[:, :], compare_op=ALU.not_equal, fill=1.0,
                                    base=0, pattern=[[-1, P]], channel_multiplier=1))
            link(pool.memset(tri[:, :], 1.0))
            link(pool.affine_select(out=tri[:, :], in_=tri[:, :], compare_op=ALU.is_gt, fill=0.0,
                                    base=0, pattern=[[1, HA]], channel_multiplier=-1))
            link(pool.memset(selj[:, :], 1.0))
            for first in (0, 32):
                v = selj[first:first + 32, :].rearrange("r (q m) -> r q m", q=2)
                link(pool.affine_select(out=v, in_=v, compare_op=ALU.is_ge, fill=0.0, base=0,
                                        pattern=[[P, 2], [1, P]], channel_multiplier=-64))
                link(pool.affine_select(out=v, in_=v, compare_op=ALU.is_ge, fill=0.0, base=63,
                                        pattern=[[-P, 2], [-1, P]], channel_multiplier=64))
            link(pool.memset(selj[64:96, :], 0.0))
            pool.drain().then_inc(const_set, 1)

            pool.wait_ge(et_in, 16 * 7)
            pool.wait_ge(ridx_ready, 1)
            for k in range(WJ * WK):
                pool.indirect_dma_start(win[:, k, :], None, edges[:, :],
                                        bass.IndirectOffsetOnAxis(ridx[:, k:k + 1], 0)).then_inc(win_in, 16)
            pool.wait_ge(win_in, 16 * WJ * WK)
            end_phase(pool, 1)
            needed = general(pool, 0, general_pool)

            bound = pool.to_reg(N - 1)

            def gather_rows(to, table, idx, ready):
                for cond, rows in ((needed == 0, table), (needed > 0, sums_d)):
                    with pool.If(cond):
                        for t in range(TILES):
                            pool.indirect_dma_start(to[:, t, :], None, rows,
                                                    bass.IndirectOffsetOnAxis(idx[:, t:t + 1], 0),
                                                    bounds_check=bound, oob_is_err=False).then_inc(ready, 16)

            for u in range(2):
                link(pool.memset(xg[u][:, :, :], 1.0))

            def gather(j, u, wait_for=None):
                i = no(j, u)
                c = first_tile(pool, j, u)
                if wait_for is not None:
                    pool.wait_ge(xgn_ready, wait_for)
                pool.tensor_copy(idx1[u][:, :], cols(idx_all, c)).then_inc(idx1_ready, 1)
                pool.wait_ge(idx1_ready, i + 1)
                pool.sem_inc(gathers_asked, 1)
                gather_rows(xg[u], x, idx1[u], xg_in[u])

            def scaled_own(j, u):
                i = no(j, u)
                c = first_tile(pool, j, u)
                pool.wait_ge(xn_ready, TILES * (i + 1))
                wait(pool, mean_ready, TILES * (i - 1))
                pool.tensor_copy(sinv1[u][:, :], cols(sinv_all, c)).then_inc(sinv_ready, 1)
                pool.wait_ge(sinv_ready, i + 1)
                pool.tensor_tensor(sx[u][:, :, :], xn[u][:, :, :],
                                   sinv1[u][:, :].unsqueeze(2).to_broadcast([P, TILES, D]),
                                   ALU.mult).then_inc(sx_ready, 1)

            for g in range(4):
                gather(g // 2, g % 2, TILES * (g - 1) if g >= 2 else None)
            for g in range(2):
                scaled_own(0, g)

            def body(j, u):
                if exists(j, u, 4):
                    gather(*ahead(j, u, 4), TILES * (no(j, u) + 3))
                if exists(j, u, 2):
                    scaled_own(*ahead(j, u, 2))

            pipeline(pool, body)
            end_phase(pool, 3)
            general(pool, 1, general_pool)

            for u in range(2):
                link(pool.memset(gg[u][:, :, :], 1.0))
            link(pool.memset(wx[:, :, :], 0.0))
            for c in (NEXP, 64 + NEXP):
                link(pool.memset(wx[:, :, c:c + 1], 1.0))

            def gather2(j, u, wait_for=None):
                i = no(j, u)
                c = first_tile(pool, j, u)
                if wait_for is not None:
                    pool.wait_ge(agg2_done, 2 * wait_for)
                pool.tensor_copy(idx2[u][:, :], cols(idx_all, c)).then_inc(idx2_ready, 1)
                pool.wait_ge(idx2_ready, i + 1)
                pool.sem_inc(gathers_asked, 1)
                gather_rows(gg[u], hl_d, idx2[u], gg_in[u])

            for g in range(3):
                gather2(g // 2, g % 2, 1 if g == 2 else None)

            def own_share(j, u):
                i = no(j, u)
                pool.wait_ge(zl_in[u], 16 * (j + 1))
                pool.tensor_tensor(zb[u][:, :, :], zb[u][:, :, :],
                                   b2b[:, None, :].to_broadcast([P, TILES, D]), ALU.add).then_inc(xb_ready, 1)
                pool.wait_ge(xr_in[u], 32 * (j + 1))
                pool.wait_ge(xb_ready, 2 * i + 1)
                pool.tensor_tensor(zb[u][:, :, :], zb[u][:, :, :], xr[u][:, :, :], ALU.add).then_inc(xb_ready, 1)

            def rest_low(j, u, r):
                i = no(j, u)
                pool.wait_ge(r_hi_a, 4 * i + r + 1)
                pool.tensor_tensor(act_lo[:, r, :], act_a[:, r, :], act_hi[:, r, :].bitcast(fp32),
                                   ALU.subtract).then_inc(r_lo_p, 1)

            for g in range(2):
                own_share(0, g)
            rest_low(0, 0, 0)
            rest_low(0, 0, 1)

            def body2(j, u):
                if exists(j, u, 3):
                    gather2(*ahead(j, u, 3), no(j, u) + 2)
                if exists(j, u, 2):
                    own_share(*ahead(j, u, 2))
                if exists(j, u, 1):
                    rest_low(*ahead(j, u, 1), 0)
                    rest_low(*ahead(j, u, 1), 1)

            pipeline(pool, body2)

        @block.scalar
        def _(act):
            for f in range(4):
                for q, (_, n) in enumerate(CHUNKS):
                    k = 3 * f + q
                    act.wait_ge(ft_done, k + 1)
                    to = keyT[0:n, q, :] if f == 0 else vT[0:n, q, :, f - 1]
                    act.activation(to, ps[k % 4][0:n, :], ACT.Copy).then_inc(ft_taken, 1)
            with act.Fori(0, GROUPS // 2) as j:
                for u in range(2):
                    act.wait_ge(slots_done, 2 * j + u + 1)
                    act.activation(info[:, bass.ds((2 * j + u) * TILES, TILES), :],
                                   ps[u][:, 0:8 * TILES].rearrange("p (t k) -> p t k", k=8),
                                   ACT.Copy).then_inc(slots_taken, 1)
            with act.Fori(0, GROUPS // 2) as j:
                for u in range(2):
                    act.wait_ge(cnt_done, 2 * j + u + 1)
                    act.activation(cnt[:, bass.ds((2 * j + u) * TILES, TILES)], ps[u][:, 0:TILES],
                                   ACT.Copy).then_inc(cnt_taken, 1)
            end_phase(act, 1)
            general(act, 0, general_scalar)

            def deviations(j, u):
                i = no(j, u)
                act.wait_ge(ln1a, i + 1)
                act.activation(sd1[u][:, :], mv1[u][:, :, 1], ACT.Sqrt, bias=eps[:, 0:1]).then_inc(std1, 1)

            def normalise(j, u, tiles):
                i = no(j, u)
                for t in tiles:
                    if t == 0:
                        act.wait_ge(ln1b, i + 1)
                        wait(act, agg_done, i - 1)
                    if t == TILES:
                        wait(act, xT_done, i - 1)
                        wait(act, sx_ready, i - 1)
                    k = (t + TILES) % (2 * TILES)
                    to, of, ready = (xgn, xg, xgn_ready) if t < TILES else (xn, xb, xn_ready)
                    act.activation(to[u][:, t % TILES, :], of[u][:, t % TILES, :], ACT.Identity,
                                   bias=nm1[u][:, k:k + 1], scale=rs1[u][:, k:k + 1]).then_inc(ready, 1)

            def part(to, done, free, taken, j, u):
                i = no(j, u)
                act.wait_ge(done, i + 1)
                wait(act, h_done, 2 * (i - 1))
                for k in range(2):
                    act.activation(to[u][:, k, :], TP[k][:, :], ACT.Copy).then_inc(taken, 1)

            def x_part(j, u):
                part(xT_hi, xT_done, None, xhi, j, u)

            def m_part(j, u):
                part(mT_hi, mT_done, None, mhi, j, u)

            def both(j, u):
                deviations(j, u)
                normalise(j, u, range(2 * TILES))

            both(0, 0)
            both(0, 1)
            x_part(0, 0)
            m_part(0, 0)
            x_part(0, 1)
            both(1, 0)

            def body(j, u):
                i = no(j, u)
                for k in range(2):
                    act.wait_ge(h_done, 2 * i + k + 1)
                    wait(act, h_lo, 2 * (i - 1) + k + 1)
                    act.activation(ha[:, k, :], HB[k][:, :], ACT.Relu,
                                   bias=bcol[:, BCOLS["b1"] + k:BCOLS["b1"] + k + 1]).then_inc(h_relu, 1)
                    act.wait_ge(h_relu, 2 * i + k + 1)
                    wait(act, z_done, TILES * i)
                    act.activation(hh[:, k, :], ha[:, k, :], ACT.Copy).then_inc(h_hi, 1)
                    if k == 0 and exists(j, u, 3):
                        deviations(*ahead(j, u, 3))
                if exists(j, u, 1):
                    m_part(*ahead(j, u, 1))
                for t in range(TILES):
                    act.wait_ge(z_done, TILES * i + t + 1)
                    if t == 0:
                        wait(act, hl_out[u], 16 * j)
                        wait(act, z_ready, TILES * (i - 1))
                    act.activation(hl[u][:, t, :], ZB[t % 2][:, 0:D], ACT.Copy).then_inc(hl_ready, 1)
                    if t == 0 and exists(j, u, 2):
                        x_part(*ahead(j, u, 2))
                    if exists(j, u, 3):
                        normalise(*ahead(j, u, 3), ((), (0, 1), (2, 3), (4, 5, 6, 7))[t])

            pipeline(act, body)
            end_phase(act, 3)
            general(act, 1, general_scalar)

            def deviations2(j, u):
                act.wait_ge(ln2a, no(j, u) + 1)
                act.activation(sd2[u][:, :], mv2[u][:, :, 1], ACT.Sqrt, bias=eps[:, 0:1]).then_inc(std2, 1)

            def normalise2(j, u, tiles):
                i = no(j, u)
                if 0 in tiles:
                    act.wait_ge(ln2b, i + 1)
                    wait(act, yT_done, i - 1)
                for t in tiles:
                    act.activation(x2n[u][:, t, :], x2[u][:, t, :], ACT.Identity, bias=nm2[u][:, t:t + 1],
                                   scale=rs2[u][:, t:t + 1]).then_inc(x2n_ready, 1)

            def y_part(j, u):
                i = no(j, u)
                act.wait_ge(yT_done, i + 1)
                for k in range(2):
                    act.activation(yT_hi[u][:, k, :], TP[k][:, :], ACT.Copy).then_inc(yhi, 1)

            def relu(j, u, r):
                i = no(j, u)
                act.wait_ge(r_done, 9 * i + r + 1)
                wait_low(act, i - 1, r)
                c = BCOLS["sb1"] + r if r < 2 else BCOLS["eb1"] + r - 2 if r < 6 else \
                    {6: BCOLS["eb2"], 7: BCOLS["sb2"], 8: BCOLS["eb2"] + 1}[r]
                act.activation(act_a[:, r, :], RB[r][:, :], ACT.Relu, bias=bcol[:, c:c + 1])\
                   .then_inc(r_relu, 1)
                if r < 4:
                    act.wait_ge(r_relu, 9 * i + r + 1)
                    act.activation(act_hi[:, r, :], act_a[:, r, :], ACT.Copy).then_inc(r_hi_a, 1)

            def gate_exp1(j, u):
                act.wait_ge(gate_step, GATE_STEPS * no(j, u) + GATE_EXP1)
                act.activation(g_t[1][:, :, :], g_t[1][:, :, :], ACT.Exp).then_inc(gate_exp, 1)

            def gate_exp2(j, u):
                act.wait_ge(gate_step, GATE_STEPS * no(j, u) + GATE_EXP2)
                act.activation(g_s[6][:, :, :], g_s[6][:, :, :], ACT.Exp).then_inc(gate_exp, 1)

            def shared_and_gates(j, u):
                gate_exp1(j, u)
                relu(j, u, 0)
                gate_exp2(j, u)
                act.activation(sqrt_table[:, :], eps[:, 0:1], ACT.Sqrt)
                relu(j, u, 1)

            deviations2(0, 0)
            normalise2(0, 0, range(TILES))
            y_part(0, 0)
            shared_and_gates(0, 0)

            def body2(j, u):
                i = no(j, u)
                more, nxt = exists(j, u, 1), ahead(j, u, 1)
                relu(j, u, 2)
                act.wait_ge(wxT_done, i + 1)
                wait(act, o_done, TILES * i)
                act.activation(wxT[:, :], TP[1][0:96, :], ACT.Copy).then_inc(wxT_hi, 1)
                relu(j, u, 3)
                if more:
                    deviations2(*nxt)
                relu(j, u, 4)
                relu(j, u, 5)
                if more:
                    normalise2(*nxt, range(TILES))
                relu(j, u, 6)
                relu(j, u, 7)
                if more:
                    y_part(*nxt)
                relu(j, u, 8)
                if more:
                    shared_and_gates(*nxt)

            pipeline(act, body2)

        @block.vector
        def _(dve):
            step = [0]

            def link(ins):
                step[0] += 1
                ins.then_inc(dstep, 1)
                dve.wait_ge(dstep, step[0])

            dve.wait_ge(dst_in, 16)
            dve.tensor_scalar(ea[:, :], dstN[:, :], 12, None, ALU.logical_shift_right)
            link(dve.tensor_scalar(ec[:, :], dstN[:, :], 7, HC - 1, ALU.logical_shift_right, ALU.bitwise_and))
            dve.wait_ge(const_set, 2)

            def edge_hots(c, b, n):
                wait(dve, hist_step, n - 1)
                at = bass.ds(25 * c, 25) if not isinstance(c, int) else slice(25 * c, 25 * c + 25)
                dve.tensor_tensor(oa[:, b, :, :], ea[:, at].unsqueeze(2).to_broadcast([EP, 25, HA]),
                                  iot33[:, None, 0:HA].to_broadcast([EP, 25, HA]), ALU.is_equal)\
                   .then_inc(hot_edge, 1)
                dve.tensor_tensor(oc[:, b, :, :], ec[:, at].unsqueeze(2).to_broadcast([EP, 25, HC + 1]),
                                  iot33[:, None, :].to_broadcast([EP, 25, HC + 1]), ALU.is_lt)\
                   .then_inc(hot_edge, 1)

            edge_hots(0, 0, 0)
            edge_hots(1, 1, 1)
            with dve.Fori(1, 12) as j:
                edge_hots(2 * j, 0, 2 * j)
                edge_hots(2 * j + 1, 1, 2 * j + 1)
            edge_hots(24, 0, 24)

            dve.wait_ge(hist_done, 1)
            dve.tensor_copy(cum[:, :], ps[4][0:HA, 0:HC + 1]).then_inc(cum_ready, 1)
            dve.wait_ge(pre_done, 1)
            link(dve.tensor_copy(pre[:, :], ps[5][0:HA, 0:1]))
            dve.tensor_scalar(sti[:, :], cum[:, 0:HC], pre[:, 0:1], None, ALU.add).then_inc(sti_ready, 1)

            dve.wait_ge(succ_in, 32)
            link(dve.tensor_tensor(falls[:, :], dstN[:, :], dstS[:, :], ALU.is_gt))
            link(dve.tensor_reduce(unfit[0:EP, :], falls[:, :], AX.X, ALU.max))

            dve.wait_ge(w_in, 16)

            def packed(name):
                a, n = WCOLS[name]
                return wst[:, a:a + n]

            def halves(name):
                return packed(name).rearrange("p (k n) -> p k n", k=2)

            link(dve.memset(ew2_hi[:, :, :].bitcast(fp32), 0.0))
            link(dve.memset(ew2_lo[:, :, :].bitcast(fp32), 0.0))
            splits = [
                (w1_hi[:, 0], w1_lo[:, 0], halves("w1l")),
                (w1_hi[:, 1], w1_lo[:, 1], halves("w1r")),
                (w2_hi[:, :], w2_lo[:, :], halves("w2")),
                (sw1_hi[:, :], sw1_lo[:, :], halves("sw1")),
                (sw2_hi[:, :], sw2_lo[:, :], halves("sw2")),
                (sw3_hi[:, :], sw3_lo[:, :], packed("sw3")),
                (ew1_hi[:, :, :, :].rearrange("p k e n -> p k (e n)"), ew1_lo[:, :, :, :].rearrange("p k e n -> p k (e n)"),
                 halves("ew1")),
                (ew3_hi[:, :], ew3_lo[:, :], halves("ew3")),
                (gw_hl[:, :, 0:NEXP], gw_hl[:, :, NEXP:2 * NEXP], halves("gw")),
            ]
            for e in range(NEXP):
                c = 64 * (e % 2)
                a = WCOLS["ew2"][0] + 64 * e
                splits.append((ew2_hi[:, e, c:c + 64], ew2_lo[:, e, c:c + 64], wst[:, a:a + 64]))
            for hi_, _, of in splits:
                dve.tensor_copy(hi_, of).then_inc(dstep, 1)
                step[0] += 1
            dve.wait_ge(dstep, step[0])
            for hi_, lo_, of in splits:
                dve.tensor_tensor(lo_, of, hi_.bitcast(fp32), ALU.subtract)
            dve.tensor_copy(sel[:, :, :], selj[:, :].rearrange("r (q m) -> r q m", q=2))
            dve.wait_ge(bias_in, 96)
            link(dve.tensor_copy(b3s[:, :], b3f[:, :]))
            link(dve.tensor_tensor(b3s[64:96, :], b3f[64:96, :], b3s[64:96, :].bitcast(fp32), ALU.subtract))

            dve.wait_ge(starts_in, 16)
            link(dve.tensor_scalar(r0[:, :], s4[:, :], 6, None, ALU.logical_shift_right))
            link(dve.tensor_copy(r0f[:, :], r0[:, :]))
            for k in range(WK):
                ins = dve.tensor_scalar(ridx[:, :].rearrange("p (j k) -> p j k", k=WK)[:, :, k], r0f[:, :],
                                        float(k), None, ALU.add)
            ins.then_inc(ridx_ready, 1)
            link(dve.memset(vT[:, :, :, :], 1.0))

            dve.wait_ge(win_in, 16 * WJ * WK)

            def jk(t):
                return t[:, :, :].rearrange("p j (k w) -> p (j k) w", w=WROW)

            link(dve.tensor_copy(jk(wd), win[:, :, 0:WROW]))
            link(dve.tensor_copy(jk(ws), win[:, :, WROW:2 * WROW]))
            link(dve.tensor_scalar(jk(shi), win[:, :, WROW:2 * WROW], 8, None, ALU.logical_shift_right))
            link(dve.tensor_scalar(jk(slo), win[:, :, WROW:2 * WROW], 255, None, ALU.bitwise_and))
            for j in range(WJ):
                link(dve.tensor_scalar(wd[:, j, :], wd[:, j, :], tb[:, j:j + 1], None, ALU.subtract))
                link(dve.tensor_scalar(ws[:, j, :], ws[:, j, :], tb[:, j:j + 1], None, ALU.subtract))
            link(dve.tensor_scalar(wv[:, :, :], wd[:, :, :], 0.0, None, ALU.is_ge))
            link(dve.scalar_tensor_tensor(out=wv[:, :, :], in0=wd[:, :, :], scalar=float(P), in1=wv[:, :, :],
                                          op0=ALU.is_lt, op1=ALU.mult))
            link(dve.tensor_tensor(wn[:, :, :], ws[:, :, :], wd[:, :, :], ALU.not_equal))
            link(dve.tensor_tensor(wn[:, :, :], wn[:, :, :], wv[:, :, :], ALU.mult))
            for j in range(WJ):
                link(dve.tensor_tensor_scan(wc[:, j, :], wn[:, j, :], wn[:, j, :], 0.0, ALU.add, ALU.max))
            link(dve.tensor_scalar(unfit_w[:, :], wc[:, :, WIN - 1], float(P), None, ALU.is_gt))
            link(dve.tensor_tensor(unfit_w[:, :], unfit_w[:, :], wv[:, :, WIN - 1], ALU.max))
            link(dve.tensor_tensor(unfit_w[:, 0:2], unfit_w[:, 0:2], unfit_w[:, 2:4], ALU.max))
            link(dve.tensor_tensor(unfit_w[:, 0:1], unfit_w[:, 0:1], unfit_w[:, 1:2], ALU.max))
            dve.tensor_tensor(unfit[:, :], unfit[:, :], unfit_w[:, 0:1], ALU.max).then_inc(unfit_ready, 1)
            link(dve.tensor_tensor(wc[:, :, :], wc[:, :, :], wn[:, :, :], ALU.mult))
            link(dve.tensor_tensor(ws[:, :, :], wv[:, :, :], wn[:, :, :], ALU.subtract))
            link(dve.scalar_tensor_tensor(out=ws[:, :, :], in0=wd[:, :, :], scalar=float(P + 1), in1=ws[:, :, :],
                                          op0=ALU.add, op1=ALU.mult))
            link(dve.scalar_tensor_tensor(out=wk_[:, :, :], in0=wc[:, :, :], scalar=-1.0, in1=ws[:, :, :],
                                          op0=ALU.add, op1=ALU.add))
            link(dve.tensor_copy(ws[:, :, :], shi[:, :, :]))
            link(dve.tensor_copy(wn[:, :, :], slo[:, :, :]))
            dve.sem_inc(fields_ready, 1)

            dve.wait_ge(ft_taken, 12)

            def key_hots(j, u):
                i = no(j, u)
                wait(dve, slots_done, i - 1)
                for t in range(TILES):
                    for q, (_, n) in enumerate(CHUNKS):
                        c = i * TILES + t
                        c = slice(c, c + 1) if isinstance(c, int) else bass.ds(c, 1)
                        ins = dve.tensor_scalar(hot[0:n, u, t, q, :], iob[0:n, :], keyT[0:n, q, c], None,
                                                ALU.is_equal)
                ins.then_inc(hot_ready, 1)

            for u in range(2):
                key_hots(0, u)
            with dve.Fori(1, GROUPS // 2) as j:
                for u in range(2):
                    key_hots(j, u)
            dve.wait_ge(unfit_sum, 1)
            link(dve.tensor_scalar(gen[:, :], ps[6][:, 0:1], 0.0, None, ALU.is_gt))
            dve.tensor_copy(gen_i[:, :], gen[0:1, :])
            dve.tensor_scalar(own[:, :], gen[:, :], -1.0, 1.0, ALU.mult, ALU.add)
            dve.tensor_scalar(neg_own[:, :], gen[:, :], 1.0, -1.0, ALU.mult, ALU.add)
            dve.wait_ge(slots_taken, GROUPS)
            link(dve.scalar_tensor_tensor(out=idxf[:, :], in0=info[:, :, 0], scalar=256.0, in1=info[:, :, 1],
                                          op0=ALU.mult, op1=ALU.add))
            link(dve.scalar_tensor_tensor(out=idxf[:, :], in0=info[:, :, 3], scalar=-OOB, in1=idxf[:, :],
                                          op0=ALU.mult, op1=ALU.add))
            link(dve.tensor_scalar(idx_all[:, :], idxf[:, :], OOB, None, ALU.add))
            link(dve.scalar_tensor_tensor(out=dloc_all[:, :], in0=info[:, :, 3], scalar=-1000.0, in1=info[:, :, 2],
                                          op0=ALU.mult, op1=ALU.add))
            link(dve.tensor_scalar(dloc_all[:, :], dloc_all[:, :], 1000.0, None, ALU.add))

            def slot_hots(j, u):
                i = no(j, u)
                wait(dve, cnt_done, i - 1)
                for t in range(TILES):
                    ins = dve.tensor_scalar(mh[:, u, t, :], iob[:, 0:P], col(dloc_all, j, u, t), None, ALU.is_equal)
                ins.then_inc(mh_ready, 1)

            for u in range(2):
                slot_hots(0, u)
            with dve.Fori(1, GROUPS // 2) as j:
                for u in range(2):
                    slot_hots(j, u)
            dve.wait_ge(cnt_taken, GROUPS)
            link(dve.tensor_tensor(cnt[:, :], cnt[:, :], info[:, :, 7], ALU.add))
            link(dve.tensor_scalar(cnt[:, :], cnt[:, :], 1.0, None, ALU.max))
            link(dve.reciprocal(inv_all[:, :], cnt[:, :]))
            link(dve.tensor_tensor(sinv_all[:, :], inv_all[:, :], info[:, :, 7], ALU.mult))
            end_phase(dve, 1)
            general(dve, 0, general_vector)

            def statistics(j, u):
                i = no(j, u)
                dve.wait_ge(x_in[u], 32 * (j + 1))
                wait(dve, xgn_ready, TILES * (i - 1))
                wait(dve, xn_ready, TILES * (i - 1))
                for t in range(TILES):
                    dve.bn_stats(st1[u][:, t, :], xb[u][:, t, :]).then_inc(stats1, 1)
                dve.wait_ge(xg_in[u], 64 * (j + 1))
                for t in range(TILES):
                    dve.bn_stats(st1[u][:, TILES + t, :], xg[u][:, t, :]).then_inc(stats1, 1)
                dve.wait_ge(stats1, 2 * TILES * (i + 1))
                wait(dve, agg_done, i - 1)
                for t in range(TILES):
                    dve.tensor_scalar(m1[u][:, t, :], iota[:, 0:P], col(dloc_all, j, u, t), None,
                                      ALU.is_equal).then_inc(m1_ready, 1)
                for t in range(2 * TILES):
                    ins = dve.bn_aggr(mv1[u][:, t, :], st1[u][:, t, :])
                ins.then_inc(ln1a, 1)

            def scales(j, u):
                i = no(j, u)
                dve.wait_ge(std1, i + 1)
                dve.reciprocal(rs1[u][:, :], sd1[u][:, :]).then_inc(rstd1, 1)
                dve.wait_ge(rstd1, 2 * i + 1)
                dve.scalar_tensor_tensor(out=nm1[u][:, 0:TILES], in0=mv1[u][:, 0:TILES, 0], scalar=-1.0,
                                         in1=rs1[u][:, 0:TILES], op0=ALU.mult, op1=ALU.mult)
                dve.scalar_tensor_tensor(out=nm1[u][:, TILES:], in0=mv1[u][:, TILES:, 0], scalar=neg_own[:, 0:1],
                                         in1=rs1[u][:, TILES:], op0=ALU.mult, op1=ALU.mult).then_inc(rstd1, 1)
                dve.wait_ge(rstd1, 2 * i + 2)
                dve.tensor_scalar(rs1[u][:, TILES:], rs1[u][:, TILES:], own[:, 0:1], gen[:, 0:1],
                                  ALU.mult, ALU.max).then_inc(ln1b, 1)

            def remainder(to, hi_, done, taken, taken_hi, j, u):
                i = no(j, u)
                for k in range(2):
                    dve.wait_ge(taken_hi, 2 * i + k + 1)
                    dve.tensor_tensor(to[u][:, k, :], TP[k][:, :], hi_[u][:, k, :].bitcast(fp32),
                                      ALU.subtract).then_inc(taken, 1)

            def means(j, u):
                i = no(j, u)
                dve.wait_ge(agg_done, i + 1)
                dve.wait_ge(sx_ready, i + 1)
                wait(dve, mT_done, i - 1)
                for t in range(TILES):
                    c = (t % 2) * D
                    dve.scalar_tensor_tensor(out=mean[u][:, t, :], in0=AG[t // 2][:, c:c + D],
                                             scalar=col(inv_all, j, u, t), in1=sx[u][:, t, :],
                                             op0=ALU.mult, op1=ALU.add).then_inc(mean_ready, 1)

            def x_rest(j, u):
                remainder(xT_lo, xT_hi, xT_done, xlo, xhi, j, u)

            def m_rest(j, u):
                remainder(mT_lo, mT_hi, mT_done, mlo, mhi, j, u)

            for g in range(2):
                statistics(0, g)
                scales(0, g)
            means(0, 0)
            x_rest(0, 0)
            m_rest(0, 0)
            x_rest(0, 1)
            means(0, 1)
            statistics(1, 0)
            scales(1, 0)

            def body(j, u):
                i = no(j, u)
                if exists(j, u, 3):
                    statistics(*ahead(j, u, 3))
                for k in range(2):
                    dve.wait_ge(h_hi, 2 * i + k + 1)
                    wait(dve, z_done, TILES * i)
                    dve.tensor_tensor(hlo[:, k, :], ha[:, k, :], hh[:, k, :].bitcast(fp32),
                                      ALU.subtract).then_inc(h_lo, 1)
                    if k == 0 and exists(j, u, 3):
                        scales(*ahead(j, u, 3))
                if exists(j, u, 1):
                    m_rest(*ahead(j, u, 1))
                if exists(j, u, 2):
                    means(*ahead(j, u, 2))
                wait(dve, z_out[u], 16 * j)
                for t in range(TILES):
                    dve.wait_ge(hl_ready, TILES * i + t + 1)
                    dve.scalar_tensor_tensor(out=zs[u][:, t, :], in0=hl[u][:, t, :],
                                             scalar=col(sinv_all, j, u, t), in1=ZB[t % 2][:, D:2 * D],
                                             op0=ALU.mult, op1=ALU.add).then_inc(z_ready, 1)
                    if t == 0 and exists(j, u, 2):
                        x_rest(*ahead(j, u, 2))

            pipeline(dve, body)
            end_phase(dve, 3)
            general(dve, 1, general_vector)

            def slots2(j, u):
                wait(dve, agg2_done, 2 * (no(j, u) - 1))
                for t in range(TILES):
                    dve.tensor_scalar(m2[u][:, t, :], iota[:, 0:P], col(dloc_all, j, u, t), None,
                                      ALU.is_equal).then_inc(m2_ready, 1)

            def second(j, u):
                i = no(j, u)
                dve.wait_ge(xb_ready, 2 * (i + 1))
                for t in range(TILES):
                    dve.wait_ge(agg2_done, 2 * i + t // 2 + 1)
                    c = (t % 2) * D
                    dve.scalar_tensor_tensor(out=x2[u][:, t, :], in0=AG[t // 2][:, c:c + D],
                                             scalar=col(inv_all, j, u, t), in1=zb[u][:, t, :],
                                             op0=ALU.mult, op1=ALU.add).then_inc(x2_ready, 1)

            def statistics2(j, u, between=None):
                i = no(j, u)
                for t in range(TILES):
                    dve.wait_ge(x2_ready, TILES * i + t + 1)
                    dve.bn_stats(st2[u][:, t, :], x2[u][:, t, :]).then_inc(stats2, 1)
                dve.wait_ge(stats2, TILES * (i + 1))
                if between is not None:
                    between()
                for t in range(TILES):
                    ins = dve.bn_aggr(mv2[u][:, t, :], st2[u][:, t, :])
                ins.then_inc(ln2a, 1)

            def scales2(j, u):
                i = no(j, u)
                dve.wait_ge(std2, i + 1)
                dve.reciprocal(rs2[u][:, :], sd2[u][:, :]).then_inc(rstd2, 1)
                dve.wait_ge(rstd2, i + 1)
                dve.scalar_tensor_tensor(out=nm2[u][:, :], in0=mv2[u][:, :, 0], scalar=-1.0, in1=rs2[u][:, :],
                                         op0=ALU.mult, op1=ALU.mult).then_inc(ln2b, 1)

            def y_rest(j, u):
                i = no(j, u)
                for k in range(2):
                    dve.wait_ge(yhi, 2 * i + k + 1)
                    dve.tensor_tensor(yT_lo[u][:, k, :], TP[k][:, :], yT_hi[u][:, k, :].bitcast(fp32),
                                      ALU.subtract).then_inc(ylo, 1)

            def rest(j, u, r):
                i = no(j, u)
                dve.wait_ge(r_relu, 9 * i + r + 1)
                if r in (6, 8):
                    q = (r - 6) // 2
                    dve.wait_ge(wb_done, 2 * i + q + 1)
                    dve.tensor_tensor(act_a[:, r, :], act_a[:, r, :], WB[q][:, :], ALU.mult).then_inc(wb_taken, 1)
                    dve.wait_ge(wb_taken, 2 * i + q + 1)
                if r >= 4:
                    if r >= 6:
                        wait(dve, o_done, TILES * i)
                    dve.tensor_copy(act_hi[:, r, :], act_a[:, r, :]).then_inc(r_hi_v, 1)
                wait_high(dve, i, r)
                dve.tensor_tensor(act_lo[:, r, :], act_a[:, r, :], act_hi[:, r, :].bitcast(fp32),
                                  ALU.subtract).then_inc(r_lo, 1)

            def gates(j, u):
                i = no(j, u)
                n = [0]
                B = [P, TILES, NEXP]
                S = [P, TILES, 1]
                lgt, d, c1, oh1, e2, q2, oh2, w1, w2 = (t[:, :, :] for t in g_t)
                mx, sm, ri, m1_, v2, m2_, d2, den, a1, a2 = (t[:, :, :] for t in g_s)
                lgs = TP[0][:, 0:8 * TILES].rearrange("p (t k) -> p t k", k=8)

                def done(ins):
                    n[0] += 1
                    ins.then_inc(gate_step, 1)

                def due():
                    dve.wait_ge(gate_step, GATE_STEPS * i + n[0])

                dve.wait_ge(lg_done, i + 1)
                done(dve.tensor_tensor(lgt, lgs[:, :, 0:NEXP], gbb[:, None, :].to_broadcast(B), ALU.add))
                yield
                due()
                done(dve.tensor_tensor(lgt, lgt, lgs[:, :, NEXP:2 * NEXP], ALU.add))
                yield
                due()
                done(dve.tensor_reduce(mx, lgt, AX.X, ALU.max))
                yield
                due()
                done(dve.tensor_tensor(d, lgt, mx.to_broadcast(B), ALU.subtract))
                done(dve.scalar_tensor_tensor(out=c1, in0=lgt, scalar=1.0, in1=mx.to_broadcast(B),
                                              op0=ALU.mult, op1=ALU.is_equal))
                assert n[0] == GATE_EXP1 + 1
                yield
                due()
                done(dve.tensor_tensor(c1, c1, prio[:, :, :], ALU.mult))
                yield
                due()
                done(dve.tensor_reduce(m1_, c1, AX.X, ALU.max))
                yield
                due()
                done(dve.tensor_tensor(oh1, c1, m1_.to_broadcast(B), ALU.is_equal))
                yield
                due()
                dve.wait_ge(gate_exp, 2 * i + 1)
                done(dve.tensor_reduce(sm, d, AX.X, ALU.add))
                done(dve.scalar_tensor_tensor(out=e2, in0=oh1, scalar=-4.0, in1=d, op0=ALU.mult, op1=ALU.add))
                yield
                due()
                done(dve.reciprocal(ri, sm))
                done(dve.tensor_reduce(v2, e2, AX.X, ALU.max))
                yield
                due()
                done(dve.scalar_tensor_tensor(out=d2, in0=v2, scalar=-1.0, in1=ri, op0=ALU.add, op1=ALU.mult))
                assert n[0] == GATE_EXP2
                done(dve.tensor_tensor(q2, e2, v2.to_broadcast(B), ALU.is_equal))
                yield
                due()
                done(dve.tensor_tensor(q2, q2, prio[:, :, :], ALU.mult))
                yield
                due()
                done(dve.tensor_reduce(m2_, q2, AX.X, ALU.max))
                yield
                due()
                done(dve.tensor_tensor(oh2, q2, m2_.to_broadcast(B), ALU.is_equal))
                yield
                due()
                dve.wait_ge(gate_exp, 2 * i + 2)
                done(dve.tensor_scalar(den, d2, 1.0, None, ALU.add))
                yield
                due()
                done(dve.reciprocal(a1, den))
                yield
                due()
                done(dve.tensor_tensor(a2, d2, a1, ALU.mult))
                done(dve.tensor_tensor(w1, oh1, a1.to_broadcast(B), ALU.mult))
                yield
                due()
                done(dve.tensor_tensor(w2, oh2, a2.to_broadcast(B), ALU.mult))
                yield
                due()
                wait(dve, wxT_done, i)
                for c in (0, 32, 64):
                    ins = dve.tensor_tensor(wx[:, :, c:c + NEXP], w1, w2, ALU.add)
                ins.then_inc(wx_ready, 1)
                assert n[0] == GATE_STEPS, n[0]

            slots2(0, 0)
            slots2(0, 1)
            second(0, 0)
            statistics2(0, 0)
            scales2(0, 0)
            y_rest(0, 0)
            for _ in gates(0, 0):
                pass

            def body2(j, u):
                i = no(j, u)
                more, nxt = exists(j, u, 1), ahead(j, u, 1)

                def weights_low():
                    dve.wait_ge(wxT_hi, i + 1)
                    dve.tensor_tensor(wxT[32:64, :], TP[1][32:64, :], wxT[32:64, :].bitcast(fp32),
                                      ALU.subtract).then_inc(wxT_lo, 1)

                if more:
                    second(*nxt)
                    statistics2(*nxt, weights_low)
                else:
                    weights_low()
                rest(j, u, 2)
                rest(j, u, 3)
                if more:
                    scales2(*nxt)
                for r in (4, 5, 6, 7):
                    rest(j, u, r)
                if more:
                    y_rest(*nxt)
                rest(j, u, 8)
                gate = gates(*nxt) if more else iter(())
                wait(dve, o_out[u], 32 * j)
                for t in range(TILES):
                    for _ in range(GATE_AHEAD[t]):
                        next(gate, None)
                    if t == 1 and exists(j, u, 2):
                        slots2(*ahead(j, u, 2))
                    dve.wait_ge(o_done, TILES * i + t + 1)
                    dve.tensor_tensor(ob[u][:, t, :], OBS[t][:, 0:D], x2[u][:, t, :],
                                      ALU.add).then_inc(o_ready, 1)
                for _ in gate:
                    pass

            pipeline(dve, body2)

        @block.tensor
        def _(pe):
            hist = ps[4][0:HA, 0:HC + 1]

            def histogram(b, n, first=False, last=False):
                pe.wait_ge(hot_edge, 2 * n + 2)
                for k in range(25):
                    ins = pe.matmul(hist, oa[:, b, k, :], oc[:, b, k, :], start=first and k == 0,
                                    stop=last and k == 24)
                ins.then_inc(hist_step, 1)
                return ins

            histogram(0, 0, first=True)
            histogram(1, 1)
            with pe.Fori(1, 12) as j:
                histogram(0, 2 * j)
                histogram(1, 2 * j + 1)
            histogram(0, 24, last=True)
            pe.wait_ge(hist_step, 25)
            pe.nop().then_inc(hist_done, 1)
            pe.wait_ge(cum_ready, 1)
            pe.wait_ge(const_set, 2)
            pe.matmul(ps[5][0:HA, 0:1], tri[:, :], cum[:, HC:HC + 1], start=True, stop=True).then_inc(pre_done, 1)
            pe.wait_ge(unfit_ready, 1)
            pe.matmul(ps[6][:, 0:1], ones[:, :], unfit[:, :], start=True, stop=True).then_inc(unfit_sum, 1)
            pe.wait_ge(fields_ready, 1)
            for f, t in enumerate((wk_, ws, wn, wd)):
                for q, (c, n) in enumerate(CHUNKS):
                    k = 3 * f + q
                    wait(pe, ft_taken, k - 3)
                    for j in range(WJ):
                        ins = pe.transpose(ps[k % 4][0:n, P * j:P * j + P], t[:, j, c:c + n], ident[:, :])
                    ins.then_inc(ft_done, 1)
            pe.wait_ge(ft_taken, 12)

            def pack(j, u):
                i = no(j, u)
                pe.wait_ge(hot_ready, i + 1)
                wait(pe, slots_taken, i - 1)
                for t in range(TILES):
                    c = (i * TILES + t) * 4
                    c = slice(c, c + 4) if isinstance(c, int) else bass.ds(c, 4)
                    for part in range(2):
                        o = ps[u][:, 8 * t + 4 * part:8 * t + 4 * part + 4]
                        for q, (_, n) in enumerate(CHUNKS):
                            ins = pe.matmul(o, hot[0:n, u, t, q, P * part:P * part + P],
                                            vT[0:n, q, :, :].rearrange("p b k -> p (b k)")[:, c],
                                            start=q == 0, stop=q == 2)
                ins.then_inc(slots_done, 1)

            for u in range(2):
                pack(0, u)
            with pe.Fori(1, GROUPS // 2) as j:
                for u in range(2):
                    pack(j, u)
            pe.wait_ge(slots_taken, GROUPS)

            def count(j, u):
                i = no(j, u)
                pe.wait_ge(mh_ready, i + 1)
                wait(pe, cnt_taken, i - 1)
                for t in range(TILES):
                    ins = pe.matmul(ps[u][:, t:t + 1], mh[:, u, t, :], oneb[:, 0:1], start=True, stop=True)
                ins.then_inc(cnt_done, 1)

            for u in range(2):
                count(0, u)
            with pe.Fori(1, GROUPS // 2) as j:
                for u in range(2):
                    count(j, u)
            end_phase(pe, 1)
            general(pe, 0, general_tensor)

            def aggregate(j, u):
                i = no(j, u)
                pe.wait_ge(m1_ready, TILES * (i + 1))
                wait(pe, mean_ready, TILES * i)
                for t in range(TILES):
                    pe.wait_ge(xgn_ready, TILES * i + t + 1)
                    c = (t % 2) * D
                    ins = pe.matmul(AG[t // 2][:, c:c + D], m1[u][:, t, :], xgn[u][:, t, :], start=True, stop=True)
                ins.then_inc(agg_done, 1)

            def transpose_own(j, u):
                i = no(j, u)
                wait(pe, mhi, 2 * i)
                wait(pe, mlo, 2 * i)
                pe.wait_ge(xn_ready, TILES * (i + 1))
                for k in range(2):
                    for t in range(TILES):
                        ins = pe.transpose(TP[k][:, P * t:P * t + P], xn[u][:, t, P * k:P * k + P], ident[:, :])
                ins.then_inc(xT_done, 1)

            def transpose_means(j, u):
                i = no(j, u)
                pe.wait_ge(mean_ready, TILES * (i + 1))
                pe.wait_ge(xhi, 2 * (i + 1))
                pe.wait_ge(xlo, 2 * (i + 1))
                for k in range(2):
                    for t in range(TILES):
                        ins = pe.transpose(TP[k][:, P * t:P * t + P], mean[u][:, t, P * k:P * k + P], ident[:, :])
                ins.then_inc(mT_done, 1)

            def layer(j, u):
                i = no(j, u)
                pe.wait_ge(mhi, 2 * (i + 1))
                pe.wait_ge(mlo, 2 * (i + 1))
                for k in range(2):
                    wait(pe, h_relu, 2 * (i - 1) + k + 1)
                    c = slice(P * k, P * k + P)
                    terms = [(side, kk) for side in range(2) for kk in range(2)]
                    for n, (side, kk) in enumerate(terms):
                        hi_, lo_ = (mT_hi, mT_lo) if side == 0 else (xT_hi, xT_lo)
                        ins = mm3(pe, HB[k][:, :], w1_hi[:, side, kk, c], w1_lo[:, side, kk, c],
                                  hi_[u][:, kk, :], lo_[u][:, kk, :], n == 0, n == 3)
                    ins.then_inc(h_done, 1)

            def second_layer(j, u):
                i = no(j, u)
                for t in range(TILES):
                    wait(pe, z_ready, TILES * i + t - 1)
                    for k in range(2):
                        if t == 0:
                            pe.wait_ge(h_hi, 2 * i + k + 1)
                            pe.wait_ge(h_lo, 2 * i + k + 1)
                        c = slice(P * t, P * t + P)
                        ins = mm3(pe, ZB[t % 2][:, :], hh[:, k, c], hlo[:, k, c], w2_hi[:, k, :], w2_lo[:, k, :],
                                  k == 0, k == 1)
                    ins.then_inc(z_done, 1)
                    if t == 0 and exists(j, u, 2):
                        transpose_own(*ahead(j, u, 2))

            aggregate(0, 0)
            transpose_own(0, 0)
            transpose_means(0, 0)
            aggregate(0, 1)
            transpose_own(0, 1)

            def body(j, u):
                layer(j, u)
                if exists(j, u, 1):
                    transpose_means(*ahead(j, u, 1))
                if exists(j, u, 2):
                    aggregate(*ahead(j, u, 2))
                second_layer(j, u)

            pipeline(pe, body)
            end_phase(pe, 3)
            general(pe, 1, general_tensor)

            def aggregate2(j, u):
                i = no(j, u)
                pe.wait_ge(m2_ready, TILES * (i + 1))
                pe.wait_ge(gg_in[u], 64 * (j + 1))
                wait(pe, x2_ready, TILES * i)
                wait(pe, o_ready, TILES * (i - 1) - 2)
                for t in range(TILES):
                    c = (t % 2) * D
                    ins = pe.matmul(AG[t // 2][:, c:c + D], m2[u][:, t, :], gg[u][:, t, :], start=True, stop=True)
                    if t % 2 == 1:
                        ins.then_inc(agg2_done, 1)

            def transpose_rows(j, u):
                i = no(j, u)
                pe.wait_ge(x2n_ready, TILES * (i + 1))
                wait(pe, gate_step, GATE_STEPS * (i - 1) + 2)
                wait(pe, wxT_lo, i)
                for k in range(2):
                    for t in range(TILES):
                        ins = pe.transpose(TP[k][:, P * t:P * t + P], x2n[u][:, t, P * k:P * k + P], ident[:, :])
                ins.then_inc(yT_done, 1)

            def first_product(j, u, r):
                i = no(j, u)
                if r in (2, 3):
                    wait(pe, o_ready, TILES * i)
                else:
                    wait(pe, r_relu, 9 * i + (r - 3 if r >= 4 else 0))
                for k in range(2):
                    if r < 2:
                        l_hi, l_lo = sw1_hi[:, k, P * r:P * r + P], sw1_lo[:, k, P * r:P * r + P]
                    else:
                        l_hi, l_lo = ew1_hi[:, k, r - 2, :], ew1_lo[:, k, r - 2, :]
                    ins = mm3(pe, RB[r][:, :], l_hi, l_lo, yT_hi[u][:, k, :], yT_lo[u][:, k, :],
                              k == 0, k == 1)
                ins.then_inc(r_done, 1)

            def second_product(j, u, r):
                i = no(j, u)
                pe.wait_ge(r_relu, 9 * i + r - 1)
                for k in range(2):
                    if r == 7:
                        of, l_hi, l_lo = k, sw2_hi[:, k, :], sw2_lo[:, k, :]
                    else:
                        e = (r - 6) + k
                        of, l_hi, l_lo = 2 + e, ew2_hi[:, e, :], ew2_lo[:, e, :]
                    wait_high(pe, i, of)
                    wait_low(pe, i, of)
                    ins = mm3(pe, RB[r][:, :], l_hi, l_lo, act_hi[:, of, :], act_lo[:, of, :], k == 0, k == 1)
                ins.then_inc(r_done, 1)

            def spread(j, u, q):
                i = no(j, u)
                pe.wait_ge(r_relu, 9 * i + 3 + q)
                pe.matmul(WB[q][:, :], sel[:, q, :], wxT[:, :], start=True, stop=True).then_inc(wb_done, 1)

            def out_terms(j, u, t, terms, first, last):
                i = no(j, u)
                c = slice(P * t, P * t + P)
                o = OBS[t][:, 0:D]
                for n, term in enumerate(terms):
                    f, l = first and n == 0, last and n == len(terms) - 1
                    if term == "bias":
                        ins = pe.matmul(o, wxT[:, c], b3s[:, :], start=f, stop=l)
                        continue
                    r = {"pair0": 6, "shared": 7, "pair1": 8}[term]
                    wait_high(pe, i, r)
                    wait_low(pe, i, r)
                    w_hi, w_lo = (sw3_hi[:, :], sw3_lo[:, :]) if r == 7 else \
                        (ew3_hi[:, (r - 6) // 2, :], ew3_lo[:, (r - 6) // 2, :])
                    ins = mm3(pe, o, act_hi[:, r, c], act_lo[:, r, c], w_hi, w_lo, f, l)
                return ins

            def logits(j, u):
                i = no(j, u)
                pe.wait_ge(yhi, 2 * (i + 1))
                pe.wait_ge(ylo, 2 * (i + 1))
                for t in range(TILES):
                    c = slice(P * t, P * t + P)
                    for k in range(2):
                        pe.matmul(TP[0][:, 8 * t:8 * t + 8], yT_hi[u][:, k, c], gw_hl[:, k, :],
                                  start=k == 0, stop=False)
                        ins = pe.matmul(TP[0][:, 8 * t:8 * t + 8], yT_lo[u][:, k, c], gw_hl[:, k, :],
                                        start=False, stop=k == 1)
                ins.then_inc(lg_done, 1)

            aggregate2(0, 0)
            transpose_rows(0, 0)
            logits(0, 0)
            first_product(0, 0, 0)
            first_product(0, 0, 1)

            def body2(j, u):
                i = no(j, u)
                more, nxt = exists(j, u, 1), ahead(j, u, 1)
                if more:
                    aggregate2(*nxt)
                first_product(j, u, 2)
                pe.wait_ge(wx_ready, i + 1)
                for t in range(TILES):
                    ins = pe.transpose(TP[1][0:96, P * t:P * t + P], wx[:, t, :], ident[:, :])
                ins.then_inc(wxT_done, 1)
                for r in range(3, 6):
                    first_product(j, u, r)
                pe.wait_ge(wxT_lo, i + 1)
                spread(j, u, 0)
                spread(j, u, 1)
                second_product(j, u, 6)
                second_product(j, u, 7)
                if more:
                    transpose_rows(*nxt)
                second_product(j, u, 8)
                for t in range(2):
                    out_terms(j, u, t, ("pair0", "bias", "shared"), True, False)
                if more:
                    logits(*nxt)
                for t in range(2):
                    if more and t == 1:
                        first_product(*nxt, 0)
                    out_terms(j, u, t, ("pair1",), False, True).then_inc(o_done, 1)
                if more:
                    first_product(*nxt, 1)
                for t in range(2, TILES):
                    pe.wait_ge(wb_taken, 2 * i + 2)
                    out_terms(j, u, t, ("pair0", "bias", "shared", "pair1"), True, True).then_inc(o_done, 1)

            pipeline(pe, body2)


def _cols(w):
    k = w.shape[0] // P
    return w.reshape(k, P, w.shape[1]).transpose(1, 0, 2).reshape(P, -1)


def kernel(**inputs):
    import numpy as np
    import concourse.bacc as bacc
    from concourse.bass_utils import run_bass_kernel_spmd

    a = {k.replace("L0_gnn_", "").replace("L0_ffn_", ""): np.asarray(v) for k, v in inputs.items()}
    w2 = np.concatenate([a["W2l"].T, a["W2r"].T], axis=1)
    ew1 = a["eW1"].transpose(1, 0, 2).reshape(D, NEXP * P)
    ew2 = a["eW2"].transpose(1, 0, 2).reshape(P, NEXP * 64)
    ew3 = a["eW3"].reshape(NEXP * 64, D)
    parts = [_cols(m) for m in (a["W1l"].T, a["W1r"].T, w2, a["sW1"])]
    parts += [_cols(a["sW2"]), a["sW3"], _cols(ew1), ew2, _cols(ew3), _cols(a["gW"])]
    bias = [a["b1"].reshape(2, P).T, a["sb1"].reshape(2, P).T, a["sb2"].reshape(1, P).T,
            a["eb1"].T, a["eb2"].reshape(2, P).T]
    arrays = {
        "x": a["x"], "src": a["src"], "dst": a["dst"],
        "wpack": np.ascontiguousarray(np.concatenate(parts, axis=1)),
        "bpack": np.ascontiguousarray(np.concatenate(bias, axis=1)),
        "b2": a["b2"], "gb": a["gb"],
        "b3": np.ascontiguousarray(np.concatenate([a["eb3"], a["sb3"][None]], axis=0)),
    }
    nc = bacc.Bacc("TRN2", target_bir_lowering=False, num_devices=1)
    args = [nc.dram_tensor(f"in_{n}", v.shape, mybir.dt.from_np(v.dtype), kind="ExternalInput").ap()
            for n, v in arrays.items()]
    out = nc.dram_tensor("out_x", (N, D), mybir.dt.float32, kind="ExternalOutput").ap()
    build(nc, *args, out)
    r = run_bass_kernel_spmd(nc, [{f"in_{n}": v for n, v in arrays.items()}], core_ids=[0])
    return r.results[0]["out_x"]
```

```python
import concourse.bass as bass
from concourse import mybir
from contextlib import ExitStack

N, E, D, P = 50000, 75000, 256, 128
TILES = 4
ROWS = TILES * P
GROUPS = -(-N // ROWS)
NPAD = GROUPS * ROWS
NBLK = GROUPS * TILES
LAST = N - (GROUPS - 1) * ROWS
EPS = 1e-5
NEXP = 4

WIN = 256
FAR = 1 << 20
WJ = 4
CHUNKS = [(0, 128), (128, 128)]
EP, EC = 120, 625
assert EP * EC == E
BATCH = 7
STEPS = NBLK // BATCH
ACT_FROM = 6
assert STEPS * BATCH == NBLK and STEPS % 2 == 0
OOB = 65536.0

WCOLS = {}
_at = 0
for _name, _n in (("w1l", 512), ("w1r", 512), ("w2", 1024), ("sw1", 512), ("sw2", 256),
                  ("sw3", 256), ("ew1", 1024), ("ew2", 256), ("ew3", 512), ("gw", 8)):
    WCOLS[_name] = (_at, _n)
    _at += _n
WTOTAL = _at
BCOLS = {"b1": 0, "sb1": 2, "sb2": 4, "eb1": 5, "eb2": 9}
BTOTAL = 11

GATE_STEPS, GATE_EXP1, GATE_EXP2 = 22, 4, 13
GATE_AHEAD = (4, 1, 6, 2)


def build(nc, x, src, dst, wpack, bpack, b2, gb, b3, out):
    fp32, fr, bf16 = mybir.dt.float32, mybir.dt.float32r, mybir.dt.bfloat16
    i32, u32 = mybir.dt.int32, mybir.dt.uint32
    ALU, ACT, AX = mybir.AluOpType, mybir.ActivationFunctionType, mybir.AxisListType

    dst_d = nc.dram_tensor("dst_far", [E + WIN, 1], i32, kind="Internal").ap()
    src_d = nc.dram_tensor("src_far", [E + WIN, 1], i32, kind="Internal").ap()
    hl_d = nc.dram_tensor("hl_rows", [NPAD, D], fp32, kind="Internal").ap()
    z_d = nc.dram_tensor("z_rows", [NPAD, D], fp32, kind="Internal").ap()
    sums_d = nc.dram_tensor("general_sums", [NPAD, D], fp32, kind="Internal").ap()

    ctx = ExitStack()
    with ctx:
        def sb(name, shape, dt=fp32, scope=ctx):
            return scope.enter_context(nc.sbuf_tensor(name, shape, dt))

        def sem(name):
            return ctx.enter_context(nc.semaphore(name))

        def sems(name, n=2):
            return [sem(f"{name}{k}") for k in range(n)]

        w1_hi, w1_lo = (sb(f"w1_{h}", [P, 2, 2, D], fr) for h in ("hi", "lo"))
        w2_hi, w2_lo = (sb(f"w2_{h}", [P, 2, 2 * D], fr) for h in ("hi", "lo"))
        sw1_hi, sw1_lo = (sb(f"sw1_{h}", [P, 2, D], fr) for h in ("hi", "lo"))
        sw2_hi, sw2_lo = (sb(f"sw2_{h}", [P, 2, P], fr) for h in ("hi", "lo"))
        sw3_hi, sw3_lo = (sb(f"sw3_{h}", [P, D], fr) for h in ("hi", "lo"))
        ew1_hi, ew1_lo = (sb(f"ew1_{h}", [P, 2, NEXP, P], fr) for h in ("hi", "lo"))
        ew2_hi, ew2_lo = (sb(f"ew2_{h}", [P, NEXP, P], fr) for h in ("hi", "lo"))
        ew3_hi, ew3_lo = (sb(f"ew3_{h}", [P, 2, D], fr) for h in ("hi", "lo"))
        gw_hl = sb("gw_hl", [P, 2, 2 * NEXP], fr)
        b3s = sb("b3s", [96, D], fr)
        sel = sb("sel", [96, 2, P], fr)
        bcol = sb("bcol", [P, BTOTAL])
        b2b = sb("b2b", [P, D])
        gbb = sb("gbb", [P, NEXP])
        prio = sb("prio", [P, TILES, NEXP])
        ident = sb("ident", [P, P])
        iota = sb("iota", [P, D])
        eps = sb("eps", [P, 1])
        idx_all = sb("idx_all", [P, NBLK], u32)
        dloc_all = sb("dloc_all", [P, NBLK])
        inv_all = sb("inv_all", [P, NBLK])
        sinv_all = sb("sinv_all", [P, NBLK])
        gen, own, neg_own = sb("gen", [P, 1]), sb("own", [P, 1]), sb("neg_own", [P, 1])
        gen_i = sb("gen_i", [1, 1], i32)

        prep = ExitStack()
        wst = sb("wst", [P, WTOTAL], scope=prep)
        b3f = sb("b3f", [96, D], scope=prep)
        selj = sb("selj", [96, 2 * P], scope=prep)
        win_d, win_s = (sb(n, [P, WJ, WIN], i32, scope=prep) for n in ("win_d", "win_s"))
        dstN = sb("dstN", [EP, EC], i32, scope=prep)
        last_dst = sb("last_dst", [EP, 1], scope=prep)
        last_diag = sb("last_diag", [EP, EP], scope=prep)
        below = sb("below", [P, WJ, EC], scope=prep)
        row_f = sb("row_f", [P, WJ], scope=prep)
        row_i = sb("row_i", [P, WJ], u32, scope=prep)
        rows_at = sb("rows_at", [P, WJ, EC], i32, scope=prep)
        in_row = sb("in_row", [P, WJ], scope=prep)
        first_edge = sb("first_edge", [P, WJ], u32, scope=prep)
        far = sb("far", [1, WIN], i32, scope=prep)
        tb = sb("tb", [P, WJ], scope=prep)
        wd, ws, wv, wn, wc, wk_ = (sb(n, [P, WJ, WIN], scope=prep)
                                   for n in ("wd", "ws", "wv", "wn", "wc", "wk_"))
        shi = sb("shi", [P, WJ, WIN], i32, scope=prep)
        slo = sb("slo", [P, WJ, WIN], i32, scope=prep)
        keyT = sb("keyT", [P, len(CHUNKS), WJ * P], scope=prep)
        vT = sb("vT", [P, len(CHUNKS), WJ * P, 4], bf16, scope=prep)
        iob = sb("iob", [P, D], bf16, scope=prep)
        hot = sb("hot", [P, 2, BATCH, len(CHUNKS), D], bf16, scope=prep)
        off = sb("off", [P, 2, BATCH - ACT_FROM, len(CHUNKS), D], bf16, scope=prep)
        mh = sb("mh", [P, 2, BATCH, P], bf16, scope=prep)
        dloc_b = sb("dloc_b", [P, NBLK], bf16, scope=prep)
        oneb = sb("oneb", [P, 2], bf16, scope=prep)
        info = sb("info", [P, NBLK, 8], scope=prep)
        cnt = sb("cnt", [P, NBLK], scope=prep)
        idxf = sb("idxf", [P, NBLK], scope=prep)
        dstS = sb("dstS", [EP, EC], i32, scope=prep)
        falls = sb("falls", [EP, EC], scope=prep)
        ones = sb("ones", [P, P], scope=prep)
        unfit = sb("unfit", [P, 1], scope=prep)
        unfit_w = sb("unfit_w", [P, WJ], scope=prep)
        prep.close()

        one = ExitStack()
        xg = [sb(f"xg{u}", [P, TILES, D], scope=one) for u in range(2)]
        xb = [sb(f"xb{u}", [P, TILES, D], scope=one) for u in range(2)]
        xn = [sb(f"xn{u}", [P, TILES, D], scope=one) for u in range(2)]
        xgn = [sb(f"xgn{u}", [P, TILES, D], scope=one) for u in range(2)]
        m1 = [sb(f"m1{u}", [P, TILES, P], scope=one) for u in range(2)]
        idx1 = [sb(f"idx1{u}", [P, TILES], u32, scope=one) for u in range(2)]
        sinv1 = [sb(f"sinv1{u}", [P, TILES], scope=one) for u in range(2)]
        st1 = [sb(f"st1{u}", [P, 2 * TILES, 6], scope=one) for u in range(2)]
        mv1 = [sb(f"mv1{u}", [P, 2 * TILES, 2], scope=one) for u in range(2)]
        sd1 = [sb(f"sd1{u}", [P, 2 * TILES], scope=one) for u in range(2)]
        rs1 = [sb(f"rs1{u}", [P, 2 * TILES], scope=one) for u in range(2)]
        nm1 = [sb(f"nm1{u}", [P, 2 * TILES], scope=one) for u in range(2)]
        sx = [sb(f"sx{u}", [P, TILES, D], scope=one) for u in range(2)]
        mean = [sb(f"mean{u}", [P, TILES, D], scope=one) for u in range(2)]
        xT_hi, xT_lo, mT_hi, mT_lo = (
            [sb(f"{n}{u}", [P, 2, ROWS], fr, scope=one) for u in range(2)]
            for n in ("xT_hi", "xT_lo", "mT_hi", "mT_lo"))
        ha = sb("ha", [P, 2, ROWS], scope=one)
        hh = sb("hh", [P, 2, ROWS], fr, scope=one)
        hlo = sb("hlo", [P, 2, ROWS], fr, scope=one)
        hl = [sb(f"hl{u}", [P, TILES, D], scope=one) for u in range(2)]
        zs = [sb(f"zs{u}", [P, TILES, D], scope=one) for u in range(2)]
        one.close()

        two = ExitStack()
        gg = [sb(f"gg{u}", [P, TILES, D], scope=two) for u in range(2)]
        zb = [sb(f"zb{u}", [P, TILES, D], scope=two) for u in range(2)]
        xr = [sb(f"xr{u}", [P, TILES, D], scope=two) for u in range(2)]
        gg_hi, gg_lo = ([sb(f"{n}{u}", [P, TILES, D], fr, scope=two) for u in range(2)]
                        for n in ("gg_hi", "gg_lo"))
        m2 = [sb(f"m2{u}", [P, TILES, P], fr, scope=two) for u in range(2)]
        idx2 = [sb(f"idx2{u}", [P, TILES], u32, scope=two) for u in range(2)]
        x2 = [sb(f"x2{u}", [P, TILES, D], scope=two) for u in range(2)]
        x2n = [sb(f"x2n{u}", [P, TILES, D], scope=two) for u in range(2)]
        st2 = [sb(f"st2{u}", [P, TILES, 6], scope=two) for u in range(2)]
        mv2 = [sb(f"mv2{u}", [P, TILES, 2], scope=two) for u in range(2)]
        sd2 = [sb(f"sd2{u}", [P, TILES], scope=two) for u in range(2)]
        rs2 = [sb(f"rs2{u}", [P, TILES], scope=two) for u in range(2)]
        nm2 = [sb(f"nm2{u}", [P, TILES], scope=two) for u in range(2)]
        yT_hi, yT_lo = ([sb(f"{n}{u}", [P, 2, ROWS], fr, scope=two) for u in range(2)]
                        for n in ("yT_hi", "yT_lo"))
        act_a = sb("act_a", [P, 9, ROWS], scope=two)
        act_hi = sb("act_hi", [P, 9, ROWS], fr, scope=two)
        act_lo = sb("act_lo", [P, 9, ROWS], fr, scope=two)
        ob = [sb(f"ob{u}", [P, TILES, D], scope=two) for u in range(2)]
        lg = sb("lg", [P, TILES, 2 * NEXP], scope=two)
        g_t = [sb(f"g_t{k}", [P, TILES, NEXP], scope=two) for k in range(9)]
        g_s = [sb(f"g_s{k}", [P, TILES, 1], scope=two) for k in range(10)]
        sqrt_table = sb("sqrt_table", [P, 1], scope=two)
        wx = sb("wx", [P, TILES, 96], scope=two)
        wxT = sb("wxT", [96, ROWS], fr, scope=two)
        two.close()

        gp = ExitStack()
        g_dst, g_src = (sb(n, [EP, EC], i32, scope=gp) for n in ("g_dst", "g_src"))
        g_dstf = sb("g_dstf", [EP, EC], scope=gp)
        g_tile, g_row = (sb(n, [EP, EC], i32, scope=gp) for n in ("g_tile", "g_row"))
        g_tilef, g_rowf = (sb(n, [EP, EC], scope=gp) for n in ("g_tilef", "g_rowf"))
        g_zero = sb("g_zero", [P, TILES, D], scope=gp)
        g_blocks = sb("g_blocks", [EP, NBLK], scope=gp)
        g_nodes = sb("g_nodes", [P, NBLK], scope=gp)
        g_lower = sb("g_lower", [EP, EP], scope=gp)
        g_from, g_to, g_keep = (sb(n, [EP, 1], u32, scope=gp) for n in ("g_from", "g_to", "g_keep"))
        g_d = sb("g_d", [EP, 1], scope=gp)
        g_db, g_same, g_twin = (sb(n, [EP, EP], scope=gp) for n in ("g_db", "g_same", "g_twin"))
        g_later = sb("g_later", [EP, 1], scope=gp)
        g_in, g_ln, g_sum = (sb(n, [EP, D], scope=gp) for n in ("g_in", "g_ln", "g_sum"))
        g_st, g_mv = sb("g_st", [EP, 6], scope=gp), sb("g_mv", [EP, 2], scope=gp)
        g_sd, g_rs = sb("g_sd", [EP, 1], scope=gp), sb("g_rs", [EP, 1], scope=gp)
        g_hrow, g_htile = sb("g_hrow", [EP, P], scope=gp), sb("g_htile", [EP, NBLK], scope=gp)
        g_cnt = sb("g_cnt", [P, NBLK], scope=gp)
        gp.close()

        ps = [ctx.enter_context(nc.psum_tensor(f"ps{k}", [P, 512], fp32)) for k in range(8)]
        TP, AG, HB, ZB = ps[0:2], ps[2:4], ps[4:6], ps[6:8]
        WB, OBS = ps[6:8], (ps[2], ps[3], ps[7], ps[6])
        RB = (*ps[4:8], *ps[4:6], ps[4], ps[5], ps[4])

        phase_end = sem("phase_end")
        w_in, bias_in, dst_in, et_in, far_set = map(sem, ("w_in", "bias_in", "dst_in", "et_in", "far_set"))
        rows_in, win_in = sem("rows_in"), sem("win_in")
        dstep, pstep = sem("vector_step"), sem("pool_step")
        const_set, last_ready, last_spread, row_ready, first_ready = map(sem, (
            "const_set", "last_ready", "last_spread", "row_ready", "first_ready"))
        fields_ready, ft_done, ft_taken, hot_ready, slots_done, slots_taken = map(sem, (
            "fields_ready", "ft_done", "ft_taken", "hot_ready", "slots_done", "slots_taken"))
        key_off, hot_act_ready = sem("key_off"), sem("hot_act_ready")
        mh_ready, cnt_done, cnt_taken = map(sem, ("mh_ready", "cnt_done", "cnt_taken"))
        x_in, xg_in, xr_in, hl_out, z_out = (sems(n) for n in ("x_in", "xg_in", "xr_in", "hl_out", "z_out"))
        stats1, ln1a, std1, rstd1, ln1b, xn_ready, xgn_ready, m1_ready = map(sem, (
            "stats1", "ln1a", "std1", "rstd1", "ln1b", "xn_ready", "xgn_ready", "m1_ready"))
        idx1_ready, sinv_ready, sx_ready, xb_ready = map(sem, ("idx1_ready", "sinv_ready", "sx_ready", "xb_ready"))
        agg_done, xT_done, mT_done, mean_ready = map(sem, ("agg_done", "xT_done", "mT_done", "mean_ready"))
        xhi, xlo, mhi, mlo = map(sem, ("xhi", "xlo", "mhi", "mlo"))
        h_done, h_relu, h_hi, h_lo, z_done, hl_ready, z1_ready, z_ready = map(sem, (
            "h_done", "h_relu", "h_hi", "h_lo", "z_done", "hl_ready", "z1_ready", "z_ready"))
        zl_in, gg_in, o_out = sems("zl_in"), sems("gg_in"), sems("o_out")
        idx2_ready, m2_ready, agg2_done, x2_ready, stats2, ln2a, std2, rstd2, ln2b, x2n_ready = map(sem, (
            "idx2_ready", "m2_ready", "agg2_done", "x2_ready", "stats2", "ln2a", "std2", "rstd2", "ln2b", "x2n_ready"))
        yT_done, yhi, ylo, lg_done, gate_step, wx_ready, wxT_done, wxT_hi, wxT_lo = map(sem, (
            "yT_done", "yhi", "ylo", "lg_done", "gate_step", "wx_ready", "wxT_done", "wxT_hi", "wxT_lo"))
        gate_exp = sem("gate_exp")
        wx_set = sem("wx_set")
        gathers_asked = sem("gathers_asked")
        r_done, r_relu, r_hi_a, r_hi_v, r_lo, wb_done, wb_taken, o_done, o_ready = map(sem, (
            "r_done", "r_relu", "r_hi_a", "r_hi_v", "r_lo", "wb_done", "wb_taken", "o_done", "o_ready"))
        r_lo_p, gg_hi_ready, gg_lo_ready = map(sem, ("r_lo_p", "gg_hi_ready", "gg_lo_ready"))
        g_edges_in, g_asked = sem("g_edges_in"), sem("g_asked")
        g_made, g_set = sems("g_made"), sems("g_set")
        g_zeroed, g_cols, g_turned, g_step, g_std, g_rows_in, g_sums_in, g_summed, g_counted, g_added, g_stored = (
            sems(n) for n in ("g_zeroed", "g_cols", "g_turned", "g_step", "g_std", "g_rows_in", "g_sums_in",
                              "g_summed", "g_counted", "g_added", "g_stored"))
        succ_in, unfit_ready, unfit_sum = map(sem, ("succ_in", "unfit_ready", "unfit_sum"))

        block = ctx.enter_context(nc.Block())

        def wait(eng, s, v):
            if isinstance(v, int) and v <= 0:
                return
            eng.wait_ge(s, v)

        def end_phase(eng, n):
            eng.drain().then_inc(phase_end, 1)
            eng.wait_ge(phase_end, 5 * n)

        def pipeline(eng, body):
            for u in range(2):
                body(0, u)
            with eng.Fori(1, GROUPS // 2 - 3) as j:
                for u in range(2):
                    body(j, u)
            for j in range(GROUPS // 2 - 3, GROUPS // 2):
                for u in range(2):
                    body(j, u)

        def ahead(j, u, k):
            return j + (u + k) // 2, (u + k) % 2

        def exists(j, u, k):
            return not isinstance(j, int) or 2 * j + u + k < GROUPS

        def no(j, u):
            return 2 * j + u

        def wait_low(eng, i, r):
            if r < 2:
                wait(eng, r_lo_p, 2 * i + r + 1)
            else:
                wait(eng, r_lo, 7 * i + r - 1)

        def wait_high(eng, i, r):
            if r < 4:
                eng.wait_ge(r_hi_a, 4 * i + r + 1)
            else:
                eng.wait_ge(r_hi_v, 5 * i + r - 3)

        def mm3(pe, o, l_hi, l_lo, r_hi_, r_lo_, first, last):
            pe.matmul(o, l_hi, r_hi_, start=first, stop=False)
            pe.matmul(o, l_hi, r_lo_, start=False, stop=False)
            return pe.matmul(o, l_lo, r_hi_, start=False, stop=last)

        def rows_of(t, j, u, half=None):
            first, n = no(j, u) * ROWS, ROWS
            if half is not None:
                first, n = first + half * 2 * P, 2 * P
            if isinstance(first, int):
                ap = t[first:first + n, :]
            else:
                ap = t[bass.ds(first, n), :]
            return ap.rearrange("(t p) d -> p t d", p=P)

        def first_tile(eng, j, u):
            c = no(j, u) * TILES
            return c if isinstance(c, int) else eng.snap(c)

        def cols(t, c):
            return t[:, c:c + TILES] if isinstance(c, int) else t[:, bass.ds(c, TILES)]

        def col(t, j, u, k):
            c = no(j, u) * TILES + k
            return t[:, c:c + 1] if isinstance(c, int) else t[:, bass.ds(c, 1)]

        def tail_rows(t, half):
            first = (GROUPS - 1) * ROWS
            if half == 0:
                return t[first:first + 2 * P, :].rearrange("(t p) d -> p t d", p=P), P
            n = LAST - 2 * P
            return t[first + 2 * P:N, :], n

        def is_last(j, u):
            return isinstance(j, int) and 2 * j + u == GROUPS - 1

        def edge_steps(eng, step):
            step(0)
            with eng.Fori(1, EC) as c:
                step(c)

        def edge_col(t, c):
            return t[:, c:c + 1] if isinstance(c, int) else t[:, bass.ds(c, 1)]

        G_STEPS = (11, 4)

        def general_pool(pool, q):
            pool.dma_start(g_dst[:, :], dst.rearrange("(p c) -> p c", p=EP)).then_inc(g_edges_in, 16)
            pool.dma_start(g_src[:, :], src.rearrange("(p c) -> p c", p=EP)).then_inc(g_edges_in, 16)
            pool.iota(g_blocks[:, :], [[1, NBLK]], base=0, channel_multiplier=0,
                      allow_small_or_imprecise_dtypes=True)
            pool.iota(g_nodes[:, :], [[P, NBLK]], base=0, channel_multiplier=1,
                      allow_small_or_imprecise_dtypes=True)
            pool.iota(dloc_all[:, :], [[0, NBLK]], base=0, channel_multiplier=1,
                      allow_small_or_imprecise_dtypes=True)
            pool.memset(g_zero[:, :, :], 0.0)
            pool.memset(g_lower[:, :], 1.0).then_inc(g_made[q], 1)
            pool.wait_ge(g_made[q], 1)
            pool.affine_select(out=g_lower[:, :], in_=g_lower[:, :], compare_op=ALU.is_gt, fill=0.0,
                               base=0, pattern=[[-1, EP]], channel_multiplier=1).then_inc(g_made[q], 1)
            pool.wait_ge(g_made[q], 2)
            with pool.Fori(0, GROUPS) as g:
                pool.dma_start(rows_of(sums_d, 0, g), g_zero[:, :, :]).then_inc(g_zeroed[q], 16)
            pool.wait_ge(g_zeroed[q], 16 * GROUPS)
            bound = pool.to_reg(N - 1)
            table = x if q == 0 else hl_d

            def step(c):
                pool.wait_ge(g_cols[q], 4 * (c + 1))
                pool.sem_inc(g_asked, 1)
                pool.indirect_dma_start(g_in[:, :], None, table,
                                        bass.IndirectOffsetOnAxis(g_from[:, 0:1], 0),
                                        bounds_check=bound, oob_is_err=False).then_inc(g_rows_in[q], 16)
                pool.indirect_dma_start(g_sum[:, :], None, sums_d,
                                        bass.IndirectOffsetOnAxis(g_to[:, 0:1], 0),
                                        bounds_check=bound, oob_is_err=False).then_inc(g_sums_in[q], 16)
                pool.wait_ge(g_added[q], c + 1)
                pool.sem_inc(g_asked, 1)
                pool.indirect_dma_start(sums_d, bass.IndirectOffsetOnAxis(g_keep[:, 0:1], 0),
                                        g_sum[:, :], None,
                                        bounds_check=bound, oob_is_err=False).then_inc(g_stored[q], 16)

            edge_steps(pool, step)
            pool.wait_ge(g_stored[q], 16 * EC)

        def general_vector(dve, q):
            dve.wait_ge(g_edges_in, 32 * (q + 1))
            dve.wait_ge(g_made[q], 2)
            dve.tensor_copy(g_dstf[:, :], g_dst[:, :]).then_inc(g_set[q], 1)
            dve.tensor_scalar(g_tile[:, :], g_dst[:, :], 7, None, ALU.logical_shift_right).then_inc(g_set[q], 1)
            dve.tensor_scalar(g_row[:, :], g_dst[:, :], P - 1, None, ALU.bitwise_and).then_inc(g_set[q], 1)
            dve.memset(g_cnt[:, :], 0.0).then_inc(g_set[q], 1)
            dve.wait_ge(g_set[q], 4)
            dve.tensor_copy(g_tilef[:, :], g_tile[:, :]).then_inc(g_set[q], 1)
            dve.tensor_copy(g_rowf[:, :], g_row[:, :]).then_inc(g_set[q], 1)
            dve.wait_ge(g_set[q], 6)

            def step(c):
                n = [0]

                def done(ins):
                    n[0] += 1
                    return ins.then_inc(g_step[q], 1)

                def due():
                    dve.wait_ge(g_step[q], G_STEPS[q] * c + n[0])

                wait(dve, g_stored[q], 16 * c)
                wait(dve, g_step[q], G_STEPS[q] * c)
                dve.tensor_copy(g_from[:, :], edge_col(g_src, c)).then_inc(g_cols[q], 1)
                dve.tensor_copy(g_to[:, :], edge_col(g_dst, c)).then_inc(g_cols[q], 1)
                dve.tensor_copy(g_d[:, :], edge_col(g_dstf, c)).then_inc(g_cols[q], 1)
                dve.tensor_copy(g_db[:, :], edge_col(g_dstf, c).to_broadcast([EP, EP])).then_inc(g_cols[q], 1)
                dve.wait_ge(g_turned[q], c + 1)
                done(dve.tensor_scalar(g_same[:, :], ps[0][0:EP, 0:EP], g_d[:, 0:1], None, ALU.is_equal))
                due()
                done(dve.tensor_tensor(g_twin[:, :], g_same[:, :], g_lower[:, :], ALU.mult))
                due()
                done(dve.tensor_reduce(g_later[:, :], g_twin[:, :], AX.X, ALU.max))
                due()
                done(dve.scalar_tensor_tensor(out=g_keep[:, :], in0=g_later[:, :], scalar=OOB, in1=g_d[:, :],
                                              op0=ALU.mult, op1=ALU.add))
                dve.wait_ge(g_rows_in[q], 16 * (c + 1))
                if q == 0:
                    done(dve.bn_stats(g_st[:, :], g_in[:, :]))
                    due()
                    done(dve.tensor_scalar(g_hrow[:, :], iota[0:EP, 0:P], edge_col(g_rowf, c), None, ALU.is_equal))
                    done(dve.bn_aggr(g_mv[:, :], g_st[:, :]))
                    done(dve.tensor_scalar(g_htile[:, :], g_blocks[:, :], edge_col(g_tilef, c), None, ALU.is_equal))
                    dve.wait_ge(g_std[q], c + 1)
                    done(dve.reciprocal(g_rs[:, :], g_sd[:, :]))
                    due()
                    done(dve.tensor_scalar(g_ln[:, :], g_in[:, :], g_mv[:, 0:1], g_rs[:, 0:1],
                                           ALU.subtract, ALU.mult))
                    dve.wait_ge(g_counted[q], c + 1)
                    done(dve.tensor_tensor(g_cnt[:, :], ps[2][:, 0:NBLK], g_cnt[:, :], ALU.add))
                assert n[0] == G_STEPS[q]
                due()
                dve.wait_ge(g_summed[q], c + 1)
                dve.wait_ge(g_sums_in[q], 16 * (c + 1))
                dve.tensor_tensor(g_sum[:, :], ps[1][0:EP, 0:D], g_sum[:, :], ALU.add).then_inc(g_added[q], 1)

            edge_steps(dve, step)
            if q == 0:
                dve.wait_ge(g_step[q], G_STEPS[q] * EC)
                dve.tensor_copy(idx_all[:, :], g_nodes[:, :])
                dve.memset(sinv_all[:, :], 0.0)
                dve.tensor_scalar(g_cnt[:, :], g_cnt[:, :], 1.0, None, ALU.max).then_inc(g_set[q], 1)
                dve.wait_ge(g_set[q], 7)
                dve.reciprocal(inv_all[:, :], g_cnt[:, :])

        def general_scalar(act, q):
            def step(c):
                act.wait_ge(g_step[q], G_STEPS[q] * c + 7)
                act.activation(g_sd[:, :], g_mv[:, 1:2], ACT.Sqrt, bias=eps[0:EP, 0:1]).then_inc(g_std[q], 1)

            if q == 0:
                edge_steps(act, step)

        def general_tensor(pe, q):
            def step(c):
                pe.wait_ge(g_cols[q], 4 * (c + 1))
                pe.transpose(ps[0][0:EP, 0:EP], g_db[:, :], ident[0:EP, 0:EP]).then_inc(g_turned[q], 1)
                if q == 0:
                    pe.wait_ge(g_step[q], G_STEPS[q] * c + 10)
                    pe.matmul(ps[1][0:EP, 0:D], g_same[:, :], g_ln[:, :], start=True, stop=True)\
                      .then_inc(g_summed[q], 1)
                    pe.matmul(ps[2][:, 0:NBLK], g_hrow[:, :], g_htile[:, :], start=True, stop=True)\
                      .then_inc(g_counted[q], 1)
                else:
                    pe.wait_ge(g_step[q], G_STEPS[q] * c + 1)
                    pe.wait_ge(g_rows_in[q], 16 * (c + 1))
                    pe.matmul(ps[1][0:EP, 0:D], g_same[:, :], g_in[:, :], start=True, stop=True)\
                      .then_inc(g_summed[q], 1)

            edge_steps(pe, step)

        def general(eng, q, program):
            needed = eng.value_load(gen_i[0:1, 0:1], min_val=0, max_val=1)
            if program is not None:
                with eng.If(needed > 0):
                    program(eng, q)
            end_phase(eng, 2 * q + 2)
            return needed

        @block.sync
        def _(sp):
            sp.dma_start(dstN[:, :], dst.rearrange("(p c) -> p c", p=EP)).then_inc(dst_in, 16)
            for of, to in ((dst, dst_d), (src, src_d)):
                sp.dma_start(to[0:E, :].rearrange("(r w) c -> r (w c)", w=EC),
                             of.rearrange("(r w) -> r w", w=EC)).then_inc(et_in, 16)
            sp.wait_ge(far_set, 2)
            for to in (dst_d, src_d):
                sp.dma_start(to[E:E + WIN, :].rearrange("w c -> c w"), far[0:1, :]).then_inc(et_in, 16)
            sp.dma_start(dstS[0:EP - 1, :], dst[1:1 + (EP - 1) * EC].rearrange("(p c) -> p c", c=EC))\
              .then_inc(succ_in, 16)
            sp.dma_start(dstS[EP - 1:EP, 0:EC - 1], dst[1 + (EP - 1) * EC:E].rearrange("(p c) -> p c", p=1))\
              .then_inc(succ_in, 16)
            sp.dma_start(wst[:, :], wpack).then_inc(w_in, 16)
            sp.dma_start(bcol[:, :], bpack).then_inc(bias_in, 16)
            sp.dma_start(b2b[:, :], b2[None, :].to_broadcast([P, D])).then_inc(bias_in, 16)
            sp.dma_start(gbb[:, :], gb[None, :].to_broadcast([P, NEXP])).then_inc(bias_in, 16)
            sp.wait_ge(const_set, 1)
            for k in (0, 32, 64):
                sp.dma_start(b3f[k:k + 5, :], b3).then_inc(bias_in, 16)
            sp.wait_ge(bias_in, 96)
            end_phase(sp, 1)
            general(sp, 0, None)

            def load_x(j, u):
                for half in range(2):
                    if is_last(j, u):
                        rows, n = tail_rows(x, half)
                        to = xb[u][0:n, 0:2, :] if half == 0 else xb[u][0:n, 2, :]
                    else:
                        rows, to = rows_of(x, j, u, half), xb[u][:, 2 * half:2 * half + 2, :]
                    sp.dma_start(to, rows).then_inc(x_in[u], 16)

            for g in range(2):
                load_x(0, g)
            for g in range(2, 4):
                sp.wait_ge(xn_ready, TILES * (g - 1))
                load_x(1, g % 2)

            def body(j, u):
                i = no(j, u)
                if exists(j, u, 4):
                    sp.wait_ge(xn_ready, TILES * (i + 3))
                    load_x(*ahead(j, u, 4))
                sp.wait_ge(hl_ready, TILES * (i + 1))
                sp.dma_start(rows_of(hl_d, j, u), hl[u][:, :, :]).then_inc(hl_out[u], 16)
                sp.wait_ge(z_ready, TILES * (i + 1))
                sp.dma_start(rows_of(z_d, j, u), zs[u][:, :, :]).then_inc(z_out[u], 16)

            pipeline(sp, body)
            for u in range(2):
                sp.wait_ge(hl_out[u], 16 * (GROUPS // 2))
                sp.wait_ge(z_out[u], 16 * (GROUPS // 2))
            end_phase(sp, 3)
            general(sp, 1, None)

            def load_xr(j, u):
                for half in range(2):
                    if is_last(j, u):
                        rows, n = tail_rows(x, half)
                        to = xr[u][0:n, 0:2, :] if half == 0 else xr[u][0:n, 2, :]
                    else:
                        rows, to = rows_of(x, j, u, half), xr[u][:, 2 * half:2 * half + 2, :]
                    sp.dma_start(to, rows).then_inc(xr_in[u], 16)

            def load_z(j, u):
                sp.dma_start(zb[u][:, :, :], rows_of(z_d, j, u)).then_inc(zl_in[u], 16)
                load_xr(j, u)

            for g in range(2):
                load_z(0, g)
            sp.wait_ge(x2_ready, TILES)
            load_z(1, 0)

            def body2(j, u):
                i = no(j, u)
                if exists(j, u, 3):
                    sp.wait_ge(x2_ready, TILES * (i + 2))
                    load_z(*ahead(j, u, 3))
                sp.wait_ge(o_ready, TILES * (i + 1))
                for half in range(2):
                    if is_last(j, u):
                        rows, n = tail_rows(out, half)
                        of = ob[u][0:n, 0:2, :] if half == 0 else ob[u][0:n, 2, :]
                    else:
                        rows, of = rows_of(out, j, u, half), ob[u][:, 2 * half:2 * half + 2, :]
                    sp.dma_start(rows, of).then_inc(o_out[u], 16)

            pipeline(sp, body2)
            for u in range(2):
                sp.wait_ge(o_out[u], 32 * (GROUPS // 2))

        @block.gpsimd
        def _(pool):
            step = [0]

            def link(ins):
                step[0] += 1
                ins.then_inc(pstep, 1)
                pool.wait_ge(pstep, step[0])

            pool.memset(far[:, :], FAR).then_inc(far_set, 1)
            pool.memset(dstS[:, :], FAR).then_inc(far_set, 1)
            pool.iota(tb[:, :], [[P * P, WJ]], base=0, channel_multiplier=P,
                      allow_small_or_imprecise_dtypes=True)
            pool.memset(ones[:, :], 1.0)
            pool.memset(unfit[:, :], 0.0)
            link(pool.memset(ident[:, :], 0.0))
            link(pool.affine_select(out=ident[:, :], in_=ident[:, :], compare_op=ALU.not_equal, fill=1.0,
                                    base=0, pattern=[[-1, P]], channel_multiplier=1))
            link(pool.memset(b3f[:, :], 0.0))
            pool.drain().then_inc(const_set, 1)

            pool.iota(iota[:, :], [[1, D]], base=0, channel_multiplier=0,
                      allow_small_or_imprecise_dtypes=True)
            pool.iota(iob[:, :], [[1, D]], base=0, channel_multiplier=0,
                      allow_small_or_imprecise_dtypes=True)
            pool.iota(prio[:, :, :], [[0, TILES], [-1, NEXP]], base=NEXP, channel_multiplier=0,
                      allow_small_or_imprecise_dtypes=True)
            pool.memset(oneb[:, :], 1.0)
            pool.memset(eps[:, :], EPS)
            link(pool.memset(selj[:, :], 1.0))
            for first in (0, 32):
                v = selj[first:first + 32, :].rearrange("r (q m) -> r q m", q=2)
                link(pool.affine_select(out=v, in_=v, compare_op=ALU.is_ge, fill=0.0, base=0,
                                        pattern=[[P, 2], [1, P]], channel_multiplier=-64))
                link(pool.affine_select(out=v, in_=v, compare_op=ALU.is_ge, fill=0.0, base=63,
                                        pattern=[[-P, 2], [-1, P]], channel_multiplier=64))
            link(pool.memset(selj[64:96, :], 0.0))
            pool.drain().then_inc(const_set, 1)

            pool.wait_ge(row_ready, 1)
            for j in range(WJ):
                pool.indirect_dma_start(rows_at[:, j, :], None, dst.rearrange("(p c) -> p c", p=EP),
                                        bass.IndirectOffsetOnAxis(row_i[:, j:j + 1], 0)).then_inc(rows_in, 16)
            pool.wait_ge(et_in, 16 * 4)
            pool.wait_ge(first_ready, 1)
            for table, to in ((dst_d, win_d), (src_d, win_s)):
                for j in range(WJ):
                    pool.indirect_dma_start(to[:, j, :], None, table,
                                            bass.IndirectOffsetOnAxis(first_edge[:, j:j + 1], 0)).then_inc(win_in, 16)
            pool.wait_ge(win_in, 16 * 2 * WJ)
            end_phase(pool, 1)
            needed = general(pool, 0, general_pool)

            bound = pool.to_reg(N - 1)

            def gather_rows(to, table, idx, ready):
                for cond, rows in ((needed == 0, table), (needed > 0, sums_d)):
                    with pool.If(cond):
                        for t in range(TILES):
                            pool.indirect_dma_start(to[:, t, :], None, rows,
                                                    bass.IndirectOffsetOnAxis(idx[:, t:t + 1], 0),
                                                    bounds_check=bound, oob_is_err=False).then_inc(ready, 16)

            def gather(j, u, wait_for=None):
                i = no(j, u)
                c = first_tile(pool, j, u)
                if wait_for is not None:
                    pool.wait_ge(xgn_ready, wait_for)
                pool.tensor_copy(idx1[u][:, :], cols(idx_all, c)).then_inc(idx1_ready, 1)
                pool.wait_ge(idx1_ready, i + 1)
                pool.sem_inc(gathers_asked, 1)
                gather_rows(xg[u], x, idx1[u], xg_in[u])

            def scaled_own(j, u):
                i = no(j, u)
                c = first_tile(pool, j, u)
                pool.wait_ge(xn_ready, TILES * (i + 1))
                wait(pool, mean_ready, TILES * (i - 1))
                pool.tensor_copy(sinv1[u][:, :], cols(sinv_all, c)).then_inc(sinv_ready, 1)
                pool.wait_ge(sinv_ready, i + 1)
                pool.tensor_tensor(sx[u][:, :, :], xn[u][:, :, :],
                                   sinv1[u][:, :].unsqueeze(2).to_broadcast([P, TILES, D]),
                                   ALU.mult).then_inc(sx_ready, 1)

            for u in range(2):
                link(pool.memset(xg[u][:, :, :], 1.0))
                gather(0, u)
            for u in range(2):
                scaled_own(0, u)
                gather(1, u, TILES * (u + 1))

            def body(j, u):
                if exists(j, u, 4):
                    gather(*ahead(j, u, 4), TILES * (no(j, u) + 3))
                if exists(j, u, 2):
                    scaled_own(*ahead(j, u, 2))

            pipeline(pool, body)
            end_phase(pool, 3)
            general(pool, 1, general_pool)

            def gather2(j, u, wait_for=None):
                i = no(j, u)
                c = first_tile(pool, j, u)
                if wait_for is not None:
                    pool.wait_ge(gg_lo_ready, wait_for)
                pool.tensor_copy(idx2[u][:, :], cols(idx_all, c)).then_inc(idx2_ready, 1)
                pool.wait_ge(idx2_ready, i + 1)
                pool.sem_inc(gathers_asked, 1)
                gather_rows(gg[u], hl_d, idx2[u], gg_in[u])

            def own_share(j, u):
                i = no(j, u)
                pool.wait_ge(zl_in[u], 16 * (j + 1))
                pool.tensor_tensor(zb[u][:, :, :], zb[u][:, :, :],
                                   b2b[:, None, :].to_broadcast([P, TILES, D]), ALU.add).then_inc(xb_ready, 1)
                pool.wait_ge(xr_in[u], 32 * (j + 1))
                pool.wait_ge(xb_ready, 2 * i + 1)
                pool.tensor_tensor(zb[u][:, :, :], zb[u][:, :, :], xr[u][:, :, :], ALU.add).then_inc(xb_ready, 1)

            def rest_low(j, u, r):
                i = no(j, u)
                pool.wait_ge(r_hi_a, 4 * i + r + 1)
                pool.tensor_tensor(act_lo[:, r, :], act_a[:, r, :], act_hi[:, r, :].bitcast(fp32),
                                   ALU.subtract).then_inc(r_lo_p, 1)

            def gathered_low(j, u):
                i = no(j, u)
                pool.wait_ge(gg_hi_ready, i + 1)
                pool.tensor_tensor(gg_lo[u][:, :, :], gg[u][:, :, :], gg_hi[u][:, :, :].bitcast(fp32),
                                   ALU.subtract).then_inc(gg_lo_ready, 1)

            for u in range(2):
                link(pool.memset(gg[u][:, :, :], 1.0))
                gather2(0, u)
                own_share(0, u)
                if u == 0:
                    gathered_low(0, 0)
                if u == 0:
                    link(pool.memset(wx[:, :, :], 0.0))
                    for c in (NEXP, 64 + NEXP):
                        link(pool.memset(wx[:, :, c:c + 1], 1.0))
                    pool.sem_inc(wx_set, 1)
            gather2(1, 0, 1)
            gathered_low(0, 1)
            rest_low(0, 0, 0)
            rest_low(0, 0, 1)

            def body2(j, u):
                if exists(j, u, 3):
                    gather2(*ahead(j, u, 3), no(j, u) + 2)
                if exists(j, u, 2):
                    own_share(*ahead(j, u, 2))
                    gathered_low(*ahead(j, u, 2))
                if exists(j, u, 1):
                    rest_low(*ahead(j, u, 1), 0)
                    rest_low(*ahead(j, u, 1), 1)

            pipeline(pool, body2)

        @block.scalar
        def _(act):
            for f in range(4):
                for q, (_, n) in enumerate(CHUNKS):
                    k = len(CHUNKS) * f + q
                    act.wait_ge(ft_done, k + 1)
                    to = keyT[0:n, q, :] if f == 0 else vT[0:n, q, :, f - 1]
                    act.activation(to, ps[k % 4][0:n, :], ACT.Copy).then_inc(ft_taken, 1)
            act.wait_ge(ft_taken, 4 * len(CHUNKS))

            def key_hots(j, u):
                i = no(j, u)
                wait(act, slots_done, i - 1)
                for t in range(ACT_FROM, BATCH):
                    c = i * BATCH + t
                    c = slice(c, c + 1) if isinstance(c, int) else bass.ds(c, 1)
                    for q in range(len(CHUNKS)):
                        ins = act.activation(off[:, u, t - ACT_FROM, q, :], iob[:, :], ACT.Abs, bias=keyT[:, q, c],
                                             scale=-1.0)
                ins.then_inc(key_off, 1)
                act.wait_ge(key_off, i + 1)
                act.activation(hot[:, u, ACT_FROM:BATCH, :, :], off[:, u, :, :, :], ACT.Relu, bias=1.0,
                               scale=-1.0).then_inc(hot_act_ready, 1)

            def take_slots(j, u):
                i = no(j, u)
                c = slice(i * BATCH, (i + 1) * BATCH) if isinstance(i, int) else bass.ds(i * BATCH, BATCH)
                act.wait_ge(slots_done, i + 1)
                act.activation(info[:, c, :], ps[u][:, 0:8 * BATCH].rearrange("p (t k) -> p t k", k=8),
                               ACT.Copy).then_inc(slots_taken, 1)

            key_hots(0, 0)
            for u in range(2):
                key_hots(*ahead(0, u, 1))
                take_slots(0, u)
            with act.Fori(1, STEPS // 2 - 1) as j:
                for u in range(2):
                    key_hots(*ahead(j, u, 1))
                    take_slots(j, u)
            key_hots(STEPS // 2 - 1, 1)
            for u in range(2):
                take_slots(STEPS // 2 - 1, u)
            with act.Fori(0, STEPS // 2) as j:
                for u in range(2):
                    act.wait_ge(cnt_done, 2 * j + u + 1)
                    act.activation(cnt[:, bass.ds((2 * j + u) * BATCH, BATCH)], ps[u][:, 0:BATCH],
                                   ACT.Copy).then_inc(cnt_taken, 1)
            end_phase(act, 1)
            general(act, 0, general_scalar)

            def deviations(j, u):
                i = no(j, u)
                act.wait_ge(ln1a, i + 1)
                act.activation(sd1[u][:, :], mv1[u][:, :, 1], ACT.Sqrt, bias=eps[:, 0:1]).then_inc(std1, 1)

            def normalise(j, u, tiles):
                i = no(j, u)
                for t in tiles:
                    if t == 0:
                        act.wait_ge(ln1b, i + 1)
                        wait(act, agg_done, i - 1)
                    if t == TILES:
                        wait(act, xT_done, i - 1)
                        wait(act, sx_ready, i - 1)
                    k = (t + TILES) % (2 * TILES)
                    to, of, ready = (xgn, xg, xgn_ready) if t < TILES else (xn, xb, xn_ready)
                    act.activation(to[u][:, t % TILES, :], of[u][:, t % TILES, :], ACT.Identity,
                                   bias=nm1[u][:, k:k + 1], scale=rs1[u][:, k:k + 1]).then_inc(ready, 1)

            def part(to, done, free, taken, j, u):
                i = no(j, u)
                act.wait_ge(done, i + 1)
                wait(act, h_done, 2 * (i - 1))
                for k in range(2):
                    act.activation(to[u][:, k, :], TP[k][:, :], ACT.Copy).then_inc(taken, 1)

            def x_part(j, u):
                part(xT_hi, xT_done, None, xhi, j, u)

            def m_part(j, u):
                part(mT_hi, mT_done, None, mhi, j, u)

            def both(j, u):
                deviations(j, u)
                normalise(j, u, range(2 * TILES))

            both(0, 0)
            both(0, 1)
            x_part(0, 0)
            m_part(0, 0)
            x_part(0, 1)
            both(1, 0)

            def body(j, u):
                i = no(j, u)
                for k in range(2):
                    act.wait_ge(h_done, 2 * i + k + 1)
                    wait(act, h_lo, 2 * (i - 1) + k + 1)
                    act.activation(ha[:, k, :], HB[k][:, :], ACT.Relu,
                                   bias=bcol[:, BCOLS["b1"] + k:BCOLS["b1"] + k + 1]).then_inc(h_relu, 1)
                    act.wait_ge(h_relu, 2 * i + k + 1)
                    wait(act, z_done, TILES * i)
                    act.activation(hh[:, k, :], ha[:, k, :], ACT.Copy).then_inc(h_hi, 1)
                    if k == 0 and exists(j, u, 3):
                        deviations(*ahead(j, u, 3))
                if exists(j, u, 1):
                    m_part(*ahead(j, u, 1))
                for t in range(TILES):
                    act.wait_ge(z_done, TILES * i + t + 1)
                    if t == 0:
                        wait(act, hl_out[u], 16 * j)
                        wait(act, z_ready, TILES * (i - 1))
                    act.activation(hl[u][:, t, :], ZB[t % 2][:, 0:D], ACT.Copy).then_inc(hl_ready, 1)
                    if t == 0 and exists(j, u, 2):
                        x_part(*ahead(j, u, 2))
                    if exists(j, u, 3):
                        normalise(*ahead(j, u, 3), ((), (0, 1), (2, 3), (4, 5, 6, 7))[t])

            pipeline(act, body)
            end_phase(act, 3)
            general(act, 1, general_scalar)

            def deviations2(j, u):
                act.wait_ge(ln2a, no(j, u) + 1)
                act.activation(sd2[u][:, :], mv2[u][:, :, 1], ACT.Sqrt, bias=eps[:, 0:1]).then_inc(std2, 1)

            def normalise2(j, u, tiles):
                i = no(j, u)
                if 0 in tiles:
                    act.wait_ge(ln2b, i + 1)
                    wait(act, yT_done, i - 1)
                for t in tiles:
                    act.activation(x2n[u][:, t, :], x2[u][:, t, :], ACT.Identity, bias=nm2[u][:, t:t + 1],
                                   scale=rs2[u][:, t:t + 1]).then_inc(x2n_ready, 1)

            def y_part(j, u):
                i = no(j, u)
                act.wait_ge(yT_done, i + 1)
                for k in range(2):
                    act.activation(yT_hi[u][:, k, :], TP[k][:, :], ACT.Copy).then_inc(yhi, 1)

            def relu(j, u, r):
                i = no(j, u)
                act.wait_ge(r_done, 9 * i + r + 1)
                wait_low(act, i - 1, r)
                c = BCOLS["sb1"] + r if r < 2 else BCOLS["eb1"] + r - 2 if r < 6 else \
                    {6: BCOLS["eb2"], 7: BCOLS["sb2"], 8: BCOLS["eb2"] + 1}[r]
                act.activation(act_a[:, r, :], RB[r][:, :], ACT.Relu, bias=bcol[:, c:c + 1])\
                   .then_inc(r_relu, 1)
                if r < 4:
                    act.wait_ge(r_relu, 9 * i + r + 1)
                    act.activation(act_hi[:, r, :], act_a[:, r, :], ACT.Copy).then_inc(r_hi_a, 1)

            def gate_exp1(j, u):
                act.wait_ge(gate_step, GATE_STEPS * no(j, u) + GATE_EXP1)
                act.activation(g_t[1][:, :, :], g_t[1][:, :, :], ACT.Exp).then_inc(gate_exp, 1)

            def gate_exp2(j, u):
                act.wait_ge(gate_step, GATE_STEPS * no(j, u) + GATE_EXP2)
                act.activation(g_s[6][:, :, :], g_s[6][:, :, :], ACT.Exp).then_inc(gate_exp, 1)

            def gathered_high(j, u):
                i = no(j, u)
                act.wait_ge(gg_in[u], 64 * (j + 1))
                wait(act, agg2_done, 2 * (i - 1))
                act.activation(gg_hi[u][:, :, :], gg[u][:, :, :], ACT.Copy).then_inc(gg_hi_ready, 1)

            def shared_and_gates(j, u):
                if exists(j, u, 1):
                    gathered_high(*ahead(j, u, 1))
                relu(j, u, 0)
                gate_exp1(j, u)
                gate_exp2(j, u)
                act.activation(sqrt_table[:, :], eps[:, 0:1], ACT.Sqrt)
                relu(j, u, 1)

            gathered_high(0, 0)
            deviations2(0, 0)
            normalise2(0, 0, range(TILES))
            y_part(0, 0)
            shared_and_gates(0, 0)

            def body2(j, u):
                i = no(j, u)
                more, nxt = exists(j, u, 1), ahead(j, u, 1)
                relu(j, u, 2)
                act.wait_ge(wxT_done, i + 1)
                wait(act, o_done, TILES * i)
                act.activation(wxT[:, :], TP[1][0:96, :], ACT.Copy).then_inc(wxT_hi, 1)
                relu(j, u, 3)
                if more:
                    deviations2(*nxt)
                relu(j, u, 4)
                relu(j, u, 5)
                if more:
                    normalise2(*nxt, range(TILES))
                relu(j, u, 6)
                relu(j, u, 7)
                if more:
                    y_part(*nxt)
                relu(j, u, 8)
                if more:
                    shared_and_gates(*nxt)

            pipeline(act, body2)

        @block.vector
        def _(dve):
            step = [0]

            def link(ins):
                step[0] += 1
                ins.then_inc(dstep, 1)
                dve.wait_ge(dstep, step[0])

            dve.wait_ge(dst_in, 16)
            link(dve.tensor_copy(last_dst[:, :], dstN[:, EC - 1:EC]))
            dve.wait_ge(const_set, 1)
            dve.tensor_scalar(last_diag[:, :], ident[0:EP, 0:EP], last_dst[:, 0:1], None,
                              ALU.mult).then_inc(last_ready, 1)
            dve.wait_ge(last_spread, 1)
            for j in range(WJ):
                ins = dve.tensor_scalar(below[:, j, 0:EP], ps[5][:, 0:EP], tb[:, j:j + 1], None, ALU.is_lt)
            link(ins)
            link(dve.tensor_reduce(row_f[:, :].unsqueeze(2), below[:, :, 0:EP], AX.X, ALU.add))
            link(dve.tensor_scalar(row_f[:, :], row_f[:, :], float(EP - 1), None, ALU.min))
            dve.tensor_copy(row_i[:, :], row_f[:, :]).then_inc(row_ready, 1)
            dve.memset(vT[:, :, :, :], 1.0)
            dve.wait_ge(rows_in, 16 * WJ)
            for j in range(WJ):
                ins = dve.tensor_scalar(below[:, j, :], rows_at[:, j, :], tb[:, j:j + 1], None, ALU.is_lt)
            link(ins)
            link(dve.tensor_reduce(in_row[:, :].unsqueeze(2), below[:, :, :], AX.X, ALU.add))
            dve.scalar_tensor_tensor(out=first_edge[:, :], in0=row_f[:, :], scalar=float(EC), in1=in_row[:, :],
                                     op0=ALU.mult, op1=ALU.add).then_inc(first_ready, 1)

            dve.wait_ge(succ_in, 32)
            link(dve.tensor_tensor(falls[:, :], dstN[:, :], dstS[:, :], ALU.is_gt))
            link(dve.tensor_reduce(unfit[0:EP, :], falls[:, :], AX.X, ALU.max))

            dve.wait_ge(w_in, 16)

            def packed(name):
                a, n = WCOLS[name]
                return wst[:, a:a + n]

            def halves(name):
                return packed(name).rearrange("p (k n) -> p k n", k=2)

            link(dve.memset(ew2_hi[:, :, :].bitcast(fp32), 0.0))
            link(dve.memset(ew2_lo[:, :, :].bitcast(fp32), 0.0))
            splits = [
                (w1_hi[:, 0], w1_lo[:, 0], halves("w1l")),
                (w1_hi[:, 1], w1_lo[:, 1], halves("w1r")),
                (w2_hi[:, :], w2_lo[:, :], halves("w2")),
                (sw1_hi[:, :], sw1_lo[:, :], halves("sw1")),
                (sw2_hi[:, :], sw2_lo[:, :], halves("sw2")),
                (sw3_hi[:, :], sw3_lo[:, :], packed("sw3")),
                (ew1_hi[:, :, :, :].rearrange("p k e n -> p k (e n)"), ew1_lo[:, :, :, :].rearrange("p k e n -> p k (e n)"),
                 halves("ew1")),
                (ew3_hi[:, :], ew3_lo[:, :], halves("ew3")),
                (gw_hl[:, :, 0:NEXP], gw_hl[:, :, NEXP:2 * NEXP], halves("gw")),
            ]
            for e in range(NEXP):
                c = 64 * (e % 2)
                a = WCOLS["ew2"][0] + 64 * e
                splits.append((ew2_hi[:, e, c:c + 64], ew2_lo[:, e, c:c + 64], wst[:, a:a + 64]))
            for hi_, _, of in splits:
                dve.tensor_copy(hi_, of).then_inc(dstep, 1)
                step[0] += 1
            dve.wait_ge(dstep, step[0])
            dve.wait_ge(win_in, 16 * 2 * WJ)
            link(dve.tensor_copy(wd[:, :, :], win_d[:, :, :]))
            link(dve.tensor_copy(ws[:, :, :], win_s[:, :, :]))
            link(dve.tensor_scalar(shi[:, :, :], win_s[:, :, :], 8, None, ALU.logical_shift_right))
            link(dve.tensor_scalar(slo[:, :, :], win_s[:, :, :], 255, None, ALU.bitwise_and))
            for j in range(WJ):
                link(dve.tensor_scalar(wd[:, j, :], wd[:, j, :], tb[:, j:j + 1], None, ALU.subtract))
                link(dve.tensor_scalar(ws[:, j, :], ws[:, j, :], tb[:, j:j + 1], None, ALU.subtract))
            link(dve.tensor_scalar(wv[:, :, :], wd[:, :, :], 0.0, None, ALU.is_ge))
            link(dve.scalar_tensor_tensor(out=wv[:, :, :], in0=wd[:, :, :], scalar=float(P), in1=wv[:, :, :],
                                          op0=ALU.is_lt, op1=ALU.mult))
            link(dve.tensor_tensor(wn[:, :, :], ws[:, :, :], wd[:, :, :], ALU.not_equal))
            link(dve.tensor_tensor(wn[:, :, :], wn[:, :, :], wv[:, :, :], ALU.mult))
            for j in range(WJ):
                link(dve.tensor_tensor_scan(wc[:, j, :], wn[:, j, :], wn[:, j, :], 0.0, ALU.add, ALU.max))
            link(dve.tensor_scalar(unfit_w[:, :], wc[:, :, WIN - 1], float(P), None, ALU.is_gt))
            link(dve.tensor_tensor(unfit_w[:, :], unfit_w[:, :], wv[:, :, WIN - 1], ALU.max))
            link(dve.tensor_tensor(unfit_w[:, 0:2], unfit_w[:, 0:2], unfit_w[:, 2:4], ALU.max))
            link(dve.tensor_tensor(unfit_w[:, 0:1], unfit_w[:, 0:1], unfit_w[:, 1:2], ALU.max))
            dve.tensor_tensor(unfit[:, :], unfit[:, :], unfit_w[:, 0:1], ALU.max).then_inc(unfit_ready, 1)
            link(dve.tensor_tensor(wc[:, :, :], wc[:, :, :], wn[:, :, :], ALU.mult))
            link(dve.tensor_tensor(ws[:, :, :], wv[:, :, :], wn[:, :, :], ALU.subtract))
            link(dve.scalar_tensor_tensor(out=ws[:, :, :], in0=wd[:, :, :], scalar=float(P + 1), in1=ws[:, :, :],
                                          op0=ALU.add, op1=ALU.mult))
            link(dve.scalar_tensor_tensor(out=wk_[:, :, :], in0=wc[:, :, :], scalar=-1.0, in1=ws[:, :, :],
                                          op0=ALU.add, op1=ALU.add))
            link(dve.tensor_copy(ws[:, :, :], shi[:, :, :]))
            link(dve.tensor_copy(wn[:, :, :], slo[:, :, :]))
            dve.sem_inc(fields_ready, 1)

            for hi_, lo_, of in splits:
                dve.tensor_tensor(lo_, of, hi_.bitcast(fp32), ALU.subtract)
            dve.wait_ge(const_set, 2)
            dve.tensor_copy(sel[:, :, :], selj[:, :].rearrange("r (q m) -> r q m", q=2))
            dve.wait_ge(bias_in, 96)
            link(dve.tensor_copy(b3s[:, :], b3f[:, :]))
            link(dve.tensor_tensor(b3s[64:96, :], b3f[64:96, :], b3s[64:96, :].bitcast(fp32), ALU.subtract))

            dve.wait_ge(ft_taken, 4 * len(CHUNKS))

            def key_hots(j, u):
                i = no(j, u)
                wait(dve, slots_done, i - 1)
                for t in range(ACT_FROM):
                    for q, (_, n) in enumerate(CHUNKS):
                        c = i * BATCH + t
                        c = slice(c, c + 1) if isinstance(c, int) else bass.ds(c, 1)
                        ins = dve.tensor_scalar(hot[0:n, u, t, q, :], iob[0:n, :], keyT[0:n, q, c], None,
                                                ALU.is_equal)
                ins.then_inc(hot_ready, 1)

            for u in range(2):
                key_hots(0, u)
            with dve.Fori(1, STEPS // 2) as j:
                for u in range(2):
                    key_hots(j, u)
            dve.wait_ge(unfit_sum, 1)
            link(dve.tensor_scalar(gen[:, :], ps[6][:, 0:1], 0.0, None, ALU.is_gt))
            dve.tensor_copy(gen_i[:, :], gen[0:1, :])
            dve.tensor_scalar(own[:, :], gen[:, :], -1.0, 1.0, ALU.mult, ALU.add)
            dve.tensor_scalar(neg_own[:, :], gen[:, :], 1.0, -1.0, ALU.mult, ALU.add)
            dve.wait_ge(slots_taken, STEPS)
            link(dve.scalar_tensor_tensor(out=idxf[:, :], in0=info[:, :, 0], scalar=256.0, in1=info[:, :, 1],
                                          op0=ALU.mult, op1=ALU.add))
            link(dve.scalar_tensor_tensor(out=idxf[:, :], in0=info[:, :, 3], scalar=-OOB, in1=idxf[:, :],
                                          op0=ALU.mult, op1=ALU.add))
            link(dve.tensor_scalar(idx_all[:, :], idxf[:, :], OOB, None, ALU.add))
            link(dve.scalar_tensor_tensor(out=dloc_all[:, :], in0=info[:, :, 3], scalar=-1000.0, in1=info[:, :, 2],
                                          op0=ALU.mult, op1=ALU.add))
            link(dve.tensor_scalar(dloc_all[:, :], dloc_all[:, :], 1000.0, None, ALU.add))
            link(dve.tensor_copy(dloc_b[:, :], dloc_all[:, :]))

            def slot_hots(j, u):
                i = no(j, u)
                wait(dve, cnt_done, i - 1)
                c = slice(i * BATCH, (i + 1) * BATCH) if isinstance(i, int) else bass.ds(i * BATCH, BATCH)
                dve.tensor_tensor(mh[:, u, :, :], iob[:, None, 0:P].to_broadcast([P, BATCH, P]),
                                  dloc_b[:, c].unsqueeze(2).to_broadcast([P, BATCH, P]),
                                  ALU.is_equal).then_inc(mh_ready, 1)

            for u in range(2):
                slot_hots(0, u)
            with dve.Fori(1, STEPS // 2) as j:
                for u in range(2):
                    slot_hots(j, u)
            dve.wait_ge(cnt_taken, STEPS)
            link(dve.tensor_tensor(cnt[:, :], cnt[:, :], info[:, :, 7], ALU.add))
            link(dve.tensor_scalar(cnt[:, :], cnt[:, :], 1.0, None, ALU.max))
            link(dve.reciprocal(inv_all[:, :], cnt[:, :]))
            link(dve.tensor_tensor(sinv_all[:, :], inv_all[:, :], info[:, :, 7], ALU.mult))
            end_phase(dve, 1)
            general(dve, 0, general_vector)

            def statistics(j, u):
                i = no(j, u)
                dve.wait_ge(x_in[u], 32 * (j + 1))
                wait(dve, xgn_ready, TILES * (i - 1))
                wait(dve, xn_ready, TILES * (i - 1))
                for t in range(TILES):
                    dve.bn_stats(st1[u][:, t, :], xb[u][:, t, :]).then_inc(stats1, 1)
                dve.wait_ge(xg_in[u], 64 * (j + 1))
                for t in range(TILES):
                    dve.bn_stats(st1[u][:, TILES + t, :], xg[u][:, t, :]).then_inc(stats1, 1)
                dve.wait_ge(stats1, 2 * TILES * (i + 1))
                wait(dve, agg_done, i - 1)
                for t in range(TILES):
                    dve.tensor_scalar(m1[u][:, t, :], iota[:, 0:P], col(dloc_all, j, u, t), None,
                                      ALU.is_equal).then_inc(m1_ready, 1)
                for t in range(2 * TILES):
                    ins = dve.bn_aggr(mv1[u][:, t, :], st1[u][:, t, :])
                ins.then_inc(ln1a, 1)

            def scales(j, u):
                i = no(j, u)
                dve.wait_ge(std1, i + 1)
                dve.reciprocal(rs1[u][:, :], sd1[u][:, :]).then_inc(rstd1, 1)
                dve.wait_ge(rstd1, 2 * i + 1)
                dve.scalar_tensor_tensor(out=nm1[u][:, 0:TILES], in0=mv1[u][:, 0:TILES, 0], scalar=-1.0,
                                         in1=rs1[u][:, 0:TILES], op0=ALU.mult, op1=ALU.mult)
                dve.scalar_tensor_tensor(out=nm1[u][:, TILES:], in0=mv1[u][:, TILES:, 0], scalar=neg_own[:, 0:1],
                                         in1=rs1[u][:, TILES:], op0=ALU.mult, op1=ALU.mult).then_inc(rstd1, 1)
                dve.wait_ge(rstd1, 2 * i + 2)
                dve.tensor_scalar(rs1[u][:, TILES:], rs1[u][:, TILES:], own[:, 0:1], gen[:, 0:1],
                                  ALU.mult, ALU.max).then_inc(ln1b, 1)

            def remainder(to, hi_, done, taken, taken_hi, j, u):
                i = no(j, u)
                for k in range(2):
                    dve.wait_ge(taken_hi, 2 * i + k + 1)
                    dve.tensor_tensor(to[u][:, k, :], TP[k][:, :], hi_[u][:, k, :].bitcast(fp32),
                                      ALU.subtract).then_inc(taken, 1)

            def means(j, u):
                i = no(j, u)
                dve.wait_ge(agg_done, i + 1)
                dve.wait_ge(sx_ready, i + 1)
                wait(dve, mT_done, i - 1)
                for t in range(TILES):
                    c = (t % 2) * D
                    dve.scalar_tensor_tensor(out=mean[u][:, t, :], in0=AG[t // 2][:, c:c + D],
                                             scalar=col(inv_all, j, u, t), in1=sx[u][:, t, :],
                                             op0=ALU.mult, op1=ALU.add).then_inc(mean_ready, 1)

            def x_rest(j, u):
                remainder(xT_lo, xT_hi, xT_done, xlo, xhi, j, u)

            def m_rest(j, u):
                remainder(mT_lo, mT_hi, mT_done, mlo, mhi, j, u)

            for g in range(2):
                statistics(0, g)
                scales(0, g)
            means(0, 0)
            x_rest(0, 0)
            m_rest(0, 0)
            x_rest(0, 1)
            means(0, 1)
            statistics(1, 0)
            scales(1, 0)

            def body(j, u):
                i = no(j, u)
                if exists(j, u, 3):
                    statistics(*ahead(j, u, 3))
                for k in range(2):
                    dve.wait_ge(h_hi, 2 * i + k + 1)
                    wait(dve, z_done, TILES * i)
                    dve.tensor_tensor(hlo[:, k, :], ha[:, k, :], hh[:, k, :].bitcast(fp32),
                                      ALU.subtract).then_inc(h_lo, 1)
                    if k == 0 and exists(j, u, 3):
                        scales(*ahead(j, u, 3))
                if exists(j, u, 1):
                    m_rest(*ahead(j, u, 1))
                if exists(j, u, 2):
                    means(*ahead(j, u, 2))
                wait(dve, z_out[u], 16 * j)
                for t in range(TILES):
                    dve.wait_ge(hl_ready, TILES * i + t + 1)
                    dve.scalar_tensor_tensor(out=zs[u][:, t, :], in0=hl[u][:, t, :],
                                             scalar=col(sinv_all, j, u, t), in1=ZB[t % 2][:, D:2 * D],
                                             op0=ALU.mult, op1=ALU.add).then_inc(z_ready, 1)
                    if t == 0 and exists(j, u, 2):
                        x_rest(*ahead(j, u, 2))

            pipeline(dve, body)
            end_phase(dve, 3)
            general(dve, 1, general_vector)

            def slots2(j, u):
                wait(dve, agg2_done, 2 * (no(j, u) - 1))
                for t in range(TILES):
                    dve.tensor_scalar(m2[u][:, t, :], iota[:, 0:P], col(dloc_all, j, u, t), None,
                                      ALU.is_equal).then_inc(m2_ready, 1)

            def second(j, u):
                i = no(j, u)
                dve.wait_ge(xb_ready, 2 * (i + 1))
                for t in range(TILES):
                    dve.wait_ge(agg2_done, 2 * i + t // 2 + 1)
                    c = (t % 2) * D
                    dve.scalar_tensor_tensor(out=x2[u][:, t, :], in0=AG[t // 2][:, c:c + D],
                                             scalar=col(inv_all, j, u, t), in1=zb[u][:, t, :],
                                             op0=ALU.mult, op1=ALU.add).then_inc(x2_ready, 1)

            def statistics2(j, u, between=None):
                i = no(j, u)
                for t in range(TILES):
                    dve.wait_ge(x2_ready, TILES * i + t + 1)
                    dve.bn_stats(st2[u][:, t, :], x2[u][:, t, :]).then_inc(stats2, 1)
                dve.wait_ge(stats2, TILES * (i + 1))
                if between is not None:
                    between()
                for t in range(TILES):
                    ins = dve.bn_aggr(mv2[u][:, t, :], st2[u][:, t, :])
                ins.then_inc(ln2a, 1)

            def scales2(j, u):
                i = no(j, u)
                dve.wait_ge(std2, i + 1)
                dve.reciprocal(rs2[u][:, :], sd2[u][:, :]).then_inc(rstd2, 1)
                dve.wait_ge(rstd2, i + 1)
                dve.scalar_tensor_tensor(out=nm2[u][:, :], in0=mv2[u][:, :, 0], scalar=-1.0, in1=rs2[u][:, :],
                                         op0=ALU.mult, op1=ALU.mult).then_inc(ln2b, 1)

            def y_rest(j, u):
                i = no(j, u)
                for k in range(2):
                    dve.wait_ge(yhi, 2 * i + k + 1)
                    dve.tensor_tensor(yT_lo[u][:, k, :], TP[k][:, :], yT_hi[u][:, k, :].bitcast(fp32),
                                      ALU.subtract).then_inc(ylo, 1)

            def rest(j, u, r):
                i = no(j, u)
                dve.wait_ge(r_relu, 9 * i + r + 1)
                if r in (6, 8):
                    q = (r - 6) // 2
                    dve.wait_ge(wb_done, 2 * i + q + 1)
                    dve.tensor_tensor(act_a[:, r, :], act_a[:, r, :], WB[q][:, :], ALU.mult).then_inc(wb_taken, 1)
                    dve.wait_ge(wb_taken, 2 * i + q + 1)
                if r >= 4:
                    if r >= 6:
                        wait(dve, o_done, TILES * i)
                    dve.tensor_copy(act_hi[:, r, :], act_a[:, r, :]).then_inc(r_hi_v, 1)
                wait_high(dve, i, r)
                dve.tensor_tensor(act_lo[:, r, :], act_a[:, r, :], act_hi[:, r, :].bitcast(fp32),
                                  ALU.subtract).then_inc(r_lo, 1)

            def gates(j, u):
                i = no(j, u)
                n = [0]
                B = [P, TILES, NEXP]
                S = [P, TILES, 1]
                lgt, d, c1, oh1, e2, q2, oh2, w1, w2 = (t[:, :, :] for t in g_t)
                mx, sm, ri, m1_, v2, m2_, d2, den, a1, a2 = (t[:, :, :] for t in g_s)
                lgs = TP[0][:, 0:8 * TILES].rearrange("p (t k) -> p t k", k=8)

                def done(ins):
                    n[0] += 1
                    ins.then_inc(gate_step, 1)

                def due():
                    dve.wait_ge(gate_step, GATE_STEPS * i + n[0])

                dve.wait_ge(lg_done, i + 1)
                done(dve.tensor_tensor(lgt, lgs[:, :, 0:NEXP], gbb[:, None, :].to_broadcast(B), ALU.add))
                yield
                due()
                done(dve.tensor_tensor(lgt, lgt, lgs[:, :, NEXP:2 * NEXP], ALU.add))
                yield
                due()
                done(dve.tensor_reduce(mx, lgt, AX.X, ALU.max))
                yield
                due()
                done(dve.tensor_tensor(d, lgt, mx.to_broadcast(B), ALU.subtract))
                done(dve.scalar_tensor_tensor(out=c1, in0=lgt, scalar=1.0, in1=mx.to_broadcast(B),
                                              op0=ALU.mult, op1=ALU.is_equal))
                assert n[0] == GATE_EXP1 + 1
                yield
                due()
                done(dve.tensor_tensor(c1, c1, prio[:, :, :], ALU.mult))
                yield
                due()
                done(dve.tensor_reduce(m1_, c1, AX.X, ALU.max))
                yield
                due()
                done(dve.tensor_tensor(oh1, c1, m1_.to_broadcast(B), ALU.is_equal))
                yield
                due()
                dve.wait_ge(gate_exp, 2 * i + 1)
                done(dve.tensor_reduce(sm, d, AX.X, ALU.add))
                done(dve.scalar_tensor_tensor(out=e2, in0=oh1, scalar=-4.0, in1=d, op0=ALU.mult, op1=ALU.add))
                yield
                due()
                done(dve.reciprocal(ri, sm))
                done(dve.tensor_reduce(v2, e2, AX.X, ALU.max))
                yield
                due()
                done(dve.scalar_tensor_tensor(out=d2, in0=v2, scalar=-1.0, in1=ri, op0=ALU.add, op1=ALU.mult))
                assert n[0] == GATE_EXP2
                done(dve.tensor_tensor(q2, e2, v2.to_broadcast(B), ALU.is_equal))
                yield
                due()
                done(dve.tensor_tensor(q2, q2, prio[:, :, :], ALU.mult))
                yield
                due()
                done(dve.tensor_reduce(m2_, q2, AX.X, ALU.max))
                yield
                due()
                done(dve.tensor_tensor(oh2, q2, m2_.to_broadcast(B), ALU.is_equal))
                yield
                due()
                dve.wait_ge(gate_exp, 2 * i + 2)
                done(dve.tensor_scalar(den, d2, 1.0, None, ALU.add))
                yield
                due()
                done(dve.reciprocal(a1, den))
                yield
                due()
                done(dve.tensor_tensor(a2, d2, a1, ALU.mult))
                done(dve.tensor_tensor(w1, oh1, a1.to_broadcast(B), ALU.mult))
                yield
                due()
                done(dve.tensor_tensor(w2, oh2, a2.to_broadcast(B), ALU.mult))
                yield
                due()
                dve.wait_ge(wx_set, 1)
                wait(dve, wxT_done, i)
                for c in (0, 32, 64):
                    ins = dve.tensor_tensor(wx[:, :, c:c + NEXP], w1, w2, ALU.add)
                ins.then_inc(wx_ready, 1)
                assert n[0] == GATE_STEPS, n[0]

            slots2(0, 0)
            slots2(0, 1)
            second(0, 0)
            statistics2(0, 0)
            scales2(0, 0)
            y_rest(0, 0)
            for _ in gates(0, 0):
                pass

            def body2(j, u):
                i = no(j, u)
                more, nxt = exists(j, u, 1), ahead(j, u, 1)

                def weights_low():
                    dve.wait_ge(wxT_hi, i + 1)
                    dve.tensor_tensor(wxT[32:64, :], TP[1][32:64, :], wxT[32:64, :].bitcast(fp32),
                                      ALU.subtract).then_inc(wxT_lo, 1)

                if more:
                    second(*nxt)
                    statistics2(*nxt, weights_low)
                else:
                    weights_low()
                rest(j, u, 2)
                rest(j, u, 3)
                if more:
                    scales2(*nxt)
                for r in (4, 5, 6, 7):
                    rest(j, u, r)
                if more:
                    y_rest(*nxt)
                rest(j, u, 8)
                gate = gates(*nxt) if more else iter(())
                wait(dve, o_out[u], 32 * j)
                for t in range(TILES):
                    for _ in range(GATE_AHEAD[t]):
                        next(gate, None)
                    if t == 1 and exists(j, u, 2):
                        slots2(*ahead(j, u, 2))
                    dve.wait_ge(o_done, TILES * i + t + 1)
                    dve.tensor_tensor(ob[u][:, t, :], OBS[t][:, 0:D], x2[u][:, t, :],
                                      ALU.add).then_inc(o_ready, 1)
                for _ in gate:
                    pass

            pipeline(dve, body2)

        @block.tensor
        def _(pe):
            pe.wait_ge(const_set, 1)
            pe.wait_ge(last_ready, 1)
            pe.matmul(ps[5][:, 0:EP], ones[0:EP, :], last_diag[:, :], start=True, stop=True).then_inc(last_spread, 1)
            pe.wait_ge(unfit_ready, 1)
            pe.matmul(ps[6][:, 0:1], ones[:, :], unfit[:, :], start=True, stop=True).then_inc(unfit_sum, 1)
            pe.wait_ge(fields_ready, 1)
            for f, t in enumerate((wk_, ws, wn, wd)):
                for q, (c, n) in enumerate(CHUNKS):
                    k = len(CHUNKS) * f + q
                    wait(pe, ft_taken, k - 3)
                    for j in range(WJ):
                        ins = pe.transpose(ps[k % 4][0:n, P * j:P * j + P], t[:, j, c:c + n], ident[:, :])
                    ins.then_inc(ft_done, 1)
            pe.wait_ge(ft_taken, 4 * len(CHUNKS))

            def pack(j, u):
                i = no(j, u)
                pe.wait_ge(hot_ready, i + 1)
                pe.wait_ge(hot_act_ready, i + 1)
                wait(pe, slots_taken, i - 1)
                for t in range(BATCH):
                    c = (i * BATCH + t) * 4
                    c = slice(c, c + 4) if isinstance(c, int) else bass.ds(c, 4)
                    for part in range(2):
                        o = ps[u][:, 8 * t + 4 * part:8 * t + 4 * part + 4]
                        for q, (_, n) in enumerate(CHUNKS):
                            ins = pe.matmul(o, hot[0:n, u, t, q, P * part:P * part + P],
                                            vT[0:n, q, :, :].rearrange("p b k -> p (b k)")[:, c],
                                            start=q == 0, stop=q == len(CHUNKS) - 1)
                ins.then_inc(slots_done, 1)

            for u in range(2):
                pack(0, u)
            with pe.Fori(1, STEPS // 2) as j:
                for u in range(2):
                    pack(j, u)
            pe.wait_ge(slots_taken, STEPS)

            def count(j, u):
                i = no(j, u)
                pe.wait_ge(mh_ready, i + 1)
                wait(pe, cnt_taken, i - 1)
                for t in range(BATCH):
                    ins = pe.matmul(ps[u][:, t:t + 1], mh[:, u, t, :], oneb[:, 0:1], start=True, stop=True)
                ins.then_inc(cnt_done, 1)

            for u in range(2):
                count(0, u)
            with pe.Fori(1, STEPS // 2) as j:
                for u in range(2):
                    count(j, u)
            end_phase(pe, 1)
            general(pe, 0, general_tensor)

            def aggregate(j, u):
                i = no(j, u)
                pe.wait_ge(m1_ready, TILES * (i + 1))
                wait(pe, mean_ready, TILES * i)
                for t in range(TILES):
                    pe.wait_ge(xgn_ready, TILES * i + t + 1)
                    c = (t % 2) * D
                    ins = pe.matmul(AG[t // 2][:, c:c + D], m1[u][:, t, :], xgn[u][:, t, :], start=True, stop=True)
                ins.then_inc(agg_done, 1)

            def transpose_own(j, u):
                i = no(j, u)
                wait(pe, mhi, 2 * i)
                wait(pe, mlo, 2 * i)
                pe.wait_ge(xn_ready, TILES * (i + 1))
                for k in range(2):
                    for t in range(TILES):
                        ins = pe.transpose(TP[k][:, P * t:P * t + P], xn[u][:, t, P * k:P * k + P], ident[:, :])
                ins.then_inc(xT_done, 1)

            def transpose_means(j, u):
                i = no(j, u)
                pe.wait_ge(mean_ready, TILES * (i + 1))
                pe.wait_ge(xhi, 2 * (i + 1))
                pe.wait_ge(xlo, 2 * (i + 1))
                for k in range(2):
                    for t in range(TILES):
                        ins = pe.transpose(TP[k][:, P * t:P * t + P], mean[u][:, t, P * k:P * k + P], ident[:, :])
                ins.then_inc(mT_done, 1)

            def layer(j, u):
                i = no(j, u)
                pe.wait_ge(mhi, 2 * (i + 1))
                pe.wait_ge(mlo, 2 * (i + 1))
                for k in range(2):
                    wait(pe, h_relu, 2 * (i - 1) + k + 1)
                    c = slice(P * k, P * k + P)
                    terms = [(side, kk) for side in range(2) for kk in range(2)]
                    for n, (side, kk) in enumerate(terms):
                        hi_, lo_ = (mT_hi, mT_lo) if side == 0 else (xT_hi, xT_lo)
                        ins = mm3(pe, HB[k][:, :], w1_hi[:, side, kk, c], w1_lo[:, side, kk, c],
                                  hi_[u][:, kk, :], lo_[u][:, kk, :], n == 0, n == 3)
                    ins.then_inc(h_done, 1)

            def second_layer(j, u):
                i = no(j, u)
                for t in range(TILES):
                    wait(pe, z_ready, TILES * i + t - 1)
                    for k in range(2):
                        if t == 0:
                            pe.wait_ge(h_hi, 2 * i + k + 1)
                            pe.wait_ge(h_lo, 2 * i + k + 1)
                        c = slice(P * t, P * t + P)
                        ins = mm3(pe, ZB[t % 2][:, :], hh[:, k, c], hlo[:, k, c], w2_hi[:, k, :], w2_lo[:, k, :],
                                  k == 0, k == 1)
                    ins.then_inc(z_done, 1)
                    if t == 0 and exists(j, u, 2):
                        transpose_own(*ahead(j, u, 2))

            aggregate(0, 0)
            transpose_own(0, 0)
            transpose_means(0, 0)
            aggregate(0, 1)
            transpose_own(0, 1)

            def body(j, u):
                layer(j, u)
                if exists(j, u, 1):
                    transpose_means(*ahead(j, u, 1))
                if exists(j, u, 2):
                    aggregate(*ahead(j, u, 2))
                second_layer(j, u)

            pipeline(pe, body)
            end_phase(pe, 3)
            general(pe, 1, general_tensor)

            def aggregate2(j, u):
                i = no(j, u)
                pe.wait_ge(m2_ready, TILES * (i + 1))
                pe.wait_ge(gg_hi_ready, i + 1)
                pe.wait_ge(gg_lo_ready, i + 1)
                wait(pe, x2_ready, TILES * i)
                wait(pe, o_ready, TILES * (i - 1) - 2)
                for t in range(TILES):
                    c = (t % 2) * D
                    pe.matmul(AG[t // 2][:, c:c + D], m2[u][:, t, :], gg_hi[u][:, t, :], start=True, stop=False)
                    ins = pe.matmul(AG[t // 2][:, c:c + D], m2[u][:, t, :], gg_lo[u][:, t, :],
                                    start=False, stop=True)
                    if t % 2 == 1:
                        ins.then_inc(agg2_done, 1)

            def transpose_rows(j, u):
                i = no(j, u)
                pe.wait_ge(x2n_ready, TILES * (i + 1))
                wait(pe, gate_step, GATE_STEPS * (i - 1) + 2)
                wait(pe, wxT_lo, i)
                for k in range(2):
                    for t in range(TILES):
                        ins = pe.transpose(TP[k][:, P * t:P * t + P], x2n[u][:, t, P * k:P * k + P], ident[:, :])
                ins.then_inc(yT_done, 1)

            def first_product(j, u, r, half=None):
                i = no(j, u)
                if r in (2, 3):
                    wait(pe, o_ready, TILES * i)
                else:
                    wait(pe, r_relu, 9 * i + (r - 3 if r >= 4 else 0))
                for k in ((0, 1) if half is None else (half,)):
                    if r < 2:
                        l_hi, l_lo = sw1_hi[:, k, P * r:P * r + P], sw1_lo[:, k, P * r:P * r + P]
                    else:
                        l_hi, l_lo = ew1_hi[:, k, r - 2, :], ew1_lo[:, k, r - 2, :]
                    ins = mm3(pe, RB[r][:, :], l_hi, l_lo, yT_hi[u][:, k, :], yT_lo[u][:, k, :],
                              k == 0, k == 1)
                if half != 0:
                    ins.then_inc(r_done, 1)

            def second_product(j, u, r):
                i = no(j, u)
                pe.wait_ge(r_relu, 9 * i + r - 1)
                for k in range(2):
                    if r == 7:
                        of, l_hi, l_lo = k, sw2_hi[:, k, :], sw2_lo[:, k, :]
                    else:
                        e = (r - 6) + k
                        of, l_hi, l_lo = 2 + e, ew2_hi[:, e, :], ew2_lo[:, e, :]
                    wait_high(pe, i, of)
                    wait_low(pe, i, of)
                    ins = mm3(pe, RB[r][:, :], l_hi, l_lo, act_hi[:, of, :], act_lo[:, of, :], k == 0, k == 1)
                ins.then_inc(r_done, 1)

            def spread(j, u, q):
                i = no(j, u)
                pe.wait_ge(r_relu, 9 * i + 3 + q)
                pe.matmul(WB[q][:, :], sel[:, q, :], wxT[:, :], start=True, stop=True).then_inc(wb_done, 1)

            def out_terms(j, u, t, terms, first, last):
                i = no(j, u)
                c = slice(P * t, P * t + P)
                o = OBS[t][:, 0:D]
                for n, term in enumerate(terms):
                    f, l = first and n == 0, last and n == len(terms) - 1
                    if term == "bias":
                        ins = pe.matmul(o, wxT[:, c], b3s[:, :], start=f, stop=l)
                        continue
                    r = {"pair0": 6, "shared": 7, "pair1": 8}[term]
                    wait_high(pe, i, r)
                    wait_low(pe, i, r)
                    w_hi, w_lo = (sw3_hi[:, :], sw3_lo[:, :]) if r == 7 else \
                        (ew3_hi[:, (r - 6) // 2, :], ew3_lo[:, (r - 6) // 2, :])
                    ins = mm3(pe, o, act_hi[:, r, c], act_lo[:, r, c], w_hi, w_lo, f, l)
                return ins

            def logits(j, u):
                i = no(j, u)
                pe.wait_ge(yhi, 2 * (i + 1))
                pe.wait_ge(ylo, 2 * (i + 1))
                for t in range(TILES):
                    c = slice(P * t, P * t + P)
                    for k in range(2):
                        pe.matmul(TP[0][:, 8 * t:8 * t + 8], yT_hi[u][:, k, c], gw_hl[:, k, :],
                                  start=k == 0, stop=False)
                        ins = pe.matmul(TP[0][:, 8 * t:8 * t + 8], yT_lo[u][:, k, c], gw_hl[:, k, :],
                                        start=False, stop=k == 1)
                    if t < 2:
                        first_product(j, u, 0, half=t)
                ins.then_inc(lg_done, 1)

            aggregate2(0, 0)
            transpose_rows(0, 0)
            logits(0, 0)
            first_product(0, 0, 1)

            def body2(j, u):
                i = no(j, u)
                more, nxt = exists(j, u, 1), ahead(j, u, 1)
                if more:
                    aggregate2(*nxt)
                first_product(j, u, 2)
                pe.wait_ge(wx_ready, i + 1)
                for t in range(TILES):
                    ins = pe.transpose(TP[1][0:96, P * t:P * t + P], wx[:, t, :], ident[:, :])
                ins.then_inc(wxT_done, 1)
                for r in range(3, 6):
                    first_product(j, u, r)
                pe.wait_ge(wxT_lo, i + 1)
                spread(j, u, 0)
                spread(j, u, 1)
                second_product(j, u, 6)
                second_product(j, u, 7)
                if more:
                    transpose_rows(*nxt)
                second_product(j, u, 8)
                for t in range(2):
                    out_terms(j, u, t, ("pair0", "bias", "shared"), True, False)
                if more:
                    logits(*nxt)
                for t in range(2):
                    out_terms(j, u, t, ("pair1",), False, True).then_inc(o_done, 1)
                if more:
                    first_product(*nxt, 1)
                for t in range(2, TILES):
                    pe.wait_ge(wb_taken, 2 * i + 2)
                    out_terms(j, u, t, ("pair0", "bias", "shared", "pair1"), True, True).then_inc(o_done, 1)

            pipeline(pe, body2)


def _cols(w):
    k = w.shape[0] // P
    return w.reshape(k, P, w.shape[1]).transpose(1, 0, 2).reshape(P, -1)


def kernel(**inputs):
    import numpy as np
    import concourse.bacc as bacc
    from concourse.bass_utils import run_bass_kernel_spmd

    a = {k.replace("L0_gnn_", "").replace("L0_ffn_", ""): np.asarray(v) for k, v in inputs.items()}
    w2 = np.concatenate([a["W2l"].T, a["W2r"].T], axis=1)
    ew1 = a["eW1"].transpose(1, 0, 2).reshape(D, NEXP * P)
    ew2 = a["eW2"].transpose(1, 0, 2).reshape(P, NEXP * 64)
    ew3 = a["eW3"].reshape(NEXP * 64, D)
    parts = [_cols(m) for m in (a["W1l"].T, a["W1r"].T, w2, a["sW1"])]
    parts += [_cols(a["sW2"]), a["sW3"], _cols(ew1), ew2, _cols(ew3), _cols(a["gW"])]
    bias = [a["b1"].reshape(2, P).T, a["sb1"].reshape(2, P).T, a["sb2"].reshape(1, P).T,
            a["eb1"].T, a["eb2"].reshape(2, P).T]
    arrays = {
        "x": a["x"], "src": a["src"], "dst": a["dst"],
        "wpack": np.ascontiguousarray(np.concatenate(parts, axis=1)),
        "bpack": np.ascontiguousarray(np.concatenate(bias, axis=1)),
        "b2": a["b2"], "gb": a["gb"],
        "b3": np.ascontiguousarray(np.concatenate([a["eb3"], a["sb3"][None]], axis=0)),
    }
    nc = bacc.Bacc("TRN2", target_bir_lowering=False, num_devices=1)
    args = [nc.dram_tensor(f"in_{n}", v.shape, mybir.dt.from_np(v.dtype), kind="ExternalInput").ap()
            for n, v in arrays.items()]
    out = nc.dram_tensor("out_x", (N, D), mybir.dt.float32, kind="ExternalOutput").ap()
    build(nc, *args, out)
    r = run_bass_kernel_spmd(nc, [{f"in_{n}": v for n, v in arrays.items()}], core_ids=[0])
    return r.results[0]["out_x"]
```
